# Optimizing a Trainium2 kernel written in Bass

```python
import numpy as np
import jax
import jax.numpy as jnp

def _softmax(x, axis=-1):
    return jax.nn.softmax(x, axis=axis)

def _gelu(x):
    return jax.nn.gelu(x, approximate=True)

def _silu(x):
    return jax.nn.silu(x)

def _sigmoid(x):
    return jax.nn.sigmoid(x)

def _layernorm(x, axis=-1, eps=1e-05):
    m = jnp.mean(x, axis=axis, keepdims=True)
    v = jnp.var(x, axis=axis, keepdims=True)
    return (x - m) / jnp.sqrt(v + eps)

def _scatter_add(tgt, idx, src, axis=0):
    return tgt.at[idx].add(src)

def _segment_sum(src, seg, n):
    return jax.ops.segment_sum(src, seg, n)
kernel_name = 'mk_gps_d1_gnn_r8_d6d706'

def setup_inputs(seed: int=0):
    np.random.seed(seed)
    _w = jnp.asarray

    def _rec_inputs():
        import jax
        import jax.numpy as jnp
        _gk = jax.random.key(seed)
        x = -0.0002117 + 1 * jax.random.normal(jax.random.fold_in(_gk, 1), (1250, 512), jnp.float32)
        _s = jax.random.randint(jax.random.fold_in(_gk, 2), (10000,), 0, 1250, jnp.int32)
        _d = jax.random.randint(jax.random.fold_in(_gk, 3), (10000,), 0, 1250, jnp.int32)
        _loop = jnp.arange(1250, dtype=jnp.int32)
        src = jnp.concatenate([_s, _d, _loop])
        dst = jnp.concatenate([_d, _s, _loop])
        _o = jnp.argsort(dst, stable=True)
        src = src[_o]
        dst = dst[_o]
        return (x, src, dst)
    x, src, dst = _rec_inputs()

    def _L0_gnn_setup():
        import jax, jax.numpy as jnp
        import numpy as np
        N_NODES = 6250
        N_EDGES = 187500
        D = 512
        LN_EPS = 1e-05

        def _layer_norm(x, gamma, beta):
            mu = jnp.mean(x, axis=-1, keepdims=True)
            var = jnp.mean(jnp.square(x - mu), axis=-1, keepdims=True)
            return (x - mu) * jax.lax.rsqrt(var + LN_EPS) * gamma + beta
        key = jax.random.key(seed)
        ks = jax.random.split(key, 8)
        scale = 1.0 / np.sqrt(D)
        return {'node_feature': jax.random.normal(ks[0], (N_NODES, D), dtype=jnp.float32), 'edge_index': jax.random.randint(ks[1], (2, N_EDGES), 0, N_NODES, dtype=jnp.int32), 'W_l': jax.random.uniform(ks[2], (D, D), jnp.float32, -scale, scale), 'b_l': jnp.zeros((D,), jnp.float32), 'W_r': jax.random.uniform(ks[3], (D, D), jnp.float32, -scale, scale), 'gamma': jnp.ones((D,), jnp.float32), 'beta': jnp.zeros((D,), jnp.float32)}
    _L0_gnn_all = _L0_gnn_setup()
    _L0_gnn_in = {k: v for k, v in _L0_gnn_all.items() if k in ('W_l', 'b_l', 'W_r', 'gamma', 'beta')}
    del _L0_gnn_all

    def _L0_mix_setup():
        import jax, jax.numpy as jnp
        import numpy as np
        NUM_HEADS = 16
        EPS = 1e-15
        key = jax.random.key(seed)
        k1, k2, k3, k4 = jax.random.split(key, 4)
        B, N, C = (4, 2048, 512)
        x = jax.random.normal(k1, (B, N, C), dtype=jnp.float32)
        qkv_weight = jax.random.normal(k2, (3 * C, C), dtype=jnp.float32) * 0.02
        proj_weight = jax.random.normal(k3, (C, C), dtype=jnp.float32) * 0.02
        proj_bias = jax.random.normal(k4, (C,), dtype=jnp.float32) * 0.02
        return {'x': x, 'qkv_weight': qkv_weight, 'proj_weight': proj_weight, 'proj_bias': proj_bias}
    _L0_mix_all = _L0_mix_setup()
    _L0_mix_in = {k: v for k, v in _L0_mix_all.items() if k in ('qkv_weight', 'proj_weight', 'proj_bias')}
    del _L0_mix_all

    def _L0_ffn_setup():
        import jax, jax.numpy as jnp
        import numpy as np
        B, S, D, O = (1, 256, 512, 512)
        H, QD, K, PK = (8, 256, 16, 256)
        N = PK * PK
        HALF = QD // 2

        def _l2norm(x):
            n = jnp.sqrt(jnp.sum(x * x, axis=-1, keepdims=True))
            return x / jnp.maximum(n, 1e-12)
        key = jax.random.key(seed)
        ks = jax.random.split(key, 9)
        return {'hidden_states': jax.random.normal(ks[0], (B, S, D), jnp.float32), 'Wq': jax.random.normal(ks[1], (H * QD, D), jnp.float32) * 0.02, 'bq': jnp.zeros((H * QD,), jnp.float32), 'ln_g': jnp.ones((QD,), jnp.float32), 'ln_b': jnp.zeros((QD,), jnp.float32), 'keys0': jax.random.normal(ks[2], (PK, HALF), jnp.float32) * 0.02, 'keys1': jax.random.normal(ks[3], (PK, HALF), jnp.float32) * 0.02, 'expert_down': jax.random.normal(ks[4], (N, D), jnp.float32) * 0.02, 'expert_up': jax.random.normal(ks[5], (N, O), jnp.float32) * 0.02}
    _L0_ffn_all = _L0_ffn_setup()
    _L0_ffn_in = {k: v for k, v in _L0_ffn_all.items() if k in ('Wq', 'bq', 'ln_g', 'ln_b', 'keys0', 'keys1', 'expert_down', 'expert_up')}
    del _L0_ffn_all
    return {'x': x, 'src': src, 'dst': dst, 'L0_gnn_W_l': _L0_gnn_in['W_l'], 'L0_gnn_b_l': _L0_gnn_in['b_l'], 'L0_gnn_W_r': _L0_gnn_in['W_r'], 'L0_gnn_gamma': _L0_gnn_in['gamma'], 'L0_gnn_beta': _L0_gnn_in['beta'], 'L0_mix_qkv_weight': _L0_mix_in['qkv_weight'], 'L0_mix_proj_weight': _L0_mix_in['proj_weight'], 'L0_mix_proj_bias': _L0_mix_in['proj_bias'], 'L0_ffn_Wq': _L0_ffn_in['Wq'], 'L0_ffn_bq': _L0_ffn_in['bq'], 'L0_ffn_ln_g': _L0_ffn_in['ln_g'], 'L0_ffn_ln_b': _L0_ffn_in['ln_b'], 'L0_ffn_keys0': _L0_ffn_in['keys0'], 'L0_ffn_keys1': _L0_ffn_in['keys1'], 'L0_ffn_expert_down': _L0_ffn_in['expert_down'], 'L0_ffn_expert_up': _L0_ffn_in['expert_up']}

def reference(x, src, dst, L0_gnn_W_l, L0_gnn_b_l, L0_gnn_W_r, L0_gnn_gamma, L0_gnn_beta, L0_mix_qkv_weight, L0_mix_proj_weight, L0_mix_proj_bias, L0_ffn_Wq, L0_ffn_bq, L0_ffn_ln_g, L0_ffn_ln_b, L0_ffn_keys0, L0_ffn_keys1, L0_ffn_expert_down, L0_ffn_expert_up):
    import jax
    import jax.numpy as jnp

    def _L0_gnn_ref(node_feature, edge_index, W_l, b_l, W_r, gamma, beta):
        import jax, jax.numpy as jnp
        import numpy as np
        N_NODES = 6250
        N_EDGES = 187500
        D = 512
        LN_EPS = 1e-05

        def _layer_norm(x, gamma, beta):
            mu = jnp.mean(x, axis=-1, keepdims=True)
            var = jnp.mean(jnp.square(x - mu), axis=-1, keepdims=True)
            return (x - mu) * jax.lax.rsqrt(var + LN_EPS) * gamma + beta
        n = node_feature.shape[0]
        residual = node_feature
        h = _layer_norm(node_feature, gamma, beta)
        src, dst = (edge_index[0], edge_index[1])
        summed = jax.ops.segment_sum(h[src], dst, num_segments=n)
        cnt = jax.ops.segment_sum(jnp.ones((src.shape[0],), h.dtype), dst, num_segments=n)
        mean = summed / jnp.maximum(cnt, 1.0)[:, None]
        out = mean @ W_l.T + b_l + h @ W_r.T
        out = jax.nn.relu(out)
        return out + residual

    def _L0_mix_ref(x, qkv_weight, proj_weight, proj_bias):
        import jax, jax.numpy as jnp
        import numpy as np
        NUM_HEADS = 16
        EPS = 1e-15
        B, N, C = x.shape
        H = NUM_HEADS
        D = C // H
        qkv = (x @ qkv_weight.T).reshape(B, N, 3, C)
        q = jax.nn.relu(qkv[:, :, 0]).reshape(B, N, H, D)
        k = jax.nn.relu(qkv[:, :, 1]).reshape(B, N, H, D)
        v = qkv[:, :, 2].reshape(B, N, H, D)
        qf = q.astype(jnp.float32)
        kf = k.astype(jnp.float32)
        vf = v.astype(jnp.float32)
        v_pad = jnp.concatenate([vf, jnp.ones_like(vf[..., :1])], axis=-1)
        vk = jnp.einsum('bnhc,bnhd->bhcd', v_pad, kf)
        vk_q = jnp.einsum('bnhd,bhcd->bnhc', qf, vk)
        proj_input = (vk_q[..., :-1] / (vk_q[..., -1:] + EPS)).astype(x.dtype).reshape(B, N, C)
        return proj_input @ proj_weight.T + proj_bias

    def _L0_ffn_ref(hidden_states, Wq, bq, ln_g, ln_b, keys0, keys1, expert_down, expert_up):
        import jax, jax.numpy as jnp
        import numpy as np
        B, S, D, O = (1, 256, 512, 512)
        H, QD, K, PK = (8, 256, 16, 256)
        N = PK * PK
        HALF = QD // 2

        def _l2norm(x):
            n = jnp.sqrt(jnp.sum(x * x, axis=-1, keepdims=True))
            return x / jnp.maximum(n, 1e-12)
        b, s, d = hidden_states.shape
        q = (hidden_states @ Wq.T + bq).reshape(b, s, H, QD)
        mu = jnp.mean(q, axis=-1, keepdims=True)
        var = jnp.mean((q - mu) ** 2, axis=-1, keepdims=True)
        q = (q - mu) / jnp.sqrt(var + 1e-05) * ln_g + ln_b
        q0, q1 = (q[..., :HALF], q[..., HALF:])
        s0 = jnp.einsum('bshq,eq->bshe', _l2norm(q0), _l2norm(keys0))
        s1 = jnp.einsum('bshq,eq->bshe', _l2norm(q1), _l2norm(keys1))
        sc0, ix0 = jax.lax.top_k(s0, K)
        sc1, ix1 = jax.lax.top_k(s1, K)
        cs = (sc0[..., :, None] + sc1[..., None, :]).reshape(b, s, H, K * K)
        ci = (ix0[..., :, None] + ix1[..., None, :]).reshape(b, s, H, K * K)
        fs, pos = jax.lax.top_k(cs, K)
        fi = jnp.take_along_axis(ci, pos, axis=-1)
        w = jax.nn.softmax(fs, axis=-1)
        down = expert_down[fi]
        up = expert_up[fi]
        inner = jnp.einsum('bsd,bshkd->bshk', hidden_states, down)
        act = jax.nn.gelu(inner, approximate=False)
        out = jnp.einsum('bshk,bshko->bso', act * w, up)
        return out
    edge_index = jnp.stack([src, dst])
    xn = _layernorm(x, axis=-1)
    x = x + _L0_gnn_ref(xn, edge_index, L0_gnn_W_l, L0_gnn_b_l, L0_gnn_W_r, L0_gnn_gamma, L0_gnn_beta) + _L0_mix_ref(xn[None], L0_mix_qkv_weight, L0_mix_proj_weight, L0_mix_proj_bias)[0]
    x = x + _L0_ffn_ref(_layernorm(x, axis=-1)[None], L0_ffn_Wq, L0_ffn_bq, L0_ffn_ln_g, L0_ffn_ln_b, L0_ffn_keys0, L0_ffn_keys1, L0_ffn_expert_down, L0_ffn_expert_up)[0]
    return x

_drawn_inputs = setup_inputs


def setup_inputs(seed=0):
    import zlib

    import numpy as np

    out = dict(_drawn_inputs(seed))
    spreads = {'L0_gnn_b_l': (0.0, 0.1),
     'L0_gnn_gamma': (1.0, 0.2),
     'L0_gnn_beta': (0.0, 0.278),
     'L0_ffn_bq': (0.0, 0.8),
     'L0_ffn_ln_g': (1.0, 0.6),
     'L0_ffn_ln_b': (0.0, 0.8)}
    factors = {'L0_mix_qkv_weight': 8.0,
     'L0_mix_proj_weight': 8.0,
     'L0_mix_proj_bias': 6.161,
     'L0_ffn_Wq': 8.0,
     'L0_ffn_keys0': 8.0,
     'L0_ffn_keys1': 8.0,
     'L0_ffn_expert_down': 8.0,
     'L0_ffn_expert_up': 8.0}
    for name, (base, spread) in spreads.items():
        noise = np.random.default_rng([zlib.crc32(name.encode()), seed]).standard_normal(out[name].shape)
        drawn = base * np.exp(spread * noise) if base else spread * noise
        out[name] = jnp.asarray(drawn.astype(out[name].dtype))
    for name, factor in factors.items():
        out[name] = (out[name] * factor).astype(out[name].dtype)
    return out
```

```python
from contextlib import ExitStack

import concourse.bass as bass
from concourse import mybir


def build(nc, x, src, dst, W_l, b_l, W_r, gamma, beta, qkv_w, proj_w, proj_b,
          Wq, bq, ln_g, ln_b, keys0, keys1, e_down, e_up, out):
    dt = mybir.dt
    F32, F16, BF16, I32, U32 = dt.float32, dt.float16, dt.bfloat16, dt.int32, dt.uint32
    ALU = mybir.AluOpType
    ACT = mybir.ActivationFunctionType
    AX = mybir.AxisListType
    ds = bass.ds

    N, D = x.shape
    T = 125
    NT = N // T
    KC = D // 128
    E = src.shape[0]
    NC = E // T
    CH = NC // 2
    AB = 418
    AW = 3 * AB
    EPS = 1e-5
    EPS_DEN = 1e-15
    H, QD = 8, 256
    TK = 16
    NK = keys0.shape[0]
    ROWS = [TK // (i + 1) for i in range(TK)]
    OFF = [sum(ROWS[:i]) for i in range(TK)]
    C = sum(ROWS)
    LO, HI = 64, 8
    TP = 126
    WSCALE = 1024.0
    LOWEST = -3.0e38
    LEAST_NORM = 1e-12

    ctx = ExitStack()
    with ctx:
        def sb(name, shape, dtype=F32):
            return ctx.enter_context(nc.sbuf_tensor(name, shape, dtype))

        def sem(name):
            return ctx.enter_context(nc.semaphore(name))

        ps = ctx.enter_context(nc.psum_tensor("ps", [128, 8, 512], F32))

        wbig = sb("wbig", [128, KC, 2560])
        qkvT, WlT, WrT = wbig[:, :, 0:1536], wbig[:, :, 1536:2048], wbig[:, :, 2048:2560]
        WqT, downT = wbig[:, :, 0:2048], wbig[:, :, 2048:2560]
        projT = sb("projT", [128, KC, D])
        up = sb("up", [128, KC, D])
        xs = sb("xs", [T, NT, D])
        arena = sb("arena", [128, 25480])
        P = arena[0:T, 0:5120].rearrange("p (t d) -> p t d", d=D)
        R = arena[0:T, 5120:10240].rearrange("p (t d) -> p t d", d=D)
        qT = arena[:, 10240:15240].rearrange("p (g n) -> p g n", n=N)
        stage = arena[:, 15240:19336].rearrange("p (s o d) -> p s o d", s=2, o=4)
        xn = arena[0:T, 19336:19848]
        xh = arena[0:T, 19848:20360]
        kS = arena[0:T, 20360:20872]
        vS = arena[0:T, 20872:21384]
        bl_bc = arena[0:T, 21384:21896]
        pb_bc = arena[0:T, 21896:22408]
        Mb = arena[:, 22408:22920].rearrange("p (g c) -> p g c", g=4)
        Kb = arena[:, 22920:23432].rearrange("p (g c) -> p g c", g=4)
        bq3 = arena[0:65, 24036:25060].bitcast(BF16)
        fs = arena[0:T, 25060:25188].rearrange("p (h r) -> p h r", h=H)
        posi = arena[0:T, 25188:25316].bitcast(U32).rearrange("p (h r) -> p h r", h=H)
        fi = arena[0:T, 25316:25444]
        bmask = arena[:, 23432:23560]
        win = arena[0:1, 8192:10240]
        ends_row = win[:, 512:852].rearrange("p (s c) -> p s c", s=2)
        edge_i = arena[0:CH, 4096:4596].bitcast(I32).rearrange("p (s h t) -> p s h t", s=2, h=2)
        edge_f = arena[0:CH, 4608:5108].rearrange("p (s h t) -> p s h t", s=2, h=2)
        keys_raw = arena[:, 5120:5632].rearrange("p (o d) -> p o d", o=4)
        keysN = arena[:, 5632:6144].rearrange("p (o d) -> p o d", o=4)
        bqf = arena[0:65, 6144:8192]
        tile_lo, chunk_up, chunk_down = win[:, 852:862], win[:, 864:1034], win[:, 1034:1204]
        wlim = win[:, 1204:1244].rearrange("p (s m) -> p s m", s=4)
        ov = arena[0:1, 0:1700].rearrange("p (m c) -> p m c", c=NC)
        ov2 = arena[0:1, 1700:3400].rearrange("p (m c) -> p m c", c=NC)
        qh = arena[0:T, 0:2048]
        sc = arena[0:T, 2048:6144].rearrange("p (h f e) -> p h f e", h=H, f=2)
        sc2 = arena[0:T, 6144:6656].rearrange("p (f e) -> p f e", f=2)
        eq = arena[0:T, 6656:9856].bitcast(F16).rearrange("p (h c r) -> p h c r", h=H, r=TK)
        cirep = arena[0:T, 9856:13056].bitcast(F16).rearrange("p (h c r) -> p h c r", h=H, r=TK)
        Lh = arena[:, 13056:17088].bitcast(F16).rearrange("p (q t) -> p q t", t=TP)
        iotaL = arena[:, 17088:21120].bitcast(F16).rearrange("p (q t) -> p q t", t=TP)
        Hh = arena[:, 21120:22632].bitcast(F16).rearrange("p (s q t) -> p s q t", s=3, t=TP)
        iotaH = arena[:, 22632:23136].bitcast(F16).rearrange("p (q t) -> p q t", t=TP)
        iotaC = arena[0:T, 23136:23536].bitcast(F16).rearrange("p (c r) -> p c r", r=TK)
        W0 = arena[:, 23536:24036].rearrange("p (t j) -> p t j", j=4)

        ident = sb("ident", [128, 128])
        ones = sb("ones", [128, 1])
        zero16 = sb("zero16", [1, 512], F16)
        iotaN = sb("iotaN", [T, AW], F16)
        ecol = sb("ecol", [T, 3 * NC])
        ends = sb("ends", [CH, 4])
        bounds = sb("bounds", [1, 3, NT], I32)
        side = sb("side", [128, 3760])
        S1 = side[0:T, 0:AW].bitcast(F16).rearrange("p (s n) -> p s n", s=2)
        As = side[0:T, AW:2 * AW]
        AT = side[0:T, 2 * AW:2 * AW + NT * T].rearrange("p (s t) -> p s t", s=NT)
        y = side[0:T, 0:512]
        vT = side[:, 512:1012].rearrange("p (f h t) -> p f h t", f=2, h=2)
        v2 = side[:, 1012:1512].rearrange("p (f h t) -> p f h t", f=2, h=2)
        top = side[0:T, 1512:1768].rearrange("p (f h r) -> p f h r", f=2, h=H)
        topi = side[0:T, 1768:2024].bitcast(U32).rearrange("p (f h r) -> p f h r", f=2, h=H)
        topif = side[0:T, 2024:2280].rearrange("p (f h r) -> p f h r", f=2, h=H)
        cs = side[0:T, 2280:2680].rearrange("p (h c) -> p h c", h=H)
        ci = side[0:T, 2680:3080].rearrange("p (h c) -> p h c", h=H)
        lo_i = side[:, 3180:3430].bitcast(I32).rearrange("p (s t) -> p s t", s=2)
        lo16, hi16, wh16, wl16 = (side[:, 3430 + 63 * n:3493 + 63 * n].bitcast(F16) for n in range(4))
        posf = side[0:T, 3682:3746].bitcast(F16).rearrange("p (h r) -> p h r", h=H)
        cs2 = side[0:T, 3080:3180].rearrange("p (s c) -> p s c", s=2)
        D1 = sb("D1", [T, 2, 128], F16)
        xnT = sb("xnT", [128, 2, KC, T])
        hT = sb("hT", [128, 1, KC, T])
        ksum = sb("ksum", [128, 4])
        den = xnT[:, 0, :, :]
        pin = xnT[:, 1, :, :]
        gnn = sb("gnn", [T, D])
        cols = sb("cols", [128, 12])
        gcol, bcol, lgc, lbc = cols[:, 0:4], cols[:, 4:8], cols[:, 8:10], cols[:, 10:12]
        bn = sb("bn", [T, H, 6])
        mv = sb("mv", [T, H, 2])
        rs = sb("rs", [T, H])
        nm = sb("nm", [T, H])
        cnt = sb("cnt", [T, 2])
        knT = sb("knT", [128, 2, NK])
        kss = sb("kss", [128, 4])
        onesb = sb("onesb", [65, T], BF16)
        yT, geluT = xnT[:, 0, :, :], xnT[:, 1, :, :]
        GT = hT[:, 0, :, :]
        nrm = sb("nrm", [T, 2 * H])
        nmean = sb("nmean", [T, H])
        minus_half = sb("minus_half", [128, 16])
        esum = sb("esum", [T, H])
        res = gnn

        norms = ps[0:T, 6, 488:504]

        scores_seen, sums_open, kv_closed = sem("scores_seen"), sem("sums_open"), sem("kv_closed")
        kss_ready, krs_ready, var1_ready, rstd1_ready, yvar_ready, yrstd_ready, qvar_ready, qrstd_ready, nvar_ready, \
            nrstd_ready = map(sem, ("kss_ready krs_ready var1_ready rstd1_ready yvar_ready yrstd_ready qvar_ready "
                                    "qrstd_ready nvar_ready nrstd_ready").split())
        x_loaded, edges_loaded, small_loaded, keys_loaded, up_loaded, bq_loaded = map(
            sem, "x_loaded edges_loaded small_loaded keys_loaded up_loaded bq_loaded".split())
        stage_loaded = [sem("stage_loaded0"), sem("stage_loaded1")]
        pool_step, consts_ready, pad_ready, iotas_ready = map(sem, "pool_step consts_ready pad_ready iotas_ready".split())
        prep_tr, prep_act, prep_dve = map(sem, "prep_tr prep_act prep_dve".split())
        edge_cast, edge_tr, ecol_ready, ends_ready, ends_tr, bounds_ready = map(
            sem, "edge_cast edge_tr ecol_ready ends_ready ends_tr bounds_ready".split())
        keys_normed, keys_tr, knT_ready, bq_ready = map(sem, "keys_normed keys_tr knT_ready bq_ready".split())
        dve_step = sem("dve_step")
        xn_ready, xh_ready, xs_ready, xnT_ps, hT_ps, xnT_ready, hT_ready = map(
            sem, "xn_ready xh_ready xs_ready xnT_ps hT_ps xnT_ready hT_ready".split())
        mm_ready, p_out, r_out, k_out, v_out, q_out, kv_done = map(
            sem, "mm_ready p_out r_out k_out v_out q_out kv_done".split())
        attn_ready = sem("attn_ready")
        onehots_free, onehots_ready, A_ready, A_out, AT_ps, AT_act, AT_dve, agg_ready, nd_ready, den_out, pin_ready, \
            proj_ready, x1_ready, agg_out = map(sem, (
                "onehots_free onehots_ready A_ready A_out AT_ps AT_act AT_dve agg_ready nd_ready den_out pin_ready "
                "proj_ready x1_ready agg_out").split())
        y_ready, yT_ps, yT_ready, inner_ps, gelu_ready, q_ps, qstat_ready, qh_ready, tr_ps, vT_ready, v2_ready, \
            nrm_ps, nrm_out, s_ps, sc_ready, topk_done = map(sem, (
                "y_ready yT_ps yT_ready inner_ps gelu_ready q_ps qstat_ready qh_ready tr_ps vT_ready v2_ready nrm_ps "
                "nrm_out s_ps sc_ready topk_done").split())
        topif_ready, ci_ready, cirep_ready, exp_in, exp_out, w_ready, wT_ps, wh_ready, onehot3, W_ps, W0_ready, \
            G_ready, out_ps, res_ready, stored, back_done = map(sem, (
                "topif_ready ci_ready cirep_ready exp_in exp_out w_ready wT_ps wh_ready onehot3 W_ps W0_ready G_ready "
                "out_ps res_ready stored back_done").split())

        def rows(w, g):
            return w[512 * g:512 * (g + 1), :].rearrange("(o p) d -> p o d", p=128)

        GROUPS = [(rows(qkv_w, g), qkvT[:, :, 512 * g:512 * (g + 1)]) for g in range(3)]
        GROUPS += [(rows(W_l, 0), WlT), (rows(W_r, 0), WrT), (rows(proj_w, 0), projT)]
        EARLY = len(GROUPS)
        GROUPS += [(rows(Wq, g), WqT[:, :, 512 * g:512 * (g + 1)]) for g in range(4)]
        GROUPS += [(rows(e_down, 0), downT)]
        PREP_BANK = [3, 4]

        FROM_ONE = [
            qh_ready, hT_ps, G_ready, xnT_ps, AT_act, v2_ready, hT_ready,
            k_out, stored, q_out, res_ready, AT_dve, xs_ready, AT_ps,
            xnT_ready, kv_done, agg_ready, x1_ready, nrm_ps, agg_out, A_out,
            proj_ready, s_ps, v_out, sc_ready,
        ]

        block = ctx.enter_context(nc.Block())

        @block.sync
        def _(sp):
            for counter in FROM_ONE:
                sp.sem_inc(counter, 1)
            sp.dma_start(edge_i[:, 0, :, :], src.rearrange("(h c t) -> c h t", h=2, t=T)).then_inc(edges_loaded, 16)
            sp.dma_start(edge_i[:, 1, :, :], dst.rearrange("(h c t) -> c h t", h=2, t=T)).then_inc(edges_loaded, 16)
            for g in range(2):
                sp.dma_start(stage[:, g, :, :], GROUPS[g][0]).then_inc(stage_loaded[g], 16)
            sp.dma_start(xs[:, :, :], x.rearrange("(t p) d -> p t d", p=T)).then_inc(x_loaded, 16)
            for g in range(2, EARLY):
                sp.wait_ge(prep_tr, 4 * (g - 1))
                sp.dma_start(stage[:, g % 2, :, :], GROUPS[g][0]).then_inc(stage_loaded[g % 2], 16)
            sp.dma_start(up[:, :, :], e_up[0:512, :].rearrange("(j p) d -> p j d", p=128)).then_inc(up_loaded, 16)
            for g in range(EARLY, len(GROUPS)):
                sp.wait_ge(prep_tr, 4 * (g - 1))
                sp.dma_start(stage[:, g % 2, :, :], GROUPS[g][0]).then_inc(stage_loaded[g % 2], 16)
            with sp.Fori(0, NT) as i:
                sp.wait_ge(res_ready, i + 2)
                sp.dma_start(out[ds(i * T, T), :], res[:, :]).then_inc(stored, 16)
            sp.wait_ge(stored, 16 * NT + 1)

        @block.gpsimd
        def _(pool):
            steps = [0]

            def step(ins):
                steps[0] += 1
                ins.then_inc(pool_step, 1)
                pool.wait_ge(pool_step, steps[0])

            def iota(ap, pattern, base=0):
                step(nc.gpsimd.iota(ap, pattern=pattern, base=base, channel_multiplier=0,
                                    allow_small_or_imprecise_dtypes=True))

            step(nc.gpsimd.memset(ident[:, :], 0.0))
            step(nc.gpsimd.affine_select(out=ident[:, :], in_=ident[:, :], compare_op=ALU.not_equal, fill=1.0, base=0,
                                         pattern=[[-1, 128]], channel_multiplier=1))
            step(nc.gpsimd.memset(bmask, 0.0))
            for b in range(4):
                step(nc.gpsimd.memset(bmask[32 * b:32 * b + 32, 32 * b:32 * b + 32], 1.0))
            for ap, value in ((ones[:, :], 1.0), (minus_half[:, :], -0.5), (zero16[:, :], 0.0), (onesb[:, :], 1.0)):
                step(nc.gpsimd.memset(ap, value))
            iota(iotaN[:, :], [[1, AW]])
            iota(tile_lo, [[T, NT]])
            iota(chunk_up, [[1, NC]], 1)
            iota(chunk_down, [[-1, NC]], NC)
            pool.sem_inc(consts_ready, 1)

            def rsqrt(ap, ready):
                nc.gpsimd.tensor_tensor(ap, ap, minus_half[0:ap.shape[0], 0:ap.shape[1]], ALU.pow).then_inc(ready, 1)

            pool.wait_ge(kss_ready, 1)
            rsqrt(kss[:, :], krs_ready)
            pool.wait_ge(small_loaded, 16 * 6)
            with pool.Fori(0, NT) as i:
                for u in range(2):
                    pool.wait_ge(var1_ready, i * 2 + (u + 1))
                    rsqrt(rs[:, u:u + 1], rstd1_ready)
                pool.wait_ge(xn_ready, i + 1)
                pool.sem_inc(sums_open, 1)
                nc.gpsimd.tensor_tensor(xs[:, ds(i, 1), :], xs[:, ds(i, 1), :], xn.unsqueeze(1), ALU.add)\
                    .then_inc(pad_ready, 1)
                pool.wait_ge(pad_ready, i + 1)
                pool.sem_inc(sums_open, 1)
                nc.gpsimd.tensor_tensor(xs[:, ds(i, 1), :], xs[:, ds(i, 1), :], pb_bc.unsqueeze(1), ALU.add)\
                    .then_inc(xs_ready, 1)
            pool.wait_ge(x1_ready, NT + 1)
            iota(iotaL, [[1, LO], [0, TP]])
            iota(iotaH, [[LO, HI], [0, TP]])
            iota(iotaC, [[1, C], [0, TK]])
            for a in (lo16, hi16, wh16, wl16):
                step(nc.gpsimd.memset(a, 0.0))
            pool.sem_inc(iotas_ready, 1)
            with pool.Fori(0, NT) as i:
                pool.wait_ge(yvar_ready, i + 1)
                rsqrt(rs[:, 0:1], yrstd_ready)
                for j in range(5):
                    if j < 4:
                        a = slice(2 * j, 2 * j + 2)
                        pool.wait_ge(qvar_ready, i * 4 + (j + 1))
                        rsqrt(rs[:, a], qrstd_ready)
                        pool.wait_ge(qrstd_ready, i * 4 + (j + 1))
                        nc.gpsimd.tensor_tensor(nm[:, a], nmean[:, a], rs[:, a], ALU.mult).then_inc(qstat_ready, 1)
                    if j == 0:
                        continue
                    j = j - 1
                    pool.wait_ge(vT_ready, i * 4 + (j + 1))
                    pool.wait_ge(nrm_ps, i * 4 + j + 1)
                    nc.gpsimd.tensor_tensor(v2[:, :, :, :], vT[:, :, :, :], vT[:, :, :, :], ALU.mult)\
                        .then_inc(v2_ready, 1)
                pool.wait_ge(nvar_ready, i + 1)
                rsqrt(nrm[:, :], nrstd_ready)
                pool.wait_ge(topif_ready, i + 1)
                a, b = topif[:, 0, :, :], topif[:, 1, :, :]
                for i0, i1 in ((0, 1), (1, 2), (2, 3), (3, 4), (4, 5), (5, 8), (8, 16)):
                    n, m = ROWS[i0], i1 - i0
                    o = ci[:, :, OFF[i0]:OFF[i0] + m * n].rearrange("p h (i j) -> p h i j", j=n)
                    last = nc.gpsimd.tensor_tensor(
                        o, a[:, :, i0:i1].unsqueeze(3).to_broadcast([T, H, m, n]),
                        b[:, :, 0:n].unsqueeze(2).to_broadcast([T, H, m, n]), ALU.add)
                last.then_inc(ci_ready, 1)

        @block.scalar
        def _(act):
            for dst_ap, src_ap in ((cols[:, 0:4], gamma.rearrange("(c p) -> p c", p=128)),
                                   (cols[:, 4:8], beta.rearrange("(c p) -> p c", p=128)),
                                   (cols[:, 8:10], ln_g.rearrange("(c p) -> p c", p=128)),
                                   (cols[:, 10:12], ln_b.rearrange("(c p) -> p c", p=128))):
                with nc.allow_non_contiguous_dma(reason="short per-feature vectors"):
                    act.dma_start(dst_ap, src_ap).then_inc(small_loaded, 16)
            act.dma_start(bl_bc, b_l.partition_broadcast(T)).then_inc(small_loaded, 16)
            act.dma_start(pb_bc, proj_b.partition_broadcast(T)).then_inc(small_loaded, 16)
            act.dma_start(keys_raw[:, 0:2, :], keys0.rearrange("(o p) d -> p o d", p=128)).then_inc(keys_loaded, 16)
            act.dma_start(keys_raw[:, 2:4, :], keys1.rearrange("(o p) d -> p o d", p=128)).then_inc(keys_loaded, 16)
            for r in range(3):
                act.dma_start(bqf[32 * r:32 * r + 1, :], bq.unsqueeze(0)).then_inc(bq_loaded, 16)

            def prep(g):
                for o in (1, 3):
                    act.wait_ge(prep_tr, 4 * g + o + 1)
                    nc.scalar.activation(GROUPS[g][1][:, :, 128 * o:128 * o + 128],
                                         ps[:, PREP_BANK[1], :].rearrange("p (k q) -> p k q", k=KC), ACT.Copy)\
                        .then_inc(prep_act, 1)

            for g in range(EARLY):
                prep(g)
            act.wait_ge(small_loaded, 16 * 6)
            with act.Fori(0, NT // 2) as i2:
                for u in range(2):
                    i = i2 * 2 + u
                    act.wait_ge(hT_ps, i + 2)
                    for k in range(KC):
                        nc.scalar.activation(hT[:, 0, k, :], ps[:, 1, T * k:T * k + T], ACT.Identity,
                                             scale=gcol[:, k:k + 1], bias=bcol[:, k:k + 1])\
                            .then_inc(hT_ready, 1)
                    act.wait_ge(mm_ready, i * 5 + 1)
                    nc.scalar.activation(P[:, ds(i, 1), :], ps[0:T, 2:3, :], ACT.Copy).then_inc(p_out, 1)
                    act.wait_ge(mm_ready, i * 5 + 3)
                    act.wait_ge(kv_done, i + 1)
                    nc.scalar.activation(kS, ps[0:T, 4, :], ACT.Relu).then_inc(k_out, 1)
                    act.wait_ge(mm_ready, i * 5 + 5)
                    nc.scalar.activation(qT[:, :, ds(i * T, T)],
                                         ps[:, 3, 0:4 * T].rearrange("p (g t) -> p g t", g=4), ACT.Relu)\
                        .then_inc(q_out, 1)
            for g in range(EARLY, len(GROUPS)):
                prep(g)
            with act.Fori(0, NT) as m:
                act.wait_ge(A_ready, m + 1)
                act.wait_ge(AT_ps, m * 3 + 1)
                nc.scalar.activation(As[:, :].rearrange("p (b a) -> p b a", b=3), ps[0:T, 0:3, 0:AB], ACT.Copy,
                                     accum_out=cnt[:, 0:1]).then_inc(A_out, 1)
                act.wait_ge(nd_ready, m + 1)
                act.wait_ge(proj_ready, m + 1)
                nc.scalar.activation(den, ps[:, 6, 0:4 * T].rearrange("p (g t) -> p g t", g=4), ACT.Copy,
                                     bias=EPS_DEN).then_inc(den_out, 1)
                for b in (0, 2):
                    act.wait_ge(AT_ps, m * 3 + (b + 1) + 1)
                    act.wait_ge(agg_ready, m + 1)
                    n = min(4, NT - 4 * b)
                    nc.scalar.activation(AT[:, 4 * b:4 * b + n, :],
                                         ps[0:T, 3, 0:n * T].rearrange("p (s t) -> p s t", s=n), ACT.Copy)\
                        .then_inc(AT_act, 1)
            with act.Fori(0, NT) as i:
                act.wait_ge(inner_ps, i + 1)
                nc.scalar.activation(geluT, ps[:, 7, 0:4 * T].rearrange("p (j t) -> p j t", j=4), ACT.Gelu)\
                    .then_inc(gelu_ready, 1)
                for j in range(4):
                    act.wait_ge(qstat_ready, i * 4 + (j + 1))
                    for h in (2 * j, 2 * j + 1):
                        nc.scalar.activation(qh[:, QD * h:QD * h + QD], ps[0:T, j % 2, QD * (h % 2):QD * (h % 2) + QD],
                                             ACT.Identity, scale=rs[:, h:h + 1], bias=nm[:, h:h + 1])\
                            .then_inc(qh_ready, 1)
                    act.wait_ge(tr_ps, i * 4 + (j + 1))
                    act.wait_ge(s_ps, i * 8 + 2 * j + 1)
                    act.wait_ge(v2_ready, i * 4 + j + 1)
                    for f in range(2):
                        last = nc.scalar.activation(
                            vT[:, f, :, :], ps[:, 2, 2 * T * f:2 * T * f + 2 * T].rearrange("p (h t) -> p h t", h=2),
                            ACT.Identity, scale=lgc[:, f:f + 1], bias=lbc[:, f:f + 1])
                    last.then_inc(vT_ready, 1)
                    for h in (2 * j, 2 * j + 1):
                        act.wait_ge(s_ps, i * 8 + (h + 2))
                        nc.scalar.activation(sc[:, h, :, :],
                                             ps[0:T, 3 + h % 2, :].rearrange("p (f e) -> p f e", f=2), ACT.Copy)\
                            .then_inc(sc_ready, 1)
                act.wait_ge(ci_ready, i + 1)
                nc.scalar.activation(cirep, ci[:, :, :].unsqueeze(3).to_broadcast([T, H, C, TK]), ACT.Copy)\
                    .then_inc(cirep_ready, 1)
                act.wait_ge(exp_in, i + 1)
                nc.scalar.activation(fs[:, :, :], fs[:, :, :], ACT.Exp).then_inc(exp_out, 1)
                act.wait_ge(wT_ps, i + 1)
                nc.scalar.activation(wh16[:, 0:T], ps[:, 7, 0:T], ACT.Copy, scale=WSCALE).then_inc(wh_ready, 1)
                for b in range(2):
                    act.wait_ge(W_ps, i * 2 + (b + 1))
                    n = min(64, T - 64 * b)
                    nc.scalar.activation(W0[:, 64 * b:64 * b + n, :],
                                         ps[:, 5 + b, 0:8 * n].rearrange("p (t j) -> p t j", j=8)[:, :, 0:4],
                                         ACT.Copy, scale=1.0 / WSCALE).then_inc(W0_ready, 1)

        @block.vector
        def _(dve):
            def prep(g):
                for o in (0, 2):
                    dve.wait_ge(prep_tr, 4 * g + o + 1)
                    nc.vector.tensor_copy(GROUPS[g][1][:, :, 128 * o:128 * o + 128],
                                          ps[:, PREP_BANK[0], :].rearrange("p (k q) -> p k q", k=KC))\
                        .then_inc(prep_dve, 1)

            steps = [0]

            def step(ins):
                steps[0] += 1
                ins.then_inc(dve_step, 1)
                dve.wait_ge(dve_step, steps[0])

            def clear_steps(n):
                dve.wait_ge(dve_step, n)
                dve.sem_clear(dve_step)

            dve.wait_ge(edges_loaded, 32)
            step(nc.vector.tensor_copy(edge_f[:, :, :, :], edge_i[:, :, :, :]))
            nc.vector.tensor_reduce(ends[:, 0:2], edge_f[:, 1, :, :], AX.X, ALU.min)
            nc.vector.tensor_reduce(ends[:, 2:4], edge_f[:, 1, :, :], AX.X, ALU.max).then_inc(edge_cast, 1)
            dve.wait_ge(edge_tr, 1)
            nc.vector.tensor_copy(ecol[:, 0:2 * NC], ps[0:T, 7, 0:2 * NC])\
                .then_inc(ecol_ready, 1)
            dve.wait_ge(ends_tr, 1)
            step(nc.vector.tensor_copy(ends_row, ps[0:1, 6, 0:2 * NC].rearrange("p (s c) -> p s c", s=2)))
            dve.wait_ge(consts_ready, 1)
            lo_bc = tile_lo.unsqueeze(2).to_broadcast([1, NT, NC])
            step(nc.vector.tensor_scalar(ends_row[:, 0, :], ends_row[:, 0, :], float(-(T - 1)), None, ALU.add))
            nc.vector.tensor_tensor(ov, ends_row[:, 1:2, :].to_broadcast([1, NT, NC]), lo_bc, ALU.is_ge)
            step(nc.vector.tensor_tensor(ov2, ends_row[:, 0:1, :].to_broadcast([1, NT, NC]), lo_bc, ALU.is_le))
            step(nc.vector.tensor_tensor(ov, ov, ov2, ALU.mult))
            step(nc.vector.tensor_tensor(ov2, ov, chunk_up.unsqueeze(1).to_broadcast([1, NT, NC]), ALU.mult))
            step(nc.vector.tensor_reduce(wlim[:, 1, :], ov2, AX.X, ALU.max))
            step(nc.vector.tensor_tensor(ov2, ov, chunk_down.unsqueeze(1).to_broadcast([1, NT, NC]), ALU.mult))
            step(nc.vector.tensor_reduce(wlim[:, 0, :], ov2, AX.X, ALU.max))
            step(nc.vector.tensor_scalar(wlim[:, 0, :], wlim[:, 0, :], -1.0, float(NC), ALU.mult, ALU.add))
            step(nc.vector.tensor_tensor(wlim[:, 1, :], wlim[:, 1, :], wlim[:, 0, :], ALU.max))
            step(nc.vector.tensor_tensor(wlim[:, 1, :], wlim[:, 1, :], wlim[:, 0, :], ALU.subtract))
            step(nc.vector.memset(wlim[:, 2, 0:1], 0.0))
            for m in range(1, NT):
                step(nc.vector.tensor_tensor(wlim[:, 2, m:m + 1], wlim[:, 2, m - 1:m], wlim[:, 1, m - 1:m], ALU.add))
            nc.vector.tensor_copy(bounds[:, :, :], wlim[:, 0:3, :]).then_inc(bounds_ready, 1)

            for g in range(EARLY):
                prep(g)

            dve.wait_ge(keys_loaded, 32)
            step(nc.vector.tensor_tensor(keysN[:, :, :], keys_raw[:, :, :], keys_raw[:, :, :], ALU.mult))
            step(nc.vector.tensor_reduce(kss[:, :], keysN[:, :, :], AX.X, ALU.add))
            nc.vector.tensor_scalar(kss[:, :], kss[:, :], LEAST_NORM ** 2, None, ALU.max).then_inc(kss_ready, 1)
            dve.wait_ge(krs_ready, 1)
            nc.vector.tensor_tensor(keysN[:, :, :], keys_raw[:, :, :], kss[:, :].unsqueeze(2).to_broadcast([128, 4, 128]),
                                    ALU.mult).then_inc(keys_normed, 1)
            dve.wait_ge(keys_tr, 1)
            nc.vector.tensor_copy(knT[:, :, :], ps[:, 7, :].rearrange("p (f e) -> p f e", f=2)).then_inc(knT_ready, 1)
            dve.wait_ge(bq_loaded, 48)
            step(nc.vector.memset(bq3[:, :], 0.0))
            step(nc.vector.tensor_copy(bq3[0:1, :], bqf[0:1, :]))
            step(nc.vector.tensor_copy(bq3[32:33, :], bqf[32:33, :]))
            step(nc.vector.tensor_tensor(bqf[32:33, :], bqf[32:33, :], bq3[32:33, :], ALU.subtract))
            step(nc.vector.tensor_copy(bq3[32:33, :], bqf[32:33, :]))
            step(nc.vector.tensor_copy(bq3[64:65, :], bqf[64:65, :]))
            step(nc.vector.tensor_tensor(bqf[64:65, :], bqf[64:65, :], bq3[64:65, :], ALU.subtract))
            step(nc.vector.tensor_copy(bq3[64:65, :], bqf[64:65, :]))
            step(nc.vector.tensor_tensor(bqf[64:65, :], bqf[64:65, :], bq3[64:65, :], ALU.subtract))
            nc.vector.tensor_copy(bq3[64:65, :], bqf[64:65, :]).then_inc(bq_ready, 1)

            clear_steps(steps[0])
            dve.wait_ge(x_loaded, 16)
            dve.wait_ge(small_loaded, 16 * 6)
            with dve.Fori(0, NT // 2) as i2:
                for u in range(2):
                    i = i2 * 2 + u
                    nc.vector.bn_stats(bn[:, 0, :], xs[:, ds(i, 1), :].rearrange("p a d -> p (a d)"))\
                        .then_inc(dve_step, 1)
                    dve.wait_ge(dve_step, 1)
                    nc.vector.bn_aggr(mv[:, 0, :], bn[:, 0, :]).then_inc(dve_step, 1)
                    dve.wait_ge(dve_step, 2)
                    nc.vector.tensor_scalar(rs[:, 0:1], mv[:, 0, 1:2], EPS, None, ALU.add)\
                        .then_inc(var1_ready, 1)
                    dve.wait_ge(rstd1_ready, i * 2 + 1)
                    dve.wait_ge(xnT_ps, i + 1)
                    dve.wait_ge(xs_ready, i + 1)
                    nc.vector.tensor_scalar(xn, xs[:, ds(i, 1), :].rearrange("p a d -> p (a d)"), mv[:, 0, 0:1],
                                            rs[:, 0:1], ALU.subtract, ALU.mult).then_inc(xn_ready, 1)
                    dve.wait_ge(xn_ready, i + 1)
                    nc.vector.bn_stats(bn[:, 1, :], xn).then_inc(dve_step, 1)
                    dve.wait_ge(dve_step, 3)
                    nc.vector.bn_aggr(mv[:, 1, :], bn[:, 1, :]).then_inc(dve_step, 1)
                    dve.wait_ge(dve_step, 4)
                    nc.vector.tensor_scalar(rs[:, 1:2], mv[:, 1, 1:2], EPS, None, ALU.add)\
                        .then_inc(var1_ready, 1)
                    dve.wait_ge(rstd1_ready, i * 2 + 2)
                    dve.wait_ge(hT_ps, i + 1)
                    nc.vector.tensor_scalar(xh, xn, mv[:, 1, 0:1], rs[:, 1:2], ALU.subtract, ALU.mult)\
                        .then_inc(xh_ready, 1)
                    dve.wait_ge(xnT_ps, i + 2)
                    dve.wait_ge(kv_done, i + 1)
                    nc.vector.tensor_copy(xnT[:, u, :, :], ps[:, 0, 0:4 * T].rearrange("p (k t) -> p k t", k=KC))\
                        .then_inc(xnT_ready, 1)
                    dve.wait_ge(mm_ready, i * 5 + 2)
                    nc.vector.tensor_tensor(R[:, ds(i, 1), :], ps[0:T, 3:4, :], bl_bc.unsqueeze(1), ALU.add)\
                        .then_inc(r_out, 1)
                    dve.wait_ge(mm_ready, i * 5 + 4)
                    dve.wait_ge(kv_done, i + 1)
                    nc.vector.tensor_copy(vS, ps[0:T, 2, :]).then_inc(v_out, 1)
                    clear_steps(4)
            dve.wait_ge(kv_closed, 1)
            nc.vector.tensor_tensor(Mb[:, :, :], ps[:, 5, :].rearrange("p (g c) -> p g c", g=4),
                                    bmask[:, :].unsqueeze(1).to_broadcast([128, 4, 128]), ALU.mult)
            nc.vector.tensor_copy(ksum[:, :], ps[:, 6, 0:4]).then_inc(attn_ready, 1)
            dve.wait_ge(attn_ready, 1)
            nc.vector.tensor_tensor(Kb[:, :, :], ksum[:, :].unsqueeze(2).to_broadcast([128, 4, 128]),
                                    bmask[:, :].unsqueeze(1).to_broadcast([128, 4, 128]), ALU.mult)\
                .then_inc(attn_ready, 1)
            for g in range(EARLY, len(GROUPS)):
                prep(g)

            dve.wait_ge(xs_ready, NT + 1)
            dve.wait_ge(p_out, NT)
            with dve.Fori(0, NT) as m:
                first = dve.value_load(bounds[0:1, 0, ds(m, 1)], min_val=0, max_val=NC)
                chunks = dve.value_load(bounds[0:1, 1, ds(m, 1)], min_val=0, max_val=NC)
                before = dve.value_load(bounds[0:1, 2, ds(m, 1)], min_val=0, max_val=NC * NT)
                with dve.Fori(0, chunks) as n:
                    k = before + n
                    slot = k % 2
                    dve.wait_ge(onehots_free, k + 1)
                    nc.vector.tensor_scalar(S1[:, ds(slot, 1), :].rearrange("p a n -> p (a n)"), iotaN[:, :],
                                            ecol[:, ds(first + n, 1)], None, ALU.is_equal)
                    nc.vector.tensor_scalar(D1[:, ds(slot, 1), 0:T].rearrange("p a n -> p (a n)"),
                                            iotaN[:, ds(m * T, T)], ecol[:, ds(first + n + NC, 1)], None, ALU.is_equal)\
                        .then_inc(onehots_ready, 1)
                dve.wait_ge(den_out, m + 1)
                nc.vector.reciprocal(den, den).then_inc(dve_step, 1)
                dve.wait_ge(dve_step, 1)
                nc.vector.tensor_tensor(pin, ps[:, 5, 0:4 * T].rearrange("p (g t) -> p g t", g=4), den, ALU.mult)\
                    .then_inc(pin_ready, 1)
                dve.wait_ge(A_out, m + 2)
                nc.vector.tensor_scalar(cnt[:, 1:2], cnt[:, 0:1], 1.0, None, ALU.max).then_inc(dve_step, 1)
                dve.wait_ge(dve_step, 2)
                nc.vector.reciprocal(cnt[:, 1:2], cnt[:, 1:2]).then_inc(dve_step, 1)
                dve.wait_ge(AT_ps, m * 3 + 3)
                dve.wait_ge(agg_ready, m + 1)
                nc.vector.tensor_copy(AT[:, 4:8, :], ps[0:T, 4, 0:4 * T].rearrange("p (s t) -> p s t", s=4))\
                    .then_inc(AT_dve, 1)
                dve.wait_ge(dve_step, 3)
                dve.wait_ge(agg_ready, m + 2)
                nc.vector.scalar_tensor_tensor(out=gnn[:, :].unsqueeze(1), in0=ps[0:T, 7:8, :], scalar=cnt[:, 1:2],
                                               in1=R[:, ds(m, 1), :], op0=ALU.mult, op1=ALU.add)\
                    .then_inc(agg_out, 1)
                dve.wait_ge(agg_out, m + 2)
                nc.vector.scalar_tensor_tensor(out=gnn[:, :].unsqueeze(1), in0=gnn[:, :].unsqueeze(1), scalar=0.0,
                                               in1=xs[:, ds(m, 1), :], op0=ALU.max, op1=ALU.add).then_inc(dve_step, 1)
                dve.wait_ge(dve_step, 4)
                dve.wait_ge(proj_ready, m + 2)
                nc.vector.tensor_tensor(xs[:, ds(m, 1), :], gnn[:, :].unsqueeze(1), ps[0:T, 5:6, :], ALU.add)\
                    .then_inc(x1_ready, 1)
                clear_steps(4)

            PAIRS = ((0, 1), (1, 2), (2, 3), (3, 4), (4, 5), (5, 8), (8, 16))
            dve.wait_ge(iotas_ready, 1)

            def stage3(i):
                count = [0]

                def done(ins):
                    count[0] += 1
                    ins.then_inc(dve_step, 1)
                    return count[0]

                def need(k):
                    dve.wait_ge(dve_step, k)

                k = done(nc.vector.bn_stats(bn[:, 0, :], xs[:, ds(i, 1), :].rearrange("p a d -> p (a d)")))
                need(k)
                k = done(nc.vector.bn_aggr(mv[:, 0, :], bn[:, 0, :]))
                need(k)
                nc.vector.tensor_scalar(rs[:, 0:1], mv[:, 0, 1:2], EPS, None, ALU.add).then_inc(yvar_ready, 1)
                dve.wait_ge(yrstd_ready, i + 1)
                nc.vector.tensor_scalar(y, xs[:, ds(i, 1), :].rearrange("p a d -> p (a d)"), mv[:, 0, 0:1],
                                        rs[:, 0:1], ALU.subtract, ALU.mult).then_inc(y_ready, 1)
                dve.wait_ge(yT_ps, i + 1)
                nc.vector.tensor_copy(yT, ps[:, 7, 0:4 * T].rearrange("p (k t) -> p k t", k=KC)).then_inc(yT_ready, 1)
                for j in range(4):
                    dve.wait_ge(q_ps, i * 4 + (j + 1))
                    hs = (2 * j, 2 * j + 1)
                    for h in hs:
                        k = done(nc.vector.bn_stats(bn[:, h, :], ps[0:T, j % 2, QD * (h % 2):QD * (h % 2) + QD]))
                    need(k)
                    for h in hs:
                        k = done(nc.vector.bn_aggr(mv[:, h, :], bn[:, h, :]))
                    need(k)
                    a = slice(2 * j, 2 * j + 2)
                    nc.vector.tensor_scalar(nmean[:, a], mv[:, a, 0], -1.0, None, ALU.mult)
                    nc.vector.tensor_scalar(rs[:, a], mv[:, a, 1], EPS, None, ALU.add).then_inc(qvar_ready, 1)
                for h in range(H):
                    dve.wait_ge(sc_ready, i * H + (h + 2))
                    dve.sem_inc(scores_seen, 1)
                    for f in range(2):
                        k = done(nc.vector.max(top[:, f, h, 0:8], sc[:, h, f, :]))
                        need(k)
                        k = done(nc.vector.match_replace(sc2[:, f, :], top[:, f, h, 0:8], sc[:, h, f, :], LOWEST))
                        nc.vector.max_index(topi[:, f, h, 0:8], top[:, f, h, 0:8], sc[:, h, f, :])
                        need(k)
                        k = done(nc.vector.max(top[:, f, h, 8:16], sc2[:, f, :]))
                        need(k)
                        k = done(nc.vector.max_index(topi[:, f, h, 8:16], top[:, f, h, 8:16], sc2[:, f, :]))
                dve.wait_ge(nrm_ps, i * 4 + 5)
                k2 = done(nc.vector.tensor_copy(nrm[:, :], norms))
                need(k)
                nc.vector.tensor_copy(topif, topi).then_inc(topif_ready, 1)
                need(k2)
                nc.vector.tensor_scalar(nrm[:, :], nrm[:, :], LEAST_NORM ** 2, None, ALU.max).then_inc(nvar_ready, 1)
                dve.wait_ge(nrstd_ready, i + 1)
                k = done(nc.vector.tensor_tensor(top, top, nrm[:, :].rearrange("p (f h) -> p f h", f=2).unsqueeze(3)
                                                 .to_broadcast([T, 2, H, TK]), ALU.mult))
                need(k)
                a, b = top[:, 0, :, :], top[:, 1, :, :]
                for i0, i1 in PAIRS:
                    n, m = ROWS[i0], i1 - i0
                    o = cs[:, :, OFF[i0]:OFF[i0] + m * n].rearrange("p h (i j) -> p h i j", j=n)
                    k = done(nc.vector.tensor_tensor(
                        o, a[:, :, i0:i1].unsqueeze(3).to_broadcast([T, H, m, n]),
                        b[:, :, 0:n].unsqueeze(2).to_broadcast([T, H, m, n]), ALU.add))
                need(k)
                for h in range(H):
                    k = done(nc.vector.max(fs[:, h, 0:8], cs[:, h, :]))
                    need(k)
                    k = done(nc.vector.match_replace(cs2[:, h % 2, :], fs[:, h, 0:8], cs[:, h, :], LOWEST))
                    nc.vector.max_index(posi[:, h, 0:8], fs[:, h, 0:8], cs[:, h, :])
                    need(k)
                    k = done(nc.vector.max(fs[:, h, 8:16], cs2[:, h % 2, :]))
                    need(k)
                    k = done(nc.vector.max_index(posi[:, h, 8:16], fs[:, h, 8:16], cs2[:, h % 2, :]))
                need(k)
                k_pos = done(nc.vector.tensor_copy(posf[:, :, :], posi[:, :, :]))
                k = done(nc.vector.tensor_copy(esum[:, :], fs[:, :, 0]))
                need(k)
                nc.vector.tensor_tensor(fs[:, :, :], fs[:, :, :], esum[:, :].unsqueeze(2).to_broadcast([T, H, TK]),
                                        ALU.subtract).then_inc(exp_in, 1)
                need(k_pos)
                k = done(nc.vector.tensor_tensor(eq, posf[:, :, :].unsqueeze(2).to_broadcast([T, H, C, TK]),
                                                 iotaC.unsqueeze(1).to_broadcast([T, H, C, TK]), ALU.is_equal))
                need(k)
                dve.wait_ge(cirep_ready, i + 1)
                k = done(nc.vector.tensor_tensor(eq, eq, cirep, ALU.mult))
                need(k)
                for n, m in ((25, 25), (12, 12), (6, 6), (3, 3), (1, 1)):
                    k = done(nc.vector.tensor_tensor(eq[:, :, 0:n, :], eq[:, :, 0:n, :], eq[:, :, n:n + m, :], ALU.add))
                    need(k)
                k = done(nc.vector.tensor_tensor(eq[:, :, 0, :], eq[:, :, 0, :], eq[:, :, 2, :], ALU.add))
                need(k)
                k_fi = done(nc.vector.tensor_tensor(fi[:, :].rearrange("p (h r) -> p h r", h=H), eq[:, :, 0, :],
                                                    eq[:, :, 24, :], ALU.add))
                dve.wait_ge(exp_out, i + 1)
                k = done(nc.vector.tensor_reduce(esum[:, :], fs[:, :, :], AX.X, ALU.add))
                need(k)
                k = done(nc.vector.reciprocal(esum[:, :], esum[:, :]))
                need(k)
                need(k_fi)
                nc.vector.tensor_tensor(fs[:, :, :], fs[:, :, :], esum[:, :].unsqueeze(2).to_broadcast([T, H, TK]),
                                        ALU.mult).then_inc(w_ready, 1)
                dve.wait_ge(wh_ready, i + 1)
                k = done(nc.vector.tensor_copy(lo_i[:, 0, :], ps[:, 7, 128:128 + T]))
                need(k)
                k = done(nc.vector.tensor_single_scalar(lo_i[:, 1, :], lo_i[:, 0, :], LO - 1, ALU.bitwise_and))
                need(k)
                k = done(nc.vector.tensor_copy(lo16[:, 0:T], lo_i[:, 1, :]))
                k = done(nc.vector.tensor_tensor(hi16[:, 0:T], lo_i[:, 0, :], lo_i[:, 1, :], ALU.subtract))
                k = done(nc.vector.scalar_tensor_tensor(out=wl16[:, 0:T], in0=ps[:, 7, 0:T], scalar=WSCALE,
                                                        in1=wh16[:, 0:T], op0=ALU.mult, op1=ALU.subtract))
                need(k)
                nc.vector.tensor_tensor(Lh, lo16[:, :].unsqueeze(1).to_broadcast([128, LO, TP]), iotaL, ALU.is_equal)
                k = done(nc.vector.tensor_tensor(Hh[:, 2, :, :], hi16[:, :].unsqueeze(1).to_broadcast([128, HI, TP]),
                                                 iotaH, ALU.is_equal))
                need(k)
                for s, w in ((0, wh16), (1, wl16)):
                    last = nc.vector.tensor_tensor(Hh[:, s, :, :], Hh[:, 2, :, :],
                                                   w[:, :].unsqueeze(1).to_broadcast([128, HI, TP]), ALU.mult)
                last.then_inc(onehot3, 1)
                dve.wait_ge(W0_ready, i * 2 + 2)
                for b2 in range(2):
                    n = min(64, T - 64 * b2)
                    k = done(nc.vector.scalar_tensor_tensor(
                        out=W0[:, 64 * b2:64 * b2 + n, :],
                        in0=ps[:, 5 + b2, 0:8 * n].rearrange("p (t j) -> p t j", j=8)[:, :, 4:8],
                        scalar=1.0 / WSCALE, in1=W0[:, 64 * b2:64 * b2 + n, :], op0=ALU.mult, op1=ALU.add))
                need(k)
                dve.wait_ge(gelu_ready, i + 1)
                nc.vector.tensor_tensor(GT, W0.rearrange("p t j -> p j t"), geluT, ALU.mult).then_inc(G_ready, 1)
                dve.wait_ge(out_ps, i + 1)
                dve.wait_ge(stored, i * 16 + 1)
                nc.vector.tensor_tensor(res[:, :].unsqueeze(1), xs[:, ds(i, 1), :], ps[0:T, 7:8, :], ALU.add)\
                    .then_inc(res_ready, 1)
                clear_steps(count[0])

            with dve.Fori(0, NT) as i:
                stage3(i)

        @block.tensor
        def _(pe):
            def prep(g):
                pe.wait_ge(stage_loaded[g % 2], 16 * (g // 2 + 1))
                for o in range(4):
                    if 2 * g + o // 2 >= 1:
                        pe.wait_ge(prep_act if o % 2 else prep_dve, 2 * g + o // 2)
                    for k in range(KC):
                        last = nc.tensor.transpose(ps[:, PREP_BANK[o % 2], 128 * k:128 * k + 128],
                                                   stage[:, g % 2, o, 128 * k:128 * k + 128], ident[:, :])
                    last.then_inc(prep_tr, 1)

            pe.wait_ge(consts_ready, 1)
            pe.wait_ge(edge_cast, 1)
            for s in range(2):
                for h in range(2):
                    last = nc.tensor.transpose(ps[0:T, 7, NC * s + CH * h:NC * s + CH * h + CH], edge_f[:, s, h, :],
                                               ident[0:CH, 0:CH])
            last.then_inc(edge_tr, 1)
            for n in range(4):
                last = nc.tensor.transpose(ps[0:1, 6, CH * n:CH * n + CH], ends[:, n:n + 1], ident[0:CH, 0:CH])
            last.then_inc(ends_tr, 1)
            for g in range(EARLY):
                prep(g)
            pe.wait_ge(keys_normed, 1)
            pe.wait_ge(ecol_ready, 1)
            for n in range(4):
                last = nc.tensor.transpose(ps[:, 7, 128 * n:128 * n + 128], keysN[:, n, :], ident[:, :])
            last.then_inc(keys_tr, 1)

            pe.wait_ge(prep_act, 2 * EARLY)
            pe.wait_ge(prep_dve, 2 * EARLY)
            pe.wait_ge(bounds_ready, 1)
            nc.tensor.matmul(ps[:, 5, :], zero16[:, 0:128], zero16[:, :], start=True, stop=False)
            nc.tensor.matmul(ps[:, 6, 0:4], zero16[:, 0:128], zero16[:, 0:4], start=True, stop=False)
            with pe.Fori(0, NT // 2) as i2:
                for u in range(2):
                    i = i2 * 2 + u
                    pe.wait_ge(xn_ready, i + 1)
                    pe.wait_ge(xnT_ready, i + 1)
                    for k in range(KC):
                        last = nc.tensor.transpose(ps[:, 0, T * k:T * k + T], xn[:, 128 * k:128 * k + 128],
                                                   ident[0:T, 0:T])
                    last.then_inc(xnT_ps, 1)
                    pe.wait_ge(xh_ready, i + 1)
                    pe.wait_ge(hT_ready, i * 4 + 1)
                    for k in range(KC):
                        last = nc.tensor.transpose(ps[:, 1, T * k:T * k + T], xh[:, 128 * k:128 * k + 128],
                                                   ident[0:T, 0:T])
                    last.then_inc(hT_ps, 1)
                    pe.wait_ge(hT_ready, i * 4 + 5)

                    def product(bank, lhs, w):
                        for k in range(KC):
                            last = nc.tensor.matmul(ps[0:T, bank, :], lhs[:, k, :], w[:, k, :],
                                                    start=(k == 0), stop=(k == KC - 1))
                        last.then_inc(mm_ready, 1)

                    pe.wait_ge(v_out, i + 1)
                    product(2, hT[:, 0, :, :], WlT)
                    pe.wait_ge(q_out, i + 1)
                    product(3, hT[:, 0, :, :], WrT)
                    pe.wait_ge(xnT_ready, i + 2)
                    pe.wait_ge(k_out, i + 1)
                    product(4, xnT[:, u, :, :], qkvT[:, :, 512:1024])
                    pe.wait_ge(p_out, i + 1)
                    product(2, xnT[:, u, :, :], qkvT[:, :, 1024:1536])
                    pe.wait_ge(r_out, i + 1)
                    for g in range(4):
                        for k in range(KC):
                            last = nc.tensor.matmul(ps[:, 3, T * g:T * g + T], qkvT[:, k, 128 * g:128 * g + 128],
                                                    xnT[:, u, k, :], start=(k == 0), stop=(k == KC - 1))
                    last.then_inc(mm_ready, 1)
                    pe.wait_ge(k_out, i + 2)
                    pe.wait_ge(v_out, i + 2)
                    for g in range(4):
                        c = slice(128 * g, 128 * g + 128)
                        nc.tensor.matmul(ps[:, 5, c], kS[:, c], vS[:, c], start=False, stop=False,
                                         skip_group_check=True)
                        last = nc.tensor.matmul(ps[:, 6, g:g + 1], kS[:, c], ones[0:T, :], start=False, stop=False,
                                                skip_group_check=True)
                    last.then_inc(kv_done, 1)
            nc.tensor.matmul(ps[:, 5, :], zero16[:, 0:128], zero16[:, :], start=False, stop=True)
            nc.tensor.matmul(ps[:, 6, 0:4], zero16[:, 0:128], zero16[:, 0:4], start=False, stop=True).then_inc(kv_closed, 1)
            pe.wait_ge(q_out, NT + 1)
            pe.wait_ge(k_out, NT + 1)
            for g in range(EARLY, len(GROUPS)):
                prep(g)

            pe.wait_ge(attn_ready, 2)
            pe.wait_ge(prep_act, 2 * len(GROUPS))
            pe.wait_ge(prep_dve, 2 * len(GROUPS))
            pe.wait_ge(q_out, NT + 1)
            pe.sem_inc(onehots_free, 2)
            with pe.Fori(0, NT) as m:
                pe.wait_ge(A_out, m + 1)
                for b in range(3):
                    nc.tensor.matmul(ps[0:T, b, 0:AB], zero16[0:1, 0:T], zero16[0:1, 0:AB], start=True, stop=False)
                chunks = pe.value_load(bounds[0:1, 1, ds(m, 1)], min_val=0, max_val=NC)
                before = pe.value_load(bounds[0:1, 2, ds(m, 1)], min_val=0, max_val=NC * NT)
                with pe.Fori(0, chunks) as n:
                    k = before + n
                    slot = k % 2
                    pe.wait_ge(onehots_ready, k + 1)
                    d_ap = D1[:, ds(slot, 1), 0:T].rearrange("p a n -> p (a n)")
                    for b in range(3):
                        last = nc.tensor.matmul(ps[0:T, b, 0:AB], d_ap,
                                                S1[:, ds(slot, 1), AB * b:AB * b + AB].rearrange("p a n -> p (a n)"),
                                                start=False, stop=False, skip_group_check=True)
                    last.then_inc(onehots_free, 1)
                for b in range(3):
                    last = nc.tensor.matmul(ps[0:T, b, 0:AB], zero16[0:1, 0:T], zero16[0:1, 0:AB], start=False, stop=True)
                last.then_inc(A_ready, 1)
                pe.wait_ge(x1_ready, m + 1)
                for g in range(4):
                    q_ap = qT[:, g, ds(m * T, T)]
                    nc.tensor.matmul(ps[:, 5, T * g:T * g + T], Mb[:, g, :], q_ap, start=True, stop=True)
                    last = nc.tensor.matmul(ps[:, 6, T * g:T * g + T], Kb[:, g, :], q_ap, start=True, stop=True)
                last.then_inc(nd_ready, 1)
                pe.wait_ge(A_out, m + 2)
                for b in range(3):
                    if b == 0:
                        pe.wait_ge(AT_act, m * 2 + 1)
                    elif b == 1:
                        pe.wait_ge(AT_dve, m + 1)
                    else:
                        pe.wait_ge(AT_act, m * 2 + 2)
                    for s in range(4 * b, min(4 * b + 4, NT)):
                        last = nc.tensor.transpose(ps[0:T, 3 + b % 2, T * (s % 4):T * (s % 4) + T],
                                                   As[:, T * s:T * s + T], ident[0:T, 0:T])
                    last.then_inc(AT_ps, 1)
                pe.wait_ge(AT_act, m * 2 + 3)
                pe.wait_ge(AT_dve, m + 2)
                pe.wait_ge(agg_out, m + 1)
                for s in range(NT):
                    last = nc.tensor.matmul(ps[0:T, 7, :], AT[:, s, :], P[:, s, :], start=(s == 0),
                                            stop=(s == NT - 1))
                last.then_inc(agg_ready, 1)
                pe.wait_ge(pin_ready, m + 1)
                for g in range(4):
                    last = nc.tensor.matmul(ps[0:T, 5, :], pin[:, g, :], projT[:, g, :], start=(g == 0),
                                            stop=(g == 3))
                last.then_inc(proj_ready, 1)

            pe.wait_ge(x1_ready, NT + 1)
            pe.wait_ge(knT_ready, 1)
            pe.wait_ge(bq_ready, 1)
            pe.wait_ge(up_loaded, 16)
            with pe.Fori(0, NT) as i:
                pe.wait_ge(y_ready, i + 1)
                pe.wait_ge(res_ready, i + 1)
                for k in range(KC):
                    last = nc.tensor.transpose(ps[:, 7, T * k:T * k + T], y[:, 128 * k:128 * k + 128],
                                               ident[0:T, 0:T])
                last.then_inc(yT_ps, 1)
                pe.wait_ge(yT_ready, i + 1)

                def queries(j):
                    if j >= 2:
                        pe.wait_ge(qh_ready, i * 8 + (2 * j - 2 + 1))
                    for k in range(KC):
                        nc.tensor.matmul(ps[0:T, j % 2, :], yT[:, k, :], WqT[:, k, 512 * j:512 * j + 512],
                                         start=(k == 0), stop=False)
                    nc.tensor.matmul(ps[0:T, j % 2, :], onesb[:, :], bq3[:, 512 * j:512 * j + 512], start=False,
                                     stop=True).then_inc(q_ps, 1)

                pe.wait_ge(qh_ready, i * 8 + 1)
                queries(0)
                for j4 in range(4):
                    for k in range(KC):
                        last = nc.tensor.matmul(ps[:, 7, T * j4:T * j4 + T], downT[:, k, 128 * j4:128 * j4 + 128],
                                                yT[:, k, :], start=(k == 0), stop=(k == KC - 1))
                last.then_inc(inner_ps, 1)
                for j in range(4):
                    if j < 3:
                        queries(j + 1)
                    pe.wait_ge(qh_ready, i * 8 + (2 * j + 3))
                    if j:
                        pe.wait_ge(vT_ready, i * 4 + j)
                    for f in range(2):
                        for h in range(2):
                            c0 = QD * (2 * j + h) + 128 * f
                            last = nc.tensor.transpose(ps[:, 2, T * (2 * f + h):T * (2 * f + h) + T],
                                                       qh[:, c0:c0 + 128], ident[0:T, 0:T])
                    last.then_inc(tr_ps, 1)
                    pe.wait_ge(vT_ready, i * 4 + (j + 1))
                    for h in range(2):
                        hh = 2 * j + h
                        pe.wait_ge(sc_ready, i * 8 + max(hh - 1, 0) + 1)
                        for f in range(2):
                            last = nc.tensor.matmul(ps[0:T, 3 + h, NK * f:NK * f + NK], vT[:, f, h, :], knT[:, f, :],
                                                    start=True, stop=True)
                        last.then_inc(s_ps, 1)
                    pe.wait_ge(v2_ready, i * 4 + (j + 2))
                    for h in range(2):
                        for f in range(2):
                            last = nc.tensor.matmul(norms[:, H * f + 2 * j + h:H * f + 2 * j + h + 1], v2[:, f, h, :], ones[:, :], start=True,
                                                    stop=True)
                    last.then_inc(nrm_ps, 1)
                pe.wait_ge(w_ready, i + 1)
                pe.wait_ge(gelu_ready, i + 1)
                nc.tensor.transpose(ps[:, 7, 0:T], fs[:, :, :].rearrange("p h r -> p (h r)"), ident[0:T, 0:T])
                nc.tensor.transpose(ps[:, 7, 128:128 + T], fi[:, :], ident[0:T, 0:T]).then_inc(wT_ps, 1)
                pe.wait_ge(onehot3, i + 1)
                pe.wait_ge(G_ready, i + 1)
                for t in range(T):
                    for g in range(2):
                        last = nc.tensor.matmul(ps[64 * g:64 * g + 64, 5 + t // 64, 8 * (t % 64):8 * (t % 64) + 8],
                                                Lh[:, :, t], Hh[:, 0:2, g:HI:2, t], start=True, stop=True)
                    if t == 63 or t == T - 1:
                        last.then_inc(W_ps, 1)
                pe.wait_ge(G_ready, i + 2)
                for j in range(4):
                    last = nc.tensor.matmul(ps[0:T, 7, :], GT[:, j, :], up[:, j, :], start=(j == 0), stop=(j == 3))
                last.then_inc(out_ps, 1)


_INS = ["x", "src", "dst", "L0_gnn_W_l", "L0_gnn_b_l", "L0_gnn_W_r", "L0_gnn_gamma", "L0_gnn_beta",
        "L0_mix_qkv_weight", "L0_mix_proj_weight", "L0_mix_proj_bias", "L0_ffn_Wq", "L0_ffn_bq", "L0_ffn_ln_g",
        "L0_ffn_ln_b", "L0_ffn_keys0", "L0_ffn_keys1", "L0_ffn_expert_down", "L0_ffn_expert_up"]


def kernel(**inputs):
    import numpy as _np
    import concourse.bacc as _bacc
    from concourse import mybir as _mybir
    from concourse.bass_utils import run_bass_kernel_spmd as _run

    nc = _bacc.Bacc("TRN2", target_bir_lowering=False, num_devices=1)
    arrays, args = {}, []
    for name in _INS:
        a = _np.ascontiguousarray(inputs[name])
        arrays[f"in_{name}"] = a
        args.append(nc.dram_tensor(f"in_{name}", a.shape, _mybir.dt.from_np(a.dtype), kind="ExternalInput").ap())
    args.append(nc.dram_tensor("out", inputs["x"].shape, _mybir.dt.float32, kind="ExternalOutput").ap())
    build(nc, *args)
    r = _run(nc, [arrays], core_ids=[0])
    return r.results[0]["out"]
```

```python
from contextlib import ExitStack

import concourse.bass as bass
from concourse import mybir


def build(nc, x, src, dst, W_l, b_l, W_r, gamma, beta, qkv_w, proj_w, proj_b,
          Wq, bq, ln_g, ln_b, keys0, keys1, e_down, e_up, out):
    dt = mybir.dt
    F32, F16, BF16, I32, U32 = dt.float32, dt.float16, dt.bfloat16, dt.int32, dt.uint32
    ALU = mybir.AluOpType
    ACT = mybir.ActivationFunctionType
    AX = mybir.AxisListType
    ds = bass.ds

    N, D = x.shape
    T = 125
    NT = N // T
    KC = D // 128
    E = src.shape[0]
    NC = E // T
    CH = NC // 2
    AB = 418
    AW = 3 * AB
    EPS = 1e-5
    EPS_DEN = 1e-15
    H, QD = 8, 256
    TK = 16
    NK = keys0.shape[0]
    ROWS = [TK // (i + 1) for i in range(TK)]
    OFF = [sum(ROWS[:i]) for i in range(TK)]
    C = sum(ROWS)
    PAIRS = ((0, 1), (1, 2), (2, 3), (3, 4), (4, 5), (5, 8), (8, 16))
    RING = 4
    LO, HI = 64, 8
    TP = 126
    WSCALE = 1024.0
    LOWEST = -3.0e38
    LEAST_NORM = 1e-12

    ctx = ExitStack()
    with ctx:
        def sb(name, shape, dtype=F32):
            return ctx.enter_context(nc.sbuf_tensor(name, shape, dtype))

        def sem(name):
            return ctx.enter_context(nc.semaphore(name))

        ps = ctx.enter_context(nc.psum_tensor("ps", [128, 8, 512], F32))

        wbig = sb("wbig", [128, KC, 2560])
        qkvT, WlT, WrT = wbig[:, :, 0:1536], wbig[:, :, 1536:2048], wbig[:, :, 2048:2560]
        WqT, downT = wbig[:, :, 0:2048], wbig[:, :, 2048:2560]
        projT = sb("projT", [128, KC, D])
        up = sb("up", [128, KC, D])
        xs = sb("xs", [T, NT, D])
        arena = sb("arena", [128, 25480])
        P = arena[0:T, 0:5120].rearrange("p (t d) -> p t d", d=D)
        R = arena[0:T, 5120:10240].rearrange("p (t d) -> p t d", d=D)
        qT = arena[:, 10240:15240].rearrange("p (g n) -> p g n", n=N)
        stage = arena[:, 15240:19336].rearrange("p (s o d) -> p s o d", s=2, o=4)
        xn = arena[0:T, 19336:19848]
        xh = arena[0:T, 19848:20360]
        kS = arena[0:T, 20360:20872]
        vS = arena[0:T, 20872:21384]
        bl_bc = arena[0:T, 21384:21896]
        pb_bc = arena[0:T, 21896:22408]
        Mb = arena[:, 22408:22920].rearrange("p (g c) -> p g c", g=4)
        Kb = arena[:, 22920:23432].rearrange("p (g c) -> p g c", g=4)
        bq3 = arena[0:65, 24036:25060].bitcast(BF16)
        fs = arena[0:T, 25060:25188].rearrange("p (h r) -> p h r", h=H)
        posi = arena[0:T, 25188:25316].bitcast(U32).rearrange("p (h r) -> p h r", h=H)
        fi = arena[0:T, 25316:25444]
        bmask = arena[:, 23432:23560]
        win = arena[0:1, 8192:10240]
        ends_row = win[:, 512:852].rearrange("p (s c) -> p s c", s=2)
        edge_i = arena[0:CH, 4096:4596].bitcast(I32).rearrange("p (s h t) -> p s h t", s=2, h=2)
        edge_f = arena[0:CH, 4608:5108].rearrange("p (s h t) -> p s h t", s=2, h=2)
        keys_raw = arena[:, 5120:5632].rearrange("p (o d) -> p o d", o=4)
        keysN = arena[:, 5632:6144].rearrange("p (o d) -> p o d", o=4)
        bqf = arena[0:65, 6144:8192]
        tile_lo, chunk_up, chunk_down = win[:, 852:862], win[:, 864:1034], win[:, 1034:1204]
        wlim = win[:, 1204:1244].rearrange("p (s m) -> p s m", s=4)
        ov = arena[0:1, 0:1700].rearrange("p (m c) -> p m c", c=NC)
        ov2 = arena[0:1, 1700:3400].rearrange("p (m c) -> p m c", c=NC)
        ring_end = 15240 + RING * AW
        S1 = arena[0:T, 15240:ring_end].bitcast(F16).rearrange("p (s u n) -> p s u n", s=RING, u=2)
        D1 = arena[0:T, ring_end:ring_end + RING * 128].bitcast(F16).rearrange("p (s u n) -> p s u n", s=RING, u=2)
        meanS = arena[0:T, 21280:21792]
        projS = arena[0:T, 21792:22304]
        qh = arena[0:T, 0:2048]
        sc = arena[0:T, 2048:6144].rearrange("p (h f e) -> p h f e", h=H, f=2)
        sc2 = arena[0:T, 6144:6656].rearrange("p (f e) -> p f e", f=2)
        eq = arena[0:T, 6656:9856].bitcast(F16).rearrange("p (h c r) -> p h c r", h=H, r=TK)
        cirep = arena[0:T, 9856:13056].bitcast(F16).rearrange("p (h c r) -> p h c r", h=H, r=TK)
        Lh = arena[:, 13056:17088].bitcast(F16).rearrange("p (q t) -> p q t", t=TP)
        iotaL = arena[:, 17088:21120].bitcast(F16).rearrange("p (q t) -> p q t", t=TP)
        Hh = arena[:, 21120:22632].bitcast(F16).rearrange("p (s q t) -> p s q t", s=3, t=TP)
        iotaH = iotaL[:, 0:HI, :]
        gelu2 = arena[:, 22632:24440].rearrange("p (s w) -> p s w", s=2)[:, :, 0:4 * T]
        iotaC = arena[0:T, 23136:23536].bitcast(F16).rearrange("p (c r) -> p c r", r=TK)

        ident = sb("ident", [128, 128])
        ones = sb("ones", [128, 1])
        zero16 = sb("zero16", [1, 512], F16)
        iotaN = sb("iotaN", [T, AW], F16)
        ecol = sb("ecol", [T, 3 * NC])
        ends = sb("ends", [CH, 4])
        bounds = sb("bounds", [1, 3, NT], I32)
        side = sb("side", [128, 3760])
        As = side[0:T, AW:2 * AW]
        AT = side[0:T, 2 * AW:2 * AW + NT * T].rearrange("p (s t) -> p s t", s=NT)
        y = side[0:T, 0:512]
        vT = side[:, 512:1012].rearrange("p (f h t) -> p f h t", f=2, h=2)
        v2 = side[:, 1012:1512].rearrange("p (f h t) -> p f h t", f=2, h=2)
        top = side[0:T, 1512:1768].rearrange("p (f h r) -> p f h r", f=2, h=H)
        topi = side[0:T, 1768:2024].bitcast(U32).rearrange("p (f h r) -> p f h r", f=2, h=H)
        topif = side[0:T, 2024:2280].rearrange("p (f h r) -> p f h r", f=2, h=H)
        cs = side[0:T, 2280:2680].rearrange("p (h c) -> p h c", h=H)
        ci = side[0:T, 2680:3080].rearrange("p (h c) -> p h c", h=H)
        lo_i = side[:, 3180:3430].bitcast(I32).rearrange("p (s t) -> p s t", s=2)
        lo16, hi16, wh16, wl16 = (side[:, 3430 + 63 * n:3493 + 63 * n].bitcast(F16) for n in range(4))
        posf = side[0:T, 3682:3746].bitcast(F16).rearrange("p (h r) -> p h r", h=H)
        cs2 = side[0:T, 3080:3180].rearrange("p (s c) -> p s c", s=2)
        xnT = sb("xnT", [128, 2, KC, T])
        hT = sb("hT", [128, 1, KC, T])
        ksum = sb("ksum", [128, 4])
        den = xnT[:, 0, :, :]
        pin = xnT[:, 1, :, :]
        gnn = sb("gnn", [T, D])
        cols = sb("cols", [128, 12])
        gcol, bcol, lgc, lbc = cols[:, 0:4], cols[:, 4:8], cols[:, 8:10], cols[:, 10:12]
        bn = sb("bn", [T, H, 6])
        mv = sb("mv", [T, H, 2])
        rs = sb("rs", [T, H])
        nm = sb("nm", [T, H])
        cnt = sb("cnt", [T, 2])
        knT = sb("knT", [128, 2, NK])
        kss = sb("kss", [128, 4])
        onesb = sb("onesb", [65, T], BF16)
        yT = xnT[:, 0, :, :]
        W0 = xnT[:, 1, :, :].rearrange("p k t -> p (k t)").rearrange("p (t j) -> p t j", j=4)
        GT = hT[:, 0, :, :]
        nrm = sb("nrm", [T, 2 * H])
        nmean = sb("nmean", [T, H])
        minus_half = sb("minus_half", [128, 16])
        esum = sb("esum", [T, H])
        res = gnn

        norms = ps[0:T, 6, 488:504]

        scores_seen, sums_open, kv_closed, gelu_open, nrm_copied = map(
            sem, "scores_seen sums_open kv_closed gelu_open nrm_copied".split())
        kss_ready, krs_ready, var1_ready, rstd1_ready, yvar_ready, yrstd_ready, qvar_ready, qrstd_ready, nvar_ready, \
            nrstd_ready = map(sem, ("kss_ready krs_ready var1_ready rstd1_ready yvar_ready yrstd_ready qvar_ready "
                                    "qrstd_ready nvar_ready nrstd_ready").split())
        x_loaded, edges_loaded, small_loaded, keys_loaded, up_loaded, bq_loaded = map(
            sem, "x_loaded edges_loaded small_loaded keys_loaded up_loaded bq_loaded".split())
        stage_loaded = [sem("stage_loaded0"), sem("stage_loaded1")]
        pool_step, consts_ready, pad_ready, iotas_ready = map(sem, "pool_step consts_ready pad_ready iotas_ready".split())
        prep_tr, prep_act, prep_dve = map(sem, "prep_tr prep_act prep_dve".split())
        edge_cast, edge_tr, ecol_ready, ends_ready, ends_tr, bounds_ready = map(
            sem, "edge_cast edge_tr ecol_ready ends_ready ends_tr bounds_ready".split())
        keys_normed, keys_tr, knT_ready, bq_ready = map(sem, "keys_normed keys_tr knT_ready bq_ready".split())
        dve_step = sem("dve_step")
        xn_ready, xh_ready, xs_ready, xnT_ps, hT_ps, xnT_ready, hT_ready = map(
            sem, "xn_ready xh_ready xs_ready xnT_ps hT_ps xnT_ready hT_ready".split())
        mm_ready, p_out, r_out, k_out, v_out, q_out, kv_done = map(
            sem, "mm_ready p_out r_out k_out v_out q_out kv_done".split())
        attn_ready = sem("attn_ready")
        onehots_free, onehots_ready, A_ready, A_out, AT_ps, AT_act, agg_ready, nd_ready, den_out, pin_ready, \
            proj_ready, x1_ready, mean_out, proj_out, degree_ready, pads_ready = map(sem, (
                "onehots_free onehots_ready A_ready A_out AT_ps AT_act agg_ready nd_ready den_out pin_ready "
                "proj_ready x1_ready mean_out proj_out degree_ready pads_ready").split())
        y_ready, yT_ps, yT_ready, inner_ps, gelu_ready, q_ps, qstat_ready, qh_ready, tr_ps, vT_ready, v2_ready, \
            nrm_ps, nrm_out, s_ps, sc_ready, topk_done = map(sem, (
                "y_ready yT_ps yT_ready inner_ps gelu_ready q_ps qstat_ready qh_ready tr_ps vT_ready v2_ready nrm_ps "
                "nrm_out s_ps sc_ready topk_done").split())
        topif_ready, ci_ready, cirep_ready, exp_in, exp_out, w_ready, wT_ps, wh_ready, onehot3, W_ps, W0_ready, \
            G_ready, out_ps, res_ready, stored, back_done = map(sem, (
                "topif_ready ci_ready cirep_ready exp_in exp_out w_ready wT_ps wh_ready onehot3 W_ps W0_ready G_ready "
                "out_ps res_ready stored back_done").split())

        def rows(w, g):
            return w[512 * g:512 * (g + 1), :].rearrange("(o p) d -> p o d", p=128)

        GROUPS = [(rows(qkv_w, g), qkvT[:, :, 512 * g:512 * (g + 1)]) for g in range(3)]
        GROUPS += [(rows(W_l, 0), WlT), (rows(W_r, 0), WrT), (rows(proj_w, 0), projT)]
        EARLY = len(GROUPS)
        GROUPS += [(rows(Wq, g), WqT[:, :, 512 * g:512 * (g + 1)]) for g in range(4)]
        GROUPS += [(rows(e_down, 0), downT)]
        PREP_BANK = [3, 4]

        FROM_ONE = [
            qh_ready, hT_ps, G_ready, xnT_ps, AT_act, v2_ready, hT_ready,
            k_out, stored, q_out, res_ready, xs_ready, AT_ps, mean_out, proj_out,
            xnT_ready, kv_done, agg_ready, x1_ready, nrm_ps, A_out, degree_ready, pin_ready,
            proj_ready, s_ps, v_out, sc_ready, vT_ready,
        ]

        def iterations(eng, prologue, iteration):
            prologue()
            iteration(0, None, 1, 2)
            with eng.Fori(1, NT - 2) as i:
                iteration(i, i - 1, i + 1, i + 2)
            iteration(NT - 2, NT - 3, NT - 1, None)
            iteration(NT - 1, NT - 2, None, None)

        def tiles(eng, iteration, last):
            iteration(0, None, None)
            iteration(1, 0, None)
            with eng.Fori(2, NT) as m:
                iteration(m, m - 1, m - 2)
            last()

        block = ctx.enter_context(nc.Block())

        @block.sync
        def _(sp):
            for counter in FROM_ONE:
                sp.sem_inc(counter, 1)
            sp.dma_start(edge_i[:, 0, :, :], src.rearrange("(h c t) -> c h t", h=2, t=T)).then_inc(edges_loaded, 16)
            sp.dma_start(edge_i[:, 1, :, :], dst.rearrange("(h c t) -> c h t", h=2, t=T)).then_inc(edges_loaded, 16)
            for g in range(2):
                sp.dma_start(stage[:, g, :, :], GROUPS[g][0]).then_inc(stage_loaded[g], 16)
            sp.dma_start(xs[:, :, :], x.rearrange("(t p) d -> p t d", p=T)).then_inc(x_loaded, 16)
            for g in range(2, EARLY):
                sp.wait_ge(prep_tr, 4 * (g - 1))
                sp.dma_start(stage[:, g % 2, :, :], GROUPS[g][0]).then_inc(stage_loaded[g % 2], 16)
            sp.dma_start(up[:, :, :], e_up[0:512, :].rearrange("(j p) d -> p j d", p=128)).then_inc(up_loaded, 16)
            for g in range(EARLY, len(GROUPS)):
                sp.wait_ge(prep_tr, 4 * (g - 1))
                sp.dma_start(stage[:, g % 2, :, :], GROUPS[g][0]).then_inc(stage_loaded[g % 2], 16)
            with sp.Fori(0, NT) as i:
                sp.wait_ge(res_ready, i + 2)
                sp.dma_start(out[ds(i * T, T), :], res[:, :]).then_inc(stored, 16)
            sp.wait_ge(stored, 16 * NT + 1)

        @block.gpsimd
        def _(pool):
            steps = [0]

            def step(ins):
                steps[0] += 1
                ins.then_inc(pool_step, 1)
                pool.wait_ge(pool_step, steps[0])

            def iota(ap, pattern, base=0):
                step(nc.gpsimd.iota(ap, pattern=pattern, base=base, channel_multiplier=0,
                                    allow_small_or_imprecise_dtypes=True))

            step(nc.gpsimd.memset(ident[:, :], 0.0))
            step(nc.gpsimd.affine_select(out=ident[:, :], in_=ident[:, :], compare_op=ALU.not_equal, fill=1.0, base=0,
                                         pattern=[[-1, 128]], channel_multiplier=1))
            step(nc.gpsimd.memset(bmask, 0.0))
            for b in range(4):
                step(nc.gpsimd.memset(bmask[32 * b:32 * b + 32, 32 * b:32 * b + 32], 1.0))
            for ap, value in ((ones[:, :], 1.0), (minus_half[:, :], -0.5), (zero16[:, :], 0.0), (onesb[:, :], 1.0)):
                step(nc.gpsimd.memset(ap, value))
            iota(iotaN[:, :], [[1, AW]])
            iota(tile_lo, [[T, NT]])
            iota(chunk_up, [[1, NC]], 1)
            iota(chunk_down, [[-1, NC]], NC)
            pool.sem_inc(consts_ready, 1)

            def rsqrt(ap, ready):
                nc.gpsimd.tensor_tensor(ap, ap, minus_half[0:ap.shape[0], 0:ap.shape[1]], ALU.pow).then_inc(ready, 1)

            pool.wait_ge(kss_ready, 1)
            rsqrt(kss[:, :], krs_ready)
            pool.wait_ge(small_loaded, 16 * 6)
            with pool.Fori(0, NT) as i:
                for u in range(2):
                    pool.wait_ge(var1_ready, i * 2 + (u + 1))
                    rsqrt(rs[:, u:u + 1], rstd1_ready)
                pool.wait_ge(xn_ready, i + 1)
                pool.sem_inc(sums_open, 1)
                nc.gpsimd.tensor_tensor(xs[:, ds(i, 1), :], xs[:, ds(i, 1), :], xn.unsqueeze(1), ALU.add)\
                    .then_inc(pad_ready, 1)
                pool.wait_ge(pad_ready, i + 1)
                pool.sem_inc(sums_open, 1)
                nc.gpsimd.tensor_tensor(xs[:, ds(i, 1), :], xs[:, ds(i, 1), :], pb_bc.unsqueeze(1), ALU.add)\
                    .then_inc(xs_ready, 1)

            def norm_x1(n):
                pool.wait_ge(yvar_ready, n + 1)
                rsqrt(rs[:, 0:1], yrstd_ready)

            def stats(n, j):
                a = slice(2 * j, 2 * j + 2)
                pool.wait_ge(qvar_ready, n * 4 + (j + 1))
                rsqrt(rs[:, a], qrstd_ready)
                pool.wait_ge(qrstd_ready, n * 4 + (j + 1))
                nc.gpsimd.tensor_tensor(nm[:, a], nmean[:, a], rs[:, a], ALU.mult).then_inc(qstat_ready, 1)

            def squares(n, j):
                pool.wait_ge(vT_ready, n * 4 + (j + 2))
                pool.wait_ge(nrm_ps, n * 4 + (j + 1))
                nc.gpsimd.tensor_tensor(v2, vT, vT, ALU.mult).then_inc(v2_ready, 1)

            def inverse_norms(n):
                pool.wait_ge(nvar_ready, n + 1)
                rsqrt(nrm[:, :], nrstd_ready)

            def index_sums(i):
                pool.wait_ge(topif_ready, i + 1)
                a, b = topif[:, 0, :, :], topif[:, 1, :, :]
                for i0, i1 in PAIRS:
                    n, m = ROWS[i0], i1 - i0
                    o = ci[:, :, OFF[i0]:OFF[i0] + m * n].rearrange("p h (i j) -> p h i j", j=n)
                    last = nc.gpsimd.tensor_tensor(
                        o, a[:, :, i0:i1].unsqueeze(3).to_broadcast([T, H, m, n]),
                        b[:, :, 0:n].unsqueeze(2).to_broadcast([T, H, m, n]), ALU.add)
                last.then_inc(ci_ready, 1)

            def prologue():
                norm_x1(0)
                stats(0, 0)
                stats(0, 1)
                squares(0, 0)
                stats(0, 2)
                squares(0, 1)
                stats(0, 3)
                squares(0, 2)
                squares(0, 3)
                inverse_norms(0)
                norm_x1(1)
                pool.wait_ge(x1_ready, NT + 1)
                iota(iotaC, [[1, C], [0, TK]])
                iota(iotaL, [[1, LO], [0, TP]])
                for a in (lo16, hi16, wh16, wl16):
                    step(nc.gpsimd.memset(a, 0.0))
                pool.sem_inc(iotas_ready, 1)

            def iteration(i, p, n, n2):
                if n is not None:
                    stats(n, 0)
                    stats(n, 1)
                    squares(n, 0)
                    stats(n, 2)
                    squares(n, 1)
                    stats(n, 3)
                if n2 is not None:
                    norm_x1(n2)
                index_sums(i)
                if n is not None:
                    squares(n, 2)
                    squares(n, 3)
                    inverse_norms(n)

            iterations(pool, prologue, iteration)

        @block.scalar
        def _(act):
            for dst_ap, src_ap in ((cols[:, 0:4], gamma.rearrange("(c p) -> p c", p=128)),
                                   (cols[:, 4:8], beta.rearrange("(c p) -> p c", p=128)),
                                   (cols[:, 8:10], ln_g.rearrange("(c p) -> p c", p=128)),
                                   (cols[:, 10:12], ln_b.rearrange("(c p) -> p c", p=128))):
                with nc.allow_non_contiguous_dma(reason="short per-feature vectors"):
                    act.dma_start(dst_ap, src_ap).then_inc(small_loaded, 16)
            act.dma_start(bl_bc, b_l.partition_broadcast(T)).then_inc(small_loaded, 16)
            act.dma_start(pb_bc, proj_b.partition_broadcast(T)).then_inc(small_loaded, 16)
            act.dma_start(keys_raw[:, 0:2, :], keys0.rearrange("(o p) d -> p o d", p=128)).then_inc(keys_loaded, 16)
            act.dma_start(keys_raw[:, 2:4, :], keys1.rearrange("(o p) d -> p o d", p=128)).then_inc(keys_loaded, 16)
            for r in range(3):
                act.dma_start(bqf[32 * r:32 * r + 1, :], bq.unsqueeze(0)).then_inc(bq_loaded, 16)

            def prep(g):
                for o in (1, 3):
                    act.wait_ge(prep_tr, 4 * g + o + 1)
                    nc.scalar.activation(GROUPS[g][1][:, :, 128 * o:128 * o + 128],
                                         ps[:, PREP_BANK[1], :].rearrange("p (k q) -> p k q", k=KC), ACT.Copy)\
                        .then_inc(prep_act, 1)

            for g in range(EARLY):
                prep(g)
            act.wait_ge(small_loaded, 16 * 6)
            with act.Fori(0, NT // 2) as i2:
                for u in range(2):
                    i = i2 * 2 + u
                    act.wait_ge(hT_ps, i + 2)
                    for k in range(KC):
                        nc.scalar.activation(hT[:, 0, k, :], ps[:, 1, T * k:T * k + T], ACT.Identity,
                                             scale=gcol[:, k:k + 1], bias=bcol[:, k:k + 1])\
                            .then_inc(hT_ready, 1)
                    act.wait_ge(mm_ready, i * 5 + 1)
                    nc.scalar.activation(P[:, ds(i, 1), :], ps[0:T, 2:3, :], ACT.Copy).then_inc(p_out, 1)
                    act.wait_ge(mm_ready, i * 5 + 3)
                    act.wait_ge(kv_done, i + 1)
                    nc.scalar.activation(kS, ps[0:T, 4, :], ACT.Relu).then_inc(k_out, 1)
                    act.wait_ge(mm_ready, i * 5 + 5)
                    nc.scalar.activation(qT[:, :, ds(i * T, T)],
                                         ps[:, 3, 0:4 * T].rearrange("p (g t) -> p g t", g=4), ACT.Relu)\
                        .then_inc(q_out, 1)
            for g in range(EARLY, len(GROUPS)):
                prep(g)
            def mean_and_projection(p):
                act.wait_ge(agg_ready, p + 2)
                act.wait_ge(x1_ready, p + 1)
                nc.scalar.activation(meanS, ps[0:T, 7, :], ACT.Identity, scale=cnt[:, 1:2]).then_inc(mean_out, 1)
                act.wait_ge(proj_ready, p + 2)
                nc.scalar.activation(projS, ps[0:T, 5, :], ACT.Copy).then_inc(proj_out, 1)

            def counts_out(m, b):
                act.wait_ge(AT_ps, m * 3 + (b + 2))
                n = min(4, NT - 4 * b)
                nc.scalar.activation(AT[:, 4 * b:4 * b + n, :],
                                     ps[0:T, 3 + b % 2, 0:n * T].rearrange("p (s t) -> p s t", s=n), ACT.Copy)\
                    .then_inc(AT_act, 1)

            def iteration2(m, p, q):
                act.wait_ge(A_ready, m + 1)
                act.wait_ge(AT_ps, m * 3 + 1)
                act.wait_ge(degree_ready, m + 1)
                nc.scalar.activation(As[:, :].rearrange("p (b a) -> p b a", b=3), ps[0:T, 0:3, 0:AB], ACT.Copy,
                                     accum_out=cnt[:, 0:1]).then_inc(A_out, 1)
                if p is not None:
                    mean_and_projection(p)
                counts_out(m, 0)
                counts_out(m, 1)
                act.wait_ge(nd_ready, m + 1)
                act.wait_ge(pin_ready, m + 1)
                nc.scalar.activation(den, ps[:, 6, 0:4 * T].rearrange("p (g t) -> p g t", g=4), ACT.Copy,
                                     bias=EPS_DEN).then_inc(den_out, 1)
                counts_out(m, 2)

            tiles(act, iteration2, lambda: mean_and_projection(NT - 1))
            def queries_in(n):
                act.wait_ge(yT_ps, n + 1)
                nc.scalar.activation(yT, ps[:, 2, 0:4 * T].rearrange("p (k t) -> p k t", k=KC), ACT.Copy)\
                    .then_inc(yT_ready, 1)

            def center(n, j):
                act.wait_ge(qstat_ready, n * 4 + (j + 1))
                for h in (2 * j, 2 * j + 1):
                    nc.scalar.activation(qh[:, QD * h:QD * h + QD], ps[0:T, j % 2, QD * (h % 2):QD * (h % 2) + QD],
                                         ACT.Identity, scale=rs[:, h:h + 1], bias=nm[:, h:h + 1])\
                        .then_inc(qh_ready, 1)

            def affine(n, j):
                act.wait_ge(tr_ps, n * 4 + (j + 1))
                act.wait_ge(s_ps, n * 8 + (2 * j + 1))
                act.wait_ge(v2_ready, n * 4 + (j + 1))
                for f in range(2):
                    last = nc.scalar.activation(
                        vT[:, f, :, :], ps[:, 2, 2 * T * f:2 * T * f + 2 * T].rearrange("p (h t) -> p h t", h=2),
                        ACT.Identity, scale=lgc[:, f:f + 1], bias=lbc[:, f:f + 1])
                last.then_inc(vT_ready, 1)

            def scores_out(n, j, cur):
                for h in (2 * j, 2 * j + 1):
                    if cur is not None:
                        act.wait_ge(topk_done, cur * 8 + (h + 1))
                    act.wait_ge(s_ps, n * 8 + (h + 2))
                    nc.scalar.activation(sc[:, h, :, :],
                                         ps[0:T, 3 + h % 2, :].rearrange("p (f e) -> p f e", f=2), ACT.Copy)\
                        .then_inc(sc_ready, 1)

            def activate(n, p):
                if p is not None:
                    act.wait_ge(G_ready, n)
                act.wait_ge(inner_ps, n + 1)
                act.sem_inc(gelu_open, 1)
                nc.scalar.activation(gelu2[:, ds(n % 2, 1), :], ps[:, 7:8, 0:4 * T], ACT.Gelu)\
                    .then_inc(gelu_ready, 1)

            def spread_sums(i, half):
                if half == 0:
                    act.wait_ge(ci_ready, i + 1)
                a = slice(4 * half, 4 * half + 4)
                nc.scalar.activation(cirep[:, a, :, :], ci[:, a, :].unsqueeze(3).to_broadcast([T, 4, C, TK]), ACT.Copy)\
                    .then_inc(cirep_ready, 1)

            def expert_weights_out(p):
                for b in range(2):
                    act.wait_ge(W_ps, p * 2 + (b + 1))
                    c = min(64, T - 64 * b)
                    nc.scalar.activation(W0[:, 64 * b:64 * b + c, :],
                                         ps[:, 5 + b, 0:8 * c].rearrange("p (t j) -> p t j", j=8)[:, :, 0:4],
                                         ACT.Copy, scale=1.0 / WSCALE).then_inc(W0_ready, 1)

            def scores(n, cur, p):
                affine(n, 0)
                scores_out(n, 0, cur)
                center(n, 2)
                affine(n, 1)
                scores_out(n, 1, cur)
                center(n, 3)
                affine(n, 2)
                activate(n, p)
                scores_out(n, 2, cur)
                affine(n, 3)
                if cur is not None:
                    spread_sums(cur, 0)
                scores_out(n, 3, cur)
                if cur is not None:
                    spread_sums(cur, 1)

            def prologue():
                queries_in(0)
                center(0, 0)
                center(0, 1)
                scores(0, None, None)
                queries_in(1)

            def iteration(i, p, n, n2):
                if n is not None:
                    center(n, 0)
                    center(n, 1)
                if p is not None:
                    expert_weights_out(p)
                if n is not None:
                    scores(n, i, p)
                else:
                    spread_sums(i, 0)
                    spread_sums(i, 1)
                if n2 is not None:
                    queries_in(n2)
                act.wait_ge(exp_in, i + 1)
                nc.scalar.activation(fs[:, :, :], fs[:, :, :], ACT.Exp).then_inc(exp_out, 1)
                act.wait_ge(wT_ps, i + 1)
                nc.scalar.activation(wh16[:, 0:T], ps[:, 7, 0:T], ACT.Copy, scale=WSCALE).then_inc(wh_ready, 1)

            iterations(act, prologue, iteration)
            expert_weights_out(NT - 1)

        @block.vector
        def _(dve):
            def prep(g):
                for o in (0, 2):
                    dve.wait_ge(prep_tr, 4 * g + o + 1)
                    nc.vector.tensor_copy(GROUPS[g][1][:, :, 128 * o:128 * o + 128],
                                          ps[:, PREP_BANK[0], :].rearrange("p (k q) -> p k q", k=KC))\
                        .then_inc(prep_dve, 1)

            steps = [0]

            def step(ins):
                steps[0] += 1
                ins.then_inc(dve_step, 1)
                dve.wait_ge(dve_step, steps[0])

            def clear_steps(n):
                dve.wait_ge(dve_step, n)
                dve.sem_clear(dve_step)

            dve.wait_ge(edges_loaded, 32)
            step(nc.vector.tensor_copy(edge_f[:, :, :, :], edge_i[:, :, :, :]))
            nc.vector.tensor_reduce(ends[:, 0:2], edge_f[:, 1, :, :], AX.X, ALU.min)
            nc.vector.tensor_reduce(ends[:, 2:4], edge_f[:, 1, :, :], AX.X, ALU.max).then_inc(edge_cast, 1)
            dve.wait_ge(edge_tr, 1)
            nc.vector.tensor_copy(ecol[:, 0:2 * NC], ps[0:T, 7, 0:2 * NC])\
                .then_inc(ecol_ready, 1)
            nc.vector.memset(ecol[:, 2 * NC:2 * NC + 1], -1.0).then_inc(pads_ready, 1)
            dve.wait_ge(ends_tr, 1)
            step(nc.vector.tensor_copy(ends_row, ps[0:1, 6, 0:2 * NC].rearrange("p (s c) -> p s c", s=2)))
            dve.wait_ge(consts_ready, 1)
            lo_bc = tile_lo.unsqueeze(2).to_broadcast([1, NT, NC])
            step(nc.vector.tensor_scalar(ends_row[:, 0, :], ends_row[:, 0, :], float(-(T - 1)), None, ALU.add))
            nc.vector.tensor_tensor(ov, ends_row[:, 1:2, :].to_broadcast([1, NT, NC]), lo_bc, ALU.is_ge)
            step(nc.vector.tensor_tensor(ov2, ends_row[:, 0:1, :].to_broadcast([1, NT, NC]), lo_bc, ALU.is_le))
            step(nc.vector.tensor_tensor(ov, ov, ov2, ALU.mult))
            step(nc.vector.tensor_tensor(ov2, ov, chunk_up.unsqueeze(1).to_broadcast([1, NT, NC]), ALU.mult))
            step(nc.vector.tensor_reduce(wlim[:, 1, :], ov2, AX.X, ALU.max))
            step(nc.vector.tensor_tensor(ov2, ov, chunk_down.unsqueeze(1).to_broadcast([1, NT, NC]), ALU.mult))
            step(nc.vector.tensor_reduce(wlim[:, 0, :], ov2, AX.X, ALU.max))
            step(nc.vector.tensor_scalar(wlim[:, 0, :], wlim[:, 0, :], -1.0, float(NC), ALU.mult, ALU.add))
            step(nc.vector.tensor_tensor(wlim[:, 1, :], wlim[:, 1, :], wlim[:, 0, :], ALU.max))
            step(nc.vector.tensor_tensor(wlim[:, 1, :], wlim[:, 1, :], wlim[:, 0, :], ALU.subtract))
            step(nc.vector.tensor_scalar(wlim[:, 1, :], wlim[:, 1, :], 1.0, None, ALU.add))
            step(nc.vector.tensor_copy(bounds[:, 1, :], wlim[:, 1, :]))
            step(nc.vector.tensor_single_scalar(bounds[:, 1, :], bounds[:, 1, :], 1, ALU.logical_shift_right))
            step(nc.vector.tensor_copy(wlim[:, 1, :], bounds[:, 1, :]))
            step(nc.vector.memset(wlim[:, 2, 0:1], 0.0))
            for m in range(1, NT):
                step(nc.vector.tensor_tensor(wlim[:, 2, m:m + 1], wlim[:, 2, m - 1:m], wlim[:, 1, m - 1:m], ALU.add))
            nc.vector.tensor_copy(bounds[:, :, :], wlim[:, 0:3, :]).then_inc(bounds_ready, 1)

            for g in range(EARLY):
                prep(g)

            dve.wait_ge(keys_loaded, 32)
            step(nc.vector.tensor_tensor(keysN[:, :, :], keys_raw[:, :, :], keys_raw[:, :, :], ALU.mult))
            step(nc.vector.tensor_reduce(kss[:, :], keysN[:, :, :], AX.X, ALU.add))
            nc.vector.tensor_scalar(kss[:, :], kss[:, :], LEAST_NORM ** 2, None, ALU.max).then_inc(kss_ready, 1)
            dve.wait_ge(krs_ready, 1)
            nc.vector.tensor_tensor(keysN[:, :, :], keys_raw[:, :, :], kss[:, :].unsqueeze(2).to_broadcast([128, 4, 128]),
                                    ALU.mult).then_inc(keys_normed, 1)
            dve.wait_ge(keys_tr, 1)
            nc.vector.tensor_copy(knT[:, :, :], ps[:, 7, :].rearrange("p (f e) -> p f e", f=2)).then_inc(knT_ready, 1)
            dve.wait_ge(bq_loaded, 48)
            step(nc.vector.memset(bq3[:, :], 0.0))
            step(nc.vector.tensor_copy(bq3[0:1, :], bqf[0:1, :]))
            step(nc.vector.tensor_copy(bq3[32:33, :], bqf[32:33, :]))
            step(nc.vector.tensor_tensor(bqf[32:33, :], bqf[32:33, :], bq3[32:33, :], ALU.subtract))
            step(nc.vector.tensor_copy(bq3[32:33, :], bqf[32:33, :]))
            step(nc.vector.tensor_copy(bq3[64:65, :], bqf[64:65, :]))
            step(nc.vector.tensor_tensor(bqf[64:65, :], bqf[64:65, :], bq3[64:65, :], ALU.subtract))
            step(nc.vector.tensor_copy(bq3[64:65, :], bqf[64:65, :]))
            step(nc.vector.tensor_tensor(bqf[64:65, :], bqf[64:65, :], bq3[64:65, :], ALU.subtract))
            nc.vector.tensor_copy(bq3[64:65, :], bqf[64:65, :]).then_inc(bq_ready, 1)

            clear_steps(steps[0])
            dve.wait_ge(x_loaded, 16)
            dve.wait_ge(small_loaded, 16 * 6)
            with dve.Fori(0, NT // 2) as i2:
                for u in range(2):
                    i = i2 * 2 + u
                    nc.vector.bn_stats(bn[:, 0, :], xs[:, ds(i, 1), :].rearrange("p a d -> p (a d)"))\
                        .then_inc(dve_step, 1)
                    dve.wait_ge(dve_step, 1)
                    nc.vector.bn_aggr(mv[:, 0, :], bn[:, 0, :]).then_inc(dve_step, 1)
                    dve.wait_ge(dve_step, 2)
                    nc.vector.tensor_scalar(rs[:, 0:1], mv[:, 0, 1:2], EPS, None, ALU.add)\
                        .then_inc(var1_ready, 1)
                    dve.wait_ge(rstd1_ready, i * 2 + 1)
                    dve.wait_ge(xnT_ps, i + 1)
                    dve.wait_ge(xs_ready, i + 1)
                    nc.vector.tensor_scalar(xn, xs[:, ds(i, 1), :].rearrange("p a d -> p (a d)"), mv[:, 0, 0:1],
                                            rs[:, 0:1], ALU.subtract, ALU.mult).then_inc(xn_ready, 1)
                    dve.wait_ge(xn_ready, i + 1)
                    nc.vector.bn_stats(bn[:, 1, :], xn).then_inc(dve_step, 1)
                    dve.wait_ge(dve_step, 3)
                    nc.vector.bn_aggr(mv[:, 1, :], bn[:, 1, :]).then_inc(dve_step, 1)
                    dve.wait_ge(dve_step, 4)
                    nc.vector.tensor_scalar(rs[:, 1:2], mv[:, 1, 1:2], EPS, None, ALU.add)\
                        .then_inc(var1_ready, 1)
                    dve.wait_ge(rstd1_ready, i * 2 + 2)
                    dve.wait_ge(hT_ps, i + 1)
                    nc.vector.tensor_scalar(xh, xn, mv[:, 1, 0:1], rs[:, 1:2], ALU.subtract, ALU.mult)\
                        .then_inc(xh_ready, 1)
                    dve.wait_ge(xnT_ps, i + 2)
                    dve.wait_ge(kv_done, i + 1)
                    nc.vector.tensor_copy(xnT[:, u, :, :], ps[:, 0, 0:4 * T].rearrange("p (k t) -> p k t", k=KC))\
                        .then_inc(xnT_ready, 1)
                    dve.wait_ge(mm_ready, i * 5 + 2)
                    nc.vector.tensor_tensor(R[:, ds(i, 1), :], ps[0:T, 3:4, :], bl_bc.unsqueeze(1), ALU.add)\
                        .then_inc(r_out, 1)
                    dve.wait_ge(mm_ready, i * 5 + 4)
                    dve.wait_ge(kv_done, i + 1)
                    nc.vector.tensor_copy(vS, ps[0:T, 2, :]).then_inc(v_out, 1)
                    clear_steps(4)
            dve.wait_ge(kv_closed, 1)
            nc.vector.tensor_tensor(Mb[:, :, :], ps[:, 5, :].rearrange("p (g c) -> p g c", g=4),
                                    bmask[:, :].unsqueeze(1).to_broadcast([128, 4, 128]), ALU.mult)
            nc.vector.tensor_copy(ksum[:, :], ps[:, 6, 0:4]).then_inc(attn_ready, 1)
            dve.wait_ge(attn_ready, 1)
            nc.vector.tensor_tensor(Kb[:, :, :], ksum[:, :].unsqueeze(2).to_broadcast([128, 4, 128]),
                                    bmask[:, :].unsqueeze(1).to_broadcast([128, 4, 128]), ALU.mult)\
                .then_inc(attn_ready, 1)
            for g in range(EARLY, len(GROUPS)):
                prep(g)

            dve.wait_ge(xs_ready, NT + 1)
            dve.wait_ge(p_out, NT)
            dve.wait_ge(pads_ready, 1)

            def onehots(m):
                first = dve.value_load(bounds[0:1, 0, ds(m, 1)], min_val=0, max_val=NC)
                pairs = dve.value_load(bounds[0:1, 1, ds(m, 1)], min_val=0, max_val=CH)
                before = dve.value_load(bounds[0:1, 2, ds(m, 1)], min_val=0, max_val=CH * NT)
                with dve.Fori(0, pairs) as n:
                    k = before + n
                    slot = k % RING
                    dve.wait_ge(onehots_free, k + 1)
                    for u in range(2):
                        nc.vector.tensor_scalar(S1[:, ds(slot, 1), u, :].rearrange("p a n -> p (a n)"), iotaN[:, :],
                                                ecol[:, ds(first + n * 2 + u, 1)], None, ALU.is_equal)
                        last = nc.vector.tensor_scalar(D1[:, ds(slot, 1), u, 0:T].rearrange("p a n -> p (a n)"),
                                                       iotaN[:, ds(m * T, T)], ecol[:, ds(first + n * 2 + (u + NC), 1)],
                                                       None, ALU.is_equal)
                    last.then_inc(onehots_ready, 1)

            def attend(p):
                dve.wait_ge(A_out, p + 2)
                dve.wait_ge(mean_out, p + 1)
                nc.vector.tensor_scalar(cnt[:, 1:2], cnt[:, 0:1], 1.0, None, ALU.max).then_inc(dve_step, 1)
                dve.wait_ge(dve_step, 1)
                nc.vector.reciprocal(cnt[:, 1:2], cnt[:, 1:2]).then_inc(degree_ready, 1)
                dve.wait_ge(den_out, p + 1)
                nc.vector.reciprocal(den, den).then_inc(dve_step, 1)
                dve.wait_ge(dve_step, 2)
                nc.vector.tensor_tensor(pin, ps[:, 5, 0:4 * T].rearrange("p (g t) -> p g t", g=4), den, ALU.mult)\
                    .then_inc(pin_ready, 1)

            def sum_up(q, k=2):
                dve.wait_ge(mean_out, q + 2)
                nc.vector.tensor_tensor(gnn[:, :].unsqueeze(1), meanS.unsqueeze(1), R[:, ds(q, 1), :], ALU.add)\
                    .then_inc(dve_step, 1)
                dve.wait_ge(dve_step, k + 1)
                nc.vector.scalar_tensor_tensor(out=gnn[:, :].unsqueeze(1), in0=gnn[:, :].unsqueeze(1), scalar=0.0,
                                               in1=xs[:, ds(q, 1), :], op0=ALU.max, op1=ALU.add).then_inc(dve_step, 1)
                dve.wait_ge(dve_step, k + 2)
                dve.wait_ge(proj_out, q + 2)
                nc.vector.tensor_tensor(xs[:, ds(q, 1), :], gnn[:, :].unsqueeze(1), projS.unsqueeze(1), ALU.add)\
                    .then_inc(x1_ready, 1)

            def iteration2(m, p, q):
                onehots(m)
                if p is not None:
                    attend(p)
                if q is not None:
                    sum_up(q)
                if p is not None:
                    clear_steps(2 if q is None else 4)

            def last_tiles():
                attend(NT - 1)
                sum_up(NT - 2)
                clear_steps(4)
                sum_up(NT - 1, 0)
                clear_steps(2)

            tiles(dve, iteration2, last_tiles)

            count = [0]

            def done(ins):
                count[0] += 1
                ins.then_inc(dve_step, 1)
                return count[0]

            def need(k):
                dve.wait_ge(dve_step, k)

            def norm_x1_stats(n):
                need(done(nc.vector.bn_stats(bn[:, 0, :], xs[:, ds(n, 1), :].rearrange("p a d -> p (a d)"))))
                need(done(nc.vector.bn_aggr(mv[:, 0, :], bn[:, 0, :])))
                nc.vector.tensor_scalar(rs[:, 0:1], mv[:, 0, 1:2], EPS, None, ALU.add).then_inc(yvar_ready, 1)

            def norm_x1(n):
                dve.wait_ge(yrstd_ready, n + 1)
                nc.vector.tensor_scalar(y, xs[:, ds(n, 1), :].rearrange("p a d -> p (a d)"), mv[:, 0, 0:1],
                                        rs[:, 0:1], ALU.subtract, ALU.mult).then_inc(y_ready, 1)

            def query_stats(n, j):
                dve.wait_ge(q_ps, n * 4 + (j + 1))
                hs = (2 * j, 2 * j + 1)
                a = slice(2 * j, 2 * j + 2)
                for h in hs:
                    k = done(nc.vector.bn_stats(bn[:, h, :], ps[0:T, j % 2, QD * (h % 2):QD * (h % 2) + QD]))
                need(k)
                for h in hs:
                    k = done(nc.vector.bn_aggr(mv[:, h, :], bn[:, h, :]))
                need(k)
                nc.vector.tensor_scalar(nmean[:, a], mv[:, a, 0], -1.0, None, ALU.mult)
                nc.vector.tensor_scalar(rs[:, a], mv[:, a, 1], EPS, None, ALU.add).then_inc(qvar_ready, 1)

            def two_rounds(pairs):
                k = [done(nc.vector.max(v[:, 0:8], x)) for x, x2, v, p in pairs]
                k2 = []
                for (x, x2, v, p), kk in zip(pairs, k):
                    need(kk)
                    k2.append(done(nc.vector.match_replace(x2, v[:, 0:8], x, LOWEST)))
                    nc.vector.max_index(p[:, 0:8], v[:, 0:8], x)
                k = []
                for (x, x2, v, p), kk in zip(pairs, k2):
                    need(kk)
                    k.append(done(nc.vector.max(v[:, 8:16], x2)))
                for (x, x2, v, p), kk in zip(pairs, k):
                    need(kk)
                    last = nc.vector.max_index(p[:, 8:16], v[:, 8:16], x2)
                return last

            def sort_scores(i, h):
                dve.wait_ge(sc_ready, i * H + (h + 2))
                dve.sem_inc(scores_seen, 1)
                two_rounds([(sc[:, h, f, :], sc2[:, f, :], top[:, f, h, :], topi[:, f, h, :]) for f in range(2)])\
                    .then_inc(topk_done, 1)

            def norms_out(n):
                dve.wait_ge(nrm_ps, n * 4 + 5)
                need(done(nc.vector.tensor_copy(nrm[:, :], norms)))
                nc.vector.tensor_scalar(nrm[:, :], nrm[:, :], LEAST_NORM ** 2, None, ALU.max).then_inc(nvar_ready, 1)

            def pair_and_weigh(i, n, n2):
                dve.wait_ge(topk_done, i * H + H)
                nc.vector.tensor_copy(topif, topi).then_inc(topif_ready, 1)
                if n2 is not None:
                    norm_x1_stats(n2)
                dve.wait_ge(nrstd_ready, i + 1)
                k = done(nc.vector.tensor_tensor(top, top, nrm[:, :].rearrange("p (f h) -> p f h", f=2).unsqueeze(3)
                                                 .to_broadcast([T, 2, H, TK]), ALU.mult))
                need(k)
                a, b = top[:, 0, :, :], top[:, 1, :, :]
                for i0, i1 in PAIRS:
                    w, m = ROWS[i0], i1 - i0
                    o = cs[:, :, OFF[i0]:OFF[i0] + m * w].rearrange("p h (i j) -> p h i j", j=w)
                    k = done(nc.vector.tensor_tensor(
                        o, a[:, :, i0:i1].unsqueeze(3).to_broadcast([T, H, m, w]),
                        b[:, :, 0:w].unsqueeze(2).to_broadcast([T, H, m, w]), ALU.add))
                need(k)
                if n2 is not None:
                    norm_x1(n2)
                for h2 in range(0, H, 2):
                    k = done(two_rounds([(cs[:, h, :], cs2[:, h % 2, :], fs[:, h, :], posi[:, h, :])
                                         for h in (h2, h2 + 1)]))
                need(k)
                k_pos = done(nc.vector.tensor_copy(posf, posi))
                k = done(nc.vector.tensor_copy(esum[:, :], fs[:, :, 0]))
                need(k)
                nc.vector.tensor_tensor(fs, fs, esum[:, :].unsqueeze(2).to_broadcast([T, H, TK]),
                                        ALU.subtract).then_inc(exp_in, 1)
                k = done(nc.vector.tensor_tensor(eq, posf.unsqueeze(2).to_broadcast([T, H, C, TK]),
                                                 iotaC.unsqueeze(1).to_broadcast([T, H, C, TK]), ALU.is_equal))
                need(k)
                for half in range(2):
                    g = slice(4 * half, 4 * half + 4)
                    dve.wait_ge(cirep_ready, i * 2 + (half + 1))
                    k = done(nc.vector.tensor_tensor(eq[:, g, :, :], eq[:, g, :, :], cirep[:, g, :, :], ALU.mult))
                need(k)
                for w, m in ((25, 25), (12, 12), (6, 6), (3, 3), (1, 1)):
                    k = done(nc.vector.tensor_tensor(eq[:, :, 0:w, :], eq[:, :, 0:w, :], eq[:, :, w:w + m, :], ALU.add))
                    need(k)
                k = done(nc.vector.tensor_tensor(eq[:, :, 0, :], eq[:, :, 0, :], eq[:, :, 2, :], ALU.add))
                need(k)
                k_fi = done(nc.vector.tensor_tensor(fi.rearrange("p (h r) -> p h r", h=H), eq[:, :, 0, :],
                                                    eq[:, :, 24, :], ALU.add))
                dve.wait_ge(exp_out, i + 1)
                k = done(nc.vector.tensor_reduce(esum[:, :], fs, AX.X, ALU.add))
                need(k)
                k = done(nc.vector.reciprocal(esum[:, :], esum[:, :]))
                need(k)
                nc.vector.tensor_tensor(fs, fs, esum[:, :].unsqueeze(2).to_broadcast([T, H, TK]),
                                        ALU.mult).then_inc(w_ready, 1)
                if n is not None:
                    norms_out(n)
                dve.wait_ge(wh_ready, i + 1)
                k = done(nc.vector.tensor_copy(lo_i[:, 0, :], ps[:, 7, 128:128 + T]))
                k_w = done(nc.vector.scalar_tensor_tensor(out=wl16[:, 0:T], in0=ps[:, 7, 0:T], scalar=WSCALE,
                                                          in1=wh16[:, 0:T], op0=ALU.mult, op1=ALU.subtract))
                need(k)
                k = done(nc.vector.tensor_single_scalar(lo_i[:, 1, :], lo_i[:, 0, :], LO - 1, ALU.bitwise_and))
                k_h = done(nc.vector.tensor_single_scalar(lo_i[:, 0, :], lo_i[:, 0, :], 6, ALU.logical_shift_right))
                need(k)
                k = done(nc.vector.tensor_copy(lo16[:, 0:T], lo_i[:, 1, :]))
                need(k_h)
                k_h = done(nc.vector.tensor_copy(hi16[:, 0:T], lo_i[:, 0, :]))
                need(k)
                nc.vector.tensor_tensor(Lh, lo16.unsqueeze(1).to_broadcast([128, LO, TP]), iotaL, ALU.is_equal)
                need(k_h)
                k = done(nc.vector.tensor_tensor(Hh[:, 2, :, :], hi16.unsqueeze(1).to_broadcast([128, HI, TP]),
                                                 iotaH, ALU.is_equal))
                need(k)
                for s, w in ((0, wh16), (1, wl16)):
                    last = nc.vector.tensor_tensor(Hh[:, s, :, :], Hh[:, 2, :, :],
                                                   w.unsqueeze(1).to_broadcast([128, HI, TP]), ALU.mult)
                last.then_inc(onehot3, 1)

            def apply_weights(p):
                dve.wait_ge(W0_ready, p * 2 + 2)
                for b2 in range(2):
                    c = min(64, T - 64 * b2)
                    k = done(nc.vector.scalar_tensor_tensor(
                        out=W0[:, 64 * b2:64 * b2 + c, :],
                        in0=ps[:, 5 + b2, 0:8 * c].rearrange("p (t j) -> p t j", j=8)[:, :, 4:8],
                        scalar=1.0 / WSCALE, in1=W0[:, 64 * b2:64 * b2 + c, :], op0=ALU.mult, op1=ALU.add))
                need(k)
                dve.wait_ge(gelu_ready, p + 1)
                nc.vector.tensor_tensor(GT, W0.rearrange("p t j -> p j t"),
                                        gelu2[:, ds(p % 2, 1), :].rearrange("p a (j t) -> p (a j) t", t=T),
                                        ALU.mult).then_inc(G_ready, 1)

            def finish(p):
                dve.wait_ge(out_ps, p + 1)
                dve.wait_ge(stored, p * 16 + 1)
                nc.vector.tensor_tensor(res[:, :].unsqueeze(1), xs[:, ds(p, 1), :], ps[0:T, 7:8, :], ALU.add)\
                    .then_inc(res_ready, 1)

            def prologue():
                norm_x1_stats(0)
                norm_x1(0)
                for j in range(4):
                    query_stats(0, j)
                norms_out(0)
                norm_x1_stats(1)
                norm_x1(1)
                clear_steps(count[0])
                count[0] = 0

            def iteration(i, p, n, n2):
                if n is not None:
                    query_stats(n, 0)
                    query_stats(n, 1)
                for h in range(4):
                    sort_scores(i, h)
                if p is not None:
                    apply_weights(p)
                sort_scores(i, 4)
                if n is not None:
                    query_stats(n, 2)
                sort_scores(i, 5)
                if p is not None:
                    finish(p)
                sort_scores(i, 6)
                if n is not None:
                    query_stats(n, 3)
                sort_scores(i, 7)
                if p is None:
                    dve.wait_ge(iotas_ready, 1)
                pair_and_weigh(i, n, n2)
                clear_steps(count[0])
                count[0] = 0

            iterations(dve, prologue, iteration)
            apply_weights(NT - 1)
            finish(NT - 1)

        @block.tensor
        def _(pe):
            def prep(g):
                pe.wait_ge(stage_loaded[g % 2], 16 * (g // 2 + 1))
                for o in range(4):
                    if 2 * g + o // 2 >= 1:
                        pe.wait_ge(prep_act if o % 2 else prep_dve, 2 * g + o // 2)
                    for k in range(KC):
                        last = nc.tensor.transpose(ps[:, PREP_BANK[o % 2], 128 * k:128 * k + 128],
                                                   stage[:, g % 2, o, 128 * k:128 * k + 128], ident[:, :])
                    last.then_inc(prep_tr, 1)

            pe.wait_ge(consts_ready, 1)
            pe.wait_ge(edge_cast, 1)
            for s in range(2):
                for h in range(2):
                    last = nc.tensor.transpose(ps[0:T, 7, NC * s + CH * h:NC * s + CH * h + CH], edge_f[:, s, h, :],
                                               ident[0:CH, 0:CH])
            last.then_inc(edge_tr, 1)
            for n in range(4):
                last = nc.tensor.transpose(ps[0:1, 6, CH * n:CH * n + CH], ends[:, n:n + 1], ident[0:CH, 0:CH])
            last.then_inc(ends_tr, 1)
            for g in range(EARLY):
                prep(g)
            pe.wait_ge(keys_normed, 1)
            pe.wait_ge(ecol_ready, 1)
            for n in range(4):
                last = nc.tensor.transpose(ps[:, 7, 128 * n:128 * n + 128], keysN[:, n, :], ident[:, :])
            last.then_inc(keys_tr, 1)

            pe.wait_ge(prep_act, 2 * EARLY)
            pe.wait_ge(prep_dve, 2 * EARLY)
            pe.wait_ge(bounds_ready, 1)
            nc.tensor.matmul(ps[:, 5, :], zero16[:, 0:128], zero16[:, :], start=True, stop=False)
            nc.tensor.matmul(ps[:, 6, 0:4], zero16[:, 0:128], zero16[:, 0:4], start=True, stop=False)
            with pe.Fori(0, NT // 2) as i2:
                for u in range(2):
                    i = i2 * 2 + u
                    pe.wait_ge(xn_ready, i + 1)
                    pe.wait_ge(xnT_ready, i + 1)
                    for k in range(KC):
                        last = nc.tensor.transpose(ps[:, 0, T * k:T * k + T], xn[:, 128 * k:128 * k + 128],
                                                   ident[0:T, 0:T])
                    last.then_inc(xnT_ps, 1)
                    pe.wait_ge(xh_ready, i + 1)
                    pe.wait_ge(hT_ready, i * 4 + 1)
                    for k in range(KC):
                        last = nc.tensor.transpose(ps[:, 1, T * k:T * k + T], xh[:, 128 * k:128 * k + 128],
                                                   ident[0:T, 0:T])
                    last.then_inc(hT_ps, 1)
                    pe.wait_ge(hT_ready, i * 4 + 5)

                    def product(bank, lhs, w):
                        for k in range(KC):
                            last = nc.tensor.matmul(ps[0:T, bank, :], lhs[:, k, :], w[:, k, :],
                                                    start=(k == 0), stop=(k == KC - 1))
                        last.then_inc(mm_ready, 1)

                    pe.wait_ge(v_out, i + 1)
                    product(2, hT[:, 0, :, :], WlT)
                    pe.wait_ge(q_out, i + 1)
                    product(3, hT[:, 0, :, :], WrT)
                    pe.wait_ge(xnT_ready, i + 2)
                    pe.wait_ge(k_out, i + 1)
                    product(4, xnT[:, u, :, :], qkvT[:, :, 512:1024])
                    pe.wait_ge(p_out, i + 1)
                    product(2, xnT[:, u, :, :], qkvT[:, :, 1024:1536])
                    pe.wait_ge(r_out, i + 1)
                    for g in range(4):
                        for k in range(KC):
                            last = nc.tensor.matmul(ps[:, 3, T * g:T * g + T], qkvT[:, k, 128 * g:128 * g + 128],
                                                    xnT[:, u, k, :], start=(k == 0), stop=(k == KC - 1))
                    last.then_inc(mm_ready, 1)
                    pe.wait_ge(k_out, i + 2)
                    pe.wait_ge(v_out, i + 2)
                    for g in range(4):
                        c = slice(128 * g, 128 * g + 128)
                        nc.tensor.matmul(ps[:, 5, c], kS[:, c], vS[:, c], start=False, stop=False,
                                         skip_group_check=True)
                        last = nc.tensor.matmul(ps[:, 6, g:g + 1], kS[:, c], ones[0:T, :], start=False, stop=False,
                                                skip_group_check=True)
                    last.then_inc(kv_done, 1)
            nc.tensor.matmul(ps[:, 5, :], zero16[:, 0:128], zero16[:, :], start=False, stop=True)
            nc.tensor.matmul(ps[:, 6, 0:4], zero16[:, 0:128], zero16[:, 0:4], start=False, stop=True).then_inc(kv_closed, 1)
            pe.wait_ge(q_out, NT + 1)
            pe.wait_ge(k_out, NT + 1)
            for g in range(EARLY, len(GROUPS)):
                prep(g)

            pe.wait_ge(attn_ready, 2)
            pe.wait_ge(prep_act, 2 * len(GROUPS))
            pe.wait_ge(prep_dve, 2 * len(GROUPS))
            pe.wait_ge(q_out, NT + 1)
            pe.sem_inc(onehots_free, RING)

            def counts(m):
                pe.wait_ge(A_out, m + 1)
                for b in range(3):
                    nc.tensor.matmul(ps[0:T, b, 0:AB], zero16[0:1, 0:T], zero16[0:1, 0:AB], start=True, stop=False)
                pairs = pe.value_load(bounds[0:1, 1, ds(m, 1)], min_val=0, max_val=CH)
                before = pe.value_load(bounds[0:1, 2, ds(m, 1)], min_val=0, max_val=CH * NT)
                with pe.Fori(0, pairs) as n:
                    k = before + n
                    slot = k % RING
                    pe.wait_ge(onehots_ready, k + 1)
                    for u in range(2):
                        d_ap = D1[:, ds(slot, 1), u, 0:T].rearrange("p a n -> p (a n)")
                        for b in range(3):
                            last = nc.tensor.matmul(ps[0:T, b, 0:AB], d_ap,
                                                    S1[:, ds(slot, 1), u, AB * b:AB * b + AB].rearrange("p a n -> p (a n)"),
                                                    start=False, stop=False, skip_group_check=True)
                    last.then_inc(onehots_free, 1)
                for b in range(3):
                    last = nc.tensor.matmul(ps[0:T, b, 0:AB], zero16[0:1, 0:T], zero16[0:1, 0:AB], start=False, stop=True)
                last.then_inc(A_ready, 1)

            def aggregate(p):
                pe.wait_ge(AT_act, p * 3 + 4)
                pe.wait_ge(mean_out, p + 1)
                for s in range(NT):
                    last = nc.tensor.matmul(ps[0:T, 7, :], AT[:, s, :], P[:, s, :], start=(s == 0),
                                            stop=(s == NT - 1))
                last.then_inc(agg_ready, 1)

            def project(p):
                pe.wait_ge(pin_ready, p + 2)
                for g in range(4):
                    last = nc.tensor.matmul(ps[0:T, 5, :], pin[:, g, :], projT[:, g, :], start=(g == 0),
                                            stop=(g == 3))
                last.then_inc(proj_ready, 1)

            def transpose_counts(m, b):
                if b == 0:
                    pe.wait_ge(A_out, m + 2)
                    pe.wait_ge(AT_act, m * 3 + 1)
                elif b == 2:
                    pe.wait_ge(AT_act, m * 3 + 2)
                for s in range(4 * b, min(4 * b + 4, NT)):
                    last = nc.tensor.transpose(ps[0:T, 3 + b % 2, T * (s % 4):T * (s % 4) + T],
                                               As[:, T * s:T * s + T], ident[0:T, 0:T])
                last.then_inc(AT_ps, 1)

            def attention(m):
                pe.wait_ge(proj_out, m + 1)
                for g in range(4):
                    q_ap = qT[:, g, ds(m * T, T)]
                    nc.tensor.matmul(ps[:, 5, T * g:T * g + T], Mb[:, g, :], q_ap, start=True, stop=True)
                    last = nc.tensor.matmul(ps[:, 6, T * g:T * g + T], Kb[:, g, :], q_ap, start=True, stop=True)
                last.then_inc(nd_ready, 1)

            def iteration2(m, p, q):
                counts(m)
                if p is not None:
                    aggregate(p)
                    project(p)
                transpose_counts(m, 0)
                transpose_counts(m, 1)
                attention(m)
                transpose_counts(m, 2)

            def last_tile():
                aggregate(NT - 1)
                project(NT - 1)

            tiles(pe, iteration2, last_tile)

            pe.wait_ge(x1_ready, NT + 1)
            pe.wait_ge(knT_ready, 1)
            pe.wait_ge(bq_ready, 1)
            pe.wait_ge(up_loaded, 16)

            def queries(n, j):
                pe.wait_ge(qh_ready, n * 8 + max(2 * j - 2, 0) + 1)
                for k in range(KC):
                    nc.tensor.matmul(ps[0:T, j % 2, :], yT[:, k, :], WqT[:, k, 512 * j:512 * j + 512],
                                     start=(k == 0), stop=False)
                nc.tensor.matmul(ps[0:T, j % 2, :], onesb[:, :], bq3[:, 512 * j:512 * j + 512], start=False,
                                 stop=True).then_inc(q_ps, 1)

            def head(n):
                pe.wait_ge(y_ready, n + 1)
                pe.wait_ge(vT_ready, n * 4 + 1)
                for k in range(KC):
                    last = nc.tensor.transpose(ps[:, 2, T * k:T * k + T], y[:, 128 * k:128 * k + 128],
                                               ident[0:T, 0:T])
                last.then_inc(yT_ps, 1)
                pe.wait_ge(yT_ready, n + 1)
                queries(n, 0)

            def transpose_queries(n, j):
                pe.wait_ge(qh_ready, n * 8 + (2 * j + 3))
                pe.wait_ge(vT_ready, n * 4 + (j + 1))
                for f in range(2):
                    for h in range(2):
                        c0 = QD * (2 * j + h) + 128 * f
                        last = nc.tensor.transpose(ps[:, 2, T * (2 * f + h):T * (2 * f + h) + T],
                                                   qh[:, c0:c0 + 128], ident[0:T, 0:T])
                last.then_inc(tr_ps, 1)

            def scores(n, j):
                pe.wait_ge(vT_ready, n * 4 + (j + 2))
                for h in range(2):
                    hh = 2 * j + h
                    pe.wait_ge(sc_ready, n * 8 + (max(hh - 1, 0) + 1))
                    for f in range(2):
                        last = nc.tensor.matmul(ps[0:T, 3 + h, NK * f:NK * f + NK], vT[:, f, h, :], knT[:, f, :],
                                                start=True, stop=True)
                    last.then_inc(s_ps, 1)

            def query_norms(n, j):
                pe.wait_ge(v2_ready, n * 4 + (j + 2))
                for h in range(2):
                    for f in range(2):
                        c = H * f + 2 * j + h
                        last = nc.tensor.matmul(norms[:, c:c + 1], v2[:, f, h, :], ones[:, :], start=True,
                                                stop=True)
                last.then_inc(nrm_ps, 1)

            def inner(n, cur, p):
                if p is not None:
                    pe.wait_ge(res_ready, n)
                elif cur is not None:
                    pe.wait_ge(gelu_ready, n)
                for b in range(4):
                    for k in range(KC):
                        last = nc.tensor.matmul(ps[:, 7, T * b:T * b + T], downT[:, k, 128 * b:128 * b + 128],
                                                yT[:, k, :], start=(k == 0), stop=(k == KC - 1))
                last.then_inc(inner_ps, 1)

            def body(n, cur, p):
                transpose_queries(n, 0)
                queries(n, 2)
                scores(n, 0)
                if cur is not None:
                    pe.wait_ge(nvar_ready, n)
                if p is not None:
                    pe.wait_ge(G_ready, p + 2)
                query_norms(n, 0)
                transpose_queries(n, 1)
                if p is not None:
                    output(p)
                queries(n, 3)
                scores(n, 1)
                query_norms(n, 1)
                transpose_queries(n, 2)
                inner(n, cur, p)
                scores(n, 2)
                query_norms(n, 2)
                transpose_queries(n, 3)
                scores(n, 3)
                query_norms(n, 3)

            def expert_weights(p):
                pe.wait_ge(onehot3, p + 1)
                pe.wait_ge(G_ready, p + 1)
                for t in range(T):
                    for g in range(2):
                        last = nc.tensor.matmul(ps[64 * g:64 * g + 64, 5 + t // 64, 8 * (t % 64):8 * (t % 64) + 8],
                                                Lh[:, :, t], Hh[:, 0:2, g:HI:2, t], start=True, stop=True)
                    if t == 63 or t == T - 1:
                        last.then_inc(W_ps, 1)

            def output(p):
                pe.wait_ge(G_ready, p + 2)
                for j in range(4):
                    last = nc.tensor.matmul(ps[0:T, 7, :], GT[:, j, :], up[:, j, :], start=(j == 0), stop=(j == 3))
                last.then_inc(out_ps, 1)

            def prologue():
                head(0)
                queries(0, 1)
                body(0, None, None)
                head(1)
                queries(1, 1)

            def iteration(i, p, n, n2):
                if p is not None:
                    pe.wait_ge(nvar_ready, i + 1)
                    expert_weights(p)
                if n is not None:
                    body(n, i, p)
                elif p is not None:
                    output(p)
                if n2 is not None:
                    head(n2)
                pe.wait_ge(w_ready, i + 1)
                if n is not None:
                    pe.wait_ge(gelu_ready, n + 1)
                else:
                    pe.wait_ge(res_ready, i + 1)
                nc.tensor.transpose(ps[:, 7, 0:T], fs.rearrange("p h r -> p (h r)"), ident[0:T, 0:T])
                nc.tensor.transpose(ps[:, 7, 128:128 + T], fi, ident[0:T, 0:T]).then_inc(wT_ps, 1)
                if n2 is not None:
                    queries(n2, 1)

            iterations(pe, prologue, iteration)
            expert_weights(NT - 1)
            output(NT - 1)


_INS = ["x", "src", "dst", "L0_gnn_W_l", "L0_gnn_b_l", "L0_gnn_W_r", "L0_gnn_gamma", "L0_gnn_beta",
        "L0_mix_qkv_weight", "L0_mix_proj_weight", "L0_mix_proj_bias", "L0_ffn_Wq", "L0_ffn_bq", "L0_ffn_ln_g",
        "L0_ffn_ln_b", "L0_ffn_keys0", "L0_ffn_keys1", "L0_ffn_expert_down", "L0_ffn_expert_up"]


def kernel(**inputs):
    import numpy as _np
    import concourse.bacc as _bacc
    from concourse import mybir as _mybir
    from concourse.bass_utils import run_bass_kernel_spmd as _run

    nc = _bacc.Bacc("TRN2", target_bir_lowering=False, num_devices=1)
    arrays, args = {}, []
    for name in _INS:
        a = _np.ascontiguousarray(inputs[name])
        arrays[f"in_{name}"] = a
        args.append(nc.dram_tensor(f"in_{name}", a.shape, _mybir.dt.from_np(a.dtype), kind="ExternalInput").ap())
    args.append(nc.dram_tensor("out", inputs["x"].shape, _mybir.dt.float32, kind="ExternalOutput").ap())
    build(nc, *args)
    r = _run(nc, [arrays], core_ids=[0])
    return r.results[0]["out"]
```

```python
from contextlib import ExitStack

import concourse.bass as bass
from concourse import mybir


def build(nc, x, src, dst, W_l, b_l, W_r, gamma, beta, qkv_w, proj_w, proj_b,
          Wq, bq, ln_g, ln_b, keys0, keys1, e_down, e_up, out):
    dt = mybir.dt
    F32, F16, BF16, I32, U32, I16 = dt.float32, dt.float16, dt.bfloat16, dt.int32, dt.uint32, dt.int16
    ALU = mybir.AluOpType
    ACT = mybir.ActivationFunctionType
    AX = mybir.AxisListType
    ds = bass.ds

    N, D = x.shape
    T = 125
    NT = N // T
    KC = D // 128
    E = src.shape[0]
    NC = E // T
    CH = NC // 2
    AB = 418
    AW = 3 * AB
    EPS = 1e-5
    EPS_DEN = 1e-15
    H, QD = 8, 256
    TK = 16
    NK = keys0.shape[0]
    ROWS = [TK // (i + 1) for i in range(TK)]
    OFF = [sum(ROWS[:i]) for i in range(TK)]
    C = sum(ROWS)
    PAIRS = ((0, 1), (1, 2), (2, 3), (3, 4), (4, 5), (5, 8), (8, 16))
    GC = 4
    GROUPS_MAX = -(-NC // GC)
    RING = 2
    LO, HI = 64, 8
    TP = 126
    CODE = 512
    WSCALE = 1024.0
    LOWEST = -3.0e38
    LEAST_NORM = 1e-12

    ctx = ExitStack()
    with ctx:
        def sb(name, shape, dtype=F32):
            return ctx.enter_context(nc.sbuf_tensor(name, shape, dtype))

        def sem(name):
            return ctx.enter_context(nc.semaphore(name))

        ps = ctx.enter_context(nc.psum_tensor("ps", [128, 8, 512], F32))

        wbig = sb("wbig", [128, KC, 2560])
        qkvT, WlT, WrT = wbig[:, :, 0:1536], wbig[:, :, 1536:2048], wbig[:, :, 2048:2560]
        WqT, downT = wbig[:, :, 0:2048], wbig[:, :, 2048:2560]
        projT = sb("projT", [128, KC, D])
        up = sb("up", [128, KC, D])
        xs = sb("xs", [T, NT, D])
        arena = sb("arena", [128, 25480])
        side = sb("side", [128, 3760])
        P = arena[0:T, 0:5120].rearrange("p (t d) -> p t d", d=D)
        R = arena[0:T, 5120:10240].rearrange("p (t d) -> p t d", d=D)
        qT = arena[:, 10240:15240].rearrange("p (g n) -> p g n", n=N)
        stage = arena[:, 15240:19336].rearrange("p (s o d) -> p s o d", s=2, o=4)
        xn = arena[0:T, 19336:19848]
        xh = arena[0:T, 19848:20360]
        kS = arena[0:T, 20360:20872]
        vS = arena[0:T, 20872:21384]
        bl_bc = arena[0:T, 21384:21896]
        pb_bc = arena[0:T, 21896:22408]
        Mb = arena[:, 22408:22920].rearrange("p (g c) -> p g c", g=4)
        Kb = arena[:, 22920:23432].rearrange("p (g c) -> p g c", g=4)
        bq3 = arena[0:65, 24036:25060].bitcast(BF16)
        fs = arena[0:T, 25060:25188].rearrange("p (h r) -> p h r", h=H)
        posi = arena[0:T, 25188:25316].bitcast(U32).rearrange("p (h r) -> p h r", h=H)
        fi = arena[0:T, 25316:25444]
        bmask = arena[:, 23432:23560]
        wmem = side[:, 2548:3760]
        ends_row = wmem[0:NT, 0:2 * NC].rearrange("p (s c) -> p s c", s=2)
        chunk_up, chunk_down = wmem[0:NT, 2 * NC:3 * NC], wmem[0:NT, 3 * NC:4 * NC]
        ov, ov2 = wmem[0:NT, 4 * NC:5 * NC], wmem[0:NT, 5 * NC:6 * NC]
        ends_b = wmem[0:CH, 1024:1064].rearrange("p (s m) -> p s m", m=NT)
        tile_lo, tile_hi = wmem[0:NT, 1064:1065], wmem[0:NT, 1065:1066]
        window = wmem[0:NT, 1066:1068]
        groups_i = wmem[0:NT, 1068:1069].bitcast(I32)
        wlim = wmem[0:1, 1072:1102].rearrange("p (s m) -> p s m", s=3)
        edge_i = arena[0:CH, 4096:4596].bitcast(I32).rearrange("p (s h t) -> p s h t", s=2, h=2)
        edge_f = arena[0:CH, 4608:5108].rearrange("p (s h t) -> p s h t", s=2, h=2)
        keys_raw = arena[:, 5120:5632].rearrange("p (o d) -> p o d", o=4)
        keysN = arena[:, 22920:23432].rearrange("p (o d) -> p o d", o=4)
        bq_parts = arena[0:H, 25060:25444].bitcast(BF16).rearrange("p (s e) -> p s e", s=3)
        ring_end = 15240 + RING * GC * AW // 2
        S1 = arena[0:T, 15240:ring_end].bitcast(F16).rearrange("p (s u n) -> p s u n", s=RING, u=GC)
        D1 = arena[0:T, ring_end:ring_end + RING * GC * 64].bitcast(F16).rearrange("p (s u n) -> p s u n", s=RING, u=GC)
        meanS = arena[0:T, 21280:21792]
        projS = arena[0:T, 21792:22304]
        qh = arena[0:T, 0:2048]
        sc = arena[0:T, 2048:6144].rearrange("p (h f e) -> p h f e", h=H, f=2)
        sc2 = arena[0:T, 6144:6656].rearrange("p (f e) -> p f e", f=2)
        found = arena[0:T, 6656:9856].bitcast(I16).rearrange("p (h c r) -> p h c r", h=H, r=TK)
        cirep = arena[0:T, 9856:13056].bitcast(I16).rearrange("p (h c r) -> p h c r", h=H, r=TK)
        Lh = arena[:, 13056:17088].bitcast(F16).rearrange("p (q t) -> p q t", t=TP)
        iotaL = arena[:, 17088:21120].bitcast(F16).rearrange("p (q t) -> p q t", t=TP)
        Hh = arena[:, 21120:22632].bitcast(F16).rearrange("p (s q t) -> p s q t", s=3, t=TP)
        iotaH = iotaL[:, 0:HI, :]
        gelu2 = arena[:, 22632:24440].rearrange("p (s w) -> p s w", s=2)[:, :, 0:4 * T]

        ident = sb("ident", [128, 128])
        ones = sb("ones", [128, 1])
        zero16 = sb("zero16", [1, 512], F16)
        iotaN = sb("iotaN", [128, AW], F16)
        ecol = sb("ecol", [T, 2 * NC + GROUPS_MAX * GC])
        ends = sb("ends", [CH, 4])
        bounds = sb("bounds", [1, 3, NT], I32)
        As = side[0:T, AW:2 * AW]
        AT = side[0:T, 2 * AW:2 * AW + NT * T].rearrange("p (s t) -> p s t", s=NT)
        y = side[0:T, 0:512]
        vT = side[:, 512:1012].rearrange("p (f h t) -> p f h t", f=2, h=2)
        v2 = side[:, 1012:1512].rearrange("p (f h t) -> p f h t", f=2, h=2)
        top = side[0:T, 1512:1768].rearrange("p (f h r) -> p f h r", f=2, h=H)
        topi = side[0:T, 1768:2024].bitcast(U32).rearrange("p (f h r) -> p f h r", f=2, h=H)
        topif = side[0:T, 2024:2280].rearrange("p (f h r) -> p f h r", f=2, h=H)
        cs = side[0:T, 2280:2680].rearrange("p (h c) -> p h c", h=H)
        ci = side[0:T, 2680:3080].rearrange("p (h c) -> p h c", h=H)
        lo_i = side[:, 3180:3430].bitcast(I32).rearrange("p (s t) -> p s t", s=2)
        lo16, hi16, wh16, wl16 = (side[:, 3430 + 63 * n:3493 + 63 * n].bitcast(F16) for n in range(4))
        place = side[0:T, 3682:3746].bitcast(I16).rearrange("p (h r) -> p h r", h=H)
        cs2 = side[0:T, 3080:3180].rearrange("p (s c) -> p s c", s=2)
        xnT = sb("xnT", [128, 2, KC, T])
        hT1 = sb("hT", [128, KC, T])
        hT = [hT1, side[:, 2048:2548].rearrange("p (k t) -> p k t", k=KC)]
        ksum = sb("ksum", [128, 4])
        den = xnT[:, 0, :, :]
        pin = xnT[:, 1, :, :]
        gnn = sb("gnn", [T, D])
        bqf = arena[0:H, 22408:22664]
        bmean = sb("bmean", [H, 1])
        wmean = sb("wmean", [128, KC, H])
        x1mean = sb("x1mean", [T, NT])
        x1rstd = sb("x1rstd", [T, NT])
        cols = sb("cols", [128, 12])
        gcol, bcol, lgc, lbc = cols[:, 0:4], cols[:, 4:8], cols[:, 8:10], cols[:, 10:12]
        bn = sb("bn", [T, H, 6])
        mv = sb("mv", [T, H, 2])
        rs = sb("rs", [T, H])
        cnt = sb("cnt", [T, 2])
        knT = sb("knT", [128, 2, NK])
        kss = sb("kss", [128, 4])
        onesb = sb("onesb", [65, T], BF16)
        yT = xnT[:, 0, :, :]
        W0 = xnT[:, 1, :, :].rearrange("p k t -> p (k t)").rearrange("p (t j) -> p t j", j=4)
        GT = hT1[:, :, :]
        nrm = sb("nrm", [T, 2 * H])
        ssq = sb("ssq", [T, H])
        minus_half = sb("minus_half", [128, 16])
        esum = sb("esum", [T, H])
        place_code = sb("place_code", [T, 2, TK])
        res = gnn

        norms = ps[0:T, 6, 488:504]

        scores_seen, sums_open, kv_closed, gelu_open, bq_split, Wq_centered, ssq_ready = map(
            sem, "scores_seen sums_open kv_closed gelu_open bq_split Wq_centered ssq_ready".split())
        kss_ready, krs_ready, var1_ready, rstd1_ready, yvar_ready, yrstd_ready, qvar_ready, nvar_ready, \
            nrstd_ready = map(sem, ("kss_ready krs_ready var1_ready rstd1_ready yvar_ready yrstd_ready qvar_ready "
                                    "nvar_ready nrstd_ready").split())
        x_loaded, edges_loaded, small_loaded, keys_loaded, up_loaded, bq_loaded = map(
            sem, "x_loaded edges_loaded small_loaded keys_loaded up_loaded bq_loaded".split())
        stage_loaded = [sem(f"stage_loaded{b}") for b in range(5)]
        pool_step, consts_ready, pad_ready, iotas_ready = map(sem, "pool_step consts_ready pad_ready iotas_ready".split())
        prep_tr, prep_act, prep_dve = map(sem, "prep_tr prep_act prep_dve".split())
        edge_cast, edge_tr, ecol_ready, ends_tr, bounds_ready, window_ready, window_tr, ends_out, x0_loaded = map(
            sem, "edge_cast edge_tr ecol_ready ends_tr bounds_ready window_ready window_tr ends_out "
                 "x0_loaded".split())
        keys_normed, keys_tr, knT_ready, bq_ready = map(sem, "keys_normed keys_tr knT_ready bq_ready".split())
        dve_step = sem("dve_step")
        xn_ready, xh_ready, xs_ready, xnT_ps, hT_ps, xnT_ready, hT_ready = map(
            sem, "xn_ready xh_ready xs_ready xnT_ps hT_ps xnT_ready hT_ready".split())
        mm_ready, p_out, r_out, k_out, v_out, q_out, kv_done = map(
            sem, "mm_ready p_out r_out k_out v_out q_out kv_done".split())
        attn_ready = sem("attn_ready")
        onehots_free, onehots_ready, A_ready, A_out, AT_ps, AT_act, agg_ready, den_ps, den_out, pin_ready, \
            proj_ready, x1_ready, mean_out, proj_out, degree_ready, pads_ready, mixed_ps, \
            mixed_ready = map(sem, (
                "onehots_free onehots_ready A_ready A_out AT_ps AT_act agg_ready den_ps den_out pin_ready "
                "proj_ready x1_ready mean_out proj_out degree_ready pads_ready mixed_ps "
                "mixed_ready").split())
        y_ready, yT_ps, yT_ready, inner_ps, gelu_ready, q_ps, qstat_ready, qh_ready, tr_ps, vT_ready, v2_ready, \
            nrm_ps, s_ps, sc_ready, topk_done = map(sem, (
                "y_ready yT_ps yT_ready inner_ps gelu_ready q_ps qstat_ready qh_ready tr_ps vT_ready v2_ready nrm_ps "
                "s_ps sc_ready topk_done").split())
        topif_ready, ci_ready, cirep_ready, exp_in, exp_out, w_ready, wT_ps, wh_ready, onehot3, W_ps, W0_ready, \
            G_ready, out_ps, res_ready, stored = map(sem, (
                "topif_ready ci_ready cirep_ready exp_in exp_out w_ready wT_ps wh_ready onehot3 W_ps W0_ready G_ready "
                "out_ps res_ready stored").split())

        def rows(w, g):
            return w[512 * g:512 * (g + 1), :].rearrange("(o p) d -> p o d", p=128)

        GROUPS = [(rows(qkv_w, g), qkvT[:, :, 512 * g:512 * (g + 1)]) for g in range(3)]
        GROUPS += [(rows(W_l, 0), WlT), (rows(W_r, 0), WrT), (rows(proj_w, 0), projT)]
        EARLY = len(GROUPS)
        GROUPS += [(rows(Wq, g), WqT[:, :, 512 * g:512 * (g + 1)]) for g in range(4)]
        GROUPS += [(rows(e_down, 0), downT)]
        PREP_BANK = [0, 1, 3, 4]
        BUFFERS = [stage[:, 0, :, :], stage[:, 1, :, :], arena[:, 10240:12288].rearrange("p (o d) -> p o d", o=4),
                   arena[:, 12288:14336].rearrange("p (o d) -> p o d", o=4),
                   side[:, 0:2048].rearrange("p (o d) -> p o d", o=4)]
        BUFFER_OF = [0, 1, 2, 3, 0, 1, 0, 1, 4, 0, 1]

        def loads(g):
            return BUFFER_OF[:g + 1].count(BUFFER_OF[g])


        FROM_ONE = [
            qh_ready, hT_ps, G_ready, xnT_ps, AT_act, v2_ready, hT_ready,
            k_out, stored, q_out, res_ready, xs_ready, AT_ps, mean_out, proj_out,
            xnT_ready, kv_done, agg_ready, x1_ready, nrm_ps, A_out, degree_ready, pin_ready,
            proj_ready, s_ps, v_out, sc_ready, vT_ready,
        ]

        def iterations(eng, prologue, iteration):
            prologue()
            iteration(0, None, 1, 2)
            with eng.Fori(1, NT - 2) as i:
                iteration(i, i - 1, i + 1, i + 2)
            iteration(NT - 2, NT - 3, NT - 1, None)
            iteration(NT - 1, NT - 2, None, None)

        def tiles(eng, iteration, last):
            iteration(0, None, None)
            iteration(1, 0, None)
            with eng.Fori(2, NT) as m:
                iteration(m, m - 1, m - 2)
            last()

        block = ctx.enter_context(nc.Block())

        @block.sync
        def _(sp):
            for counter in FROM_ONE:
                sp.sem_inc(counter, 1)
            sp.dma_start(edge_i[:, 0, :, :], src.rearrange("(h c t) -> c h t", h=2, t=T)).then_inc(edges_loaded, 16)
            sp.dma_start(edge_i[:, 1, :, :], dst.rearrange("(h c t) -> c h t", h=2, t=T)).then_inc(edges_loaded, 16)
            def load(g):
                if loads(g) > 1:
                    before = max(e for e in range(g) if BUFFER_OF[e] == BUFFER_OF[g])
                    sp.wait_ge(prep_tr, 4 * (before + 1))
                b = BUFFER_OF[g]
                sp.dma_start(BUFFERS[b], GROUPS[g][0]).then_inc(stage_loaded[b], 16)

            load(0)
            load(1)
            sp.dma_start(xs[:, 0, :], x[0:T, :]).then_inc(x0_loaded, 16)
            for g in range(2, EARLY):
                load(g)
            sp.dma_start(xs[:, 1:NT, :], x[T:N, :].rearrange("(t p) d -> p t d", p=T)).then_inc(x_loaded, 16)
            for g in range(EARLY, EARLY + 3):
                load(g)
            sp.wait_ge(bq_split, 1)
            for r in range(3):
                sp.dma_start(bq3[32 * r:32 * r + 1, :], bq_parts[:, r, :]).then_inc(bq_ready, 16)
            for g in range(EARLY + 3, len(GROUPS)):
                load(g)
            sp.dma_start(up[:, :, :], e_up[0:512, :].rearrange("(j p) d -> p j d", p=128)).then_inc(up_loaded, 16)
            with sp.Fori(0, NT) as i:
                sp.wait_ge(res_ready, i + 2)
                sp.dma_start(out[ds(i * T, T), :], res[:, :]).then_inc(stored, 16)
            sp.wait_ge(stored, 16 * NT + 1)

        @block.gpsimd
        def _(pool):
            steps = [0]

            def step(ins):
                steps[0] += 1
                ins.then_inc(pool_step, 1)
                pool.wait_ge(pool_step, steps[0])

            def iota(ap, pattern, base=0, per_partition=0):
                step(nc.gpsimd.iota(ap, pattern=pattern, base=base, channel_multiplier=per_partition,
                                    allow_small_or_imprecise_dtypes=True))

            step(nc.gpsimd.memset(ident[:, :], 0.0))
            step(nc.gpsimd.affine_select(out=ident[:, :], in_=ident[:, :], compare_op=ALU.not_equal, fill=1.0, base=0,
                                         pattern=[[-1, 128]], channel_multiplier=1))
            step(nc.gpsimd.memset(bmask, 0.0))
            for b in range(4):
                step(nc.gpsimd.memset(bmask[32 * b:32 * b + 32, 32 * b:32 * b + 32], 1.0))
            for ap, value in ((ones[:, :], 1.0), (minus_half[:, :], -0.5), (zero16[:, :], 0.0), (onesb[:, :], 1.0)):
                step(nc.gpsimd.memset(ap, value))
            iota(iotaN[:, :], [[1, AW]])
            iota(tile_lo, [[0, 1]], 0, T)
            iota(tile_hi, [[0, 1]], T - 1, T)
            iota(chunk_up, [[1, NC]], 1)
            iota(chunk_down, [[-1, NC]], NC)
            pool.sem_inc(consts_ready, 1)

            def rsqrt(ap, ready):
                nc.gpsimd.tensor_tensor(ap, ap, minus_half[0:ap.shape[0], 0:ap.shape[1]], ALU.pow).then_inc(ready, 1)

            pool.wait_ge(small_loaded, 16 * 6)

            def iteration1(i):
                for u in range(2):
                    pool.wait_ge(var1_ready, i * 2 + (u + 1))
                    rsqrt(rs[:, u:u + 1], rstd1_ready)
                pool.wait_ge(xn_ready, i + 1)
                pool.sem_inc(sums_open, 1)
                nc.gpsimd.tensor_tensor(xs[:, ds(i, 1), :], xs[:, ds(i, 1), :], xn.unsqueeze(1), ALU.add)\
                    .then_inc(pad_ready, 1)
                pool.wait_ge(pad_ready, i + 1)
                pool.sem_inc(sums_open, 1)
                nc.gpsimd.tensor_tensor(xs[:, ds(i, 1), :], xs[:, ds(i, 1), :], pb_bc.unsqueeze(1), ALU.add)\
                    .then_inc(xs_ready, 1)

            iteration1(0)
            pool.wait_ge(kss_ready, 1)
            rsqrt(kss[:, :], krs_ready)
            with pool.Fori(1, NT) as i:
                iteration1(i)
            for a, b in ((0, NT - 1), (NT - 1, NT)):
                pool.wait_ge(yvar_ready, b)
                nc.gpsimd.tensor_tensor(x1rstd[:, a:b], x1rstd[:, a:b], minus_half[0:T, a:b], ALU.pow)\
                    .then_inc(yrstd_ready, 1)

            def stats(n, j):
                a = slice(2 * j, 2 * j + 2)
                pool.wait_ge(ssq_ready, n * 8 + (2 * j + 2))
                pool.sem_inc(sums_open, 1)
                nc.gpsimd.tensor_scalar(rs[:, a], ssq[:, a], EPS, None, ALU.add).then_inc(qvar_ready, 1)
                pool.wait_ge(qvar_ready, n * 4 + (j + 1))
                rsqrt(rs[:, a], qstat_ready)

            def squares(n, j):
                pool.wait_ge(vT_ready, n * 4 + (j + 2))
                pool.wait_ge(nrm_ps, n * 4 + (j + 1))
                nc.gpsimd.tensor_tensor(v2, vT, vT, ALU.mult).then_inc(v2_ready, 1)

            def inverse_norms(n):
                pool.wait_ge(nvar_ready, n + 1)
                rsqrt(nrm[:, :], nrstd_ready)

            def index_sums(i):
                pool.wait_ge(topif_ready, i + 1)
                a, b = topif[:, 0, :, :], topif[:, 1, :, :]
                for i0, i1 in PAIRS:
                    n, m = ROWS[i0], i1 - i0
                    o = ci[:, :, OFF[i0]:OFF[i0] + m * n].rearrange("p h (i j) -> p h i j", j=n)
                    last = nc.gpsimd.tensor_tensor(
                        o, a[:, :, i0:i1].unsqueeze(3).to_broadcast([T, H, m, n]),
                        b[:, :, 0:n].unsqueeze(2).to_broadcast([T, H, m, n]), ALU.add)
                last.then_inc(ci_ready, 1)

            def prologue():
                stats(0, 0)
                stats(0, 1)
                squares(0, 0)
                stats(0, 2)
                squares(0, 1)
                stats(0, 3)
                squares(0, 2)
                squares(0, 3)

            def iteration(i, p, n, n2):
                if n is not None:
                    stats(n, 0)
                    stats(n, 1)
                if p is None:
                    inverse_norms(i)
                    index_sums(i)
                if n is not None:
                    squares(n, 0)
                if n is not None:
                    stats(n, 2)
                    squares(n, 1)
                if p is not None:
                    index_sums(i)
                if n is not None:
                    stats(n, 3)
                    squares(n, 2)
                    squares(n, 3)
                    inverse_norms(n)

            iterations(pool, prologue, iteration)

        @block.scalar
        def _(act):
            for dst_ap, src_ap in ((cols[:, 0:4], gamma.rearrange("(c p) -> p c", p=128)),
                                   (cols[:, 4:8], beta.rearrange("(c p) -> p c", p=128)),
                                   (cols[:, 8:10], ln_g.rearrange("(c p) -> p c", p=128)),
                                   (cols[:, 10:12], ln_b.rearrange("(c p) -> p c", p=128))):
                with nc.allow_non_contiguous_dma(reason="short per-feature vectors"):
                    act.dma_start(dst_ap, src_ap).then_inc(small_loaded, 16)
            act.dma_start(bl_bc, b_l.partition_broadcast(T)).then_inc(small_loaded, 16)
            act.dma_start(pb_bc, proj_b.partition_broadcast(T)).then_inc(small_loaded, 16)
            act.dma_start(keys_raw[:, 0:2, :], keys0.rearrange("(o p) d -> p o d", p=128)).then_inc(keys_loaded, 16)
            act.dma_start(keys_raw[:, 2:4, :], keys1.rearrange("(o p) d -> p o d", p=128)).then_inc(keys_loaded, 16)
            act.dma_start(bqf, bq.rearrange("(h e) -> h e", h=H)).then_inc(bq_loaded, 16)

            def prep(g):
                for o in (1, 3):
                    act.wait_ge(prep_tr, 4 * g + o + 1)
                    nc.scalar.activation(GROUPS[g][1][:, :, 128 * o:128 * o + 128],
                                         ps[:, PREP_BANK[o], :].rearrange("p (k q) -> p k q", k=KC), ACT.Copy)\
                        .then_inc(prep_act, 1)

            for g in range(EARLY):
                prep(g)
            act.wait_ge(small_loaded, 16 * 6)
            def transposed(i, u):
                act.wait_ge(hT_ps, i + 2)
                for k in range(KC):
                    nc.scalar.activation(hT[u][:, k, :], ps[:, 1, T * k:T * k + T], ACT.Identity,
                                         scale=gcol[:, k:k + 1], bias=bcol[:, k:k + 1])\
                        .then_inc(hT_ready, 1)

            def iteration1(i, u, more=True):
                act.wait_ge(mm_ready, i * 5 + 1)
                nc.scalar.activation(P[:, ds(i, 1), :], ps[0:T, 2:3, :], ACT.Copy).then_inc(p_out, 1)
                act.wait_ge(mm_ready, i * 5 + 3)
                act.wait_ge(kv_done, i + 1)
                nc.scalar.activation(kS, ps[0:T, 4, :], ACT.Relu).then_inc(k_out, 1)
                if more:
                    transposed(i + 1, 1 - u)
                act.wait_ge(mm_ready, i * 5 + 5)
                nc.scalar.activation(qT[:, :, ds(i * T, T)],
                                     ps[:, 3, 0:4 * T].rearrange("p (g t) -> p g t", g=4), ACT.Relu)\
                    .then_inc(q_out, 1)

            transposed(0, 0)
            with act.Fori(0, NT // 2 - 1) as i2:
                for u in range(2):
                    iteration1(i2 * 2 + u, u)
            iteration1(NT - 2, 0)
            iteration1(NT - 1, 1, False)
            for g in range(EARLY, len(GROUPS)):
                prep(g)
            act.wait_ge(mixed_ps, 1)
            nc.scalar.activation(projT[:, :, :], ps[:, 4:8, :], ACT.Copy).then_inc(mixed_ready, 1)

            def mean_and_projection(p):
                act.wait_ge(agg_ready, p + 2)
                act.wait_ge(degree_ready, p + 2)
                act.wait_ge(x1_ready, p + 1)
                nc.scalar.activation(meanS, ps[0:T, 7, :], ACT.Identity, scale=cnt[:, 1:2]).then_inc(mean_out, 1)
                act.wait_ge(proj_ready, p + 2)
                nc.scalar.activation(projS, ps[0:T, 5, :], ACT.Copy).then_inc(proj_out, 1)

            def counts_out(m, b):
                act.wait_ge(AT_ps, m * 3 + (b + 2))
                n = min(4, NT - 4 * b)
                nc.scalar.activation(AT[:, 4 * b:4 * b + n, :],
                                     ps[0:T, 3 + b % 2, 0:n * T].rearrange("p (s t) -> p s t", s=n), ACT.Copy)\
                    .then_inc(AT_act, 1)

            def iteration2(m, p, q):
                act.wait_ge(A_ready, m + 1)
                act.wait_ge(AT_ps, m * 3 + 1)
                act.wait_ge(degree_ready, m + 1)
                nc.scalar.activation(As[:, :].rearrange("p (b a) -> p b a", b=3), ps[0:T, 0:3, 0:AB], ACT.Copy,
                                     accum_out=cnt[:, 0:1]).then_inc(A_out, 1)
                if p is not None:
                    mean_and_projection(p)
                counts_out(m, 0)
                counts_out(m, 1)
                act.wait_ge(den_ps, m + 1)
                act.wait_ge(pin_ready, m + 1)
                nc.scalar.activation(den, ps[:, 6, 0:4 * T].rearrange("p (g t) -> p g t", g=4), ACT.Copy,
                                     bias=EPS_DEN).then_inc(den_out, 1)
                counts_out(m, 2)

            tiles(act, iteration2, lambda: mean_and_projection(NT - 1))
            def queries_in(n):
                act.wait_ge(yT_ps, n + 1)
                nc.scalar.activation(yT, ps[:, 2, 0:4 * T].rearrange("p (k t) -> p k t", k=KC), ACT.Copy)\
                    .then_inc(yT_ready, 1)

            def square(n, j):
                act.wait_ge(q_ps, n * 4 + (j + 1))
                for h in (2 * j, 2 * j + 1):
                    nc.scalar.activation(qh[:, QD * h:QD * h + QD], ps[0:T, j % 2, QD * (h % 2):QD * (h % 2) + QD],
                                         ACT.Square, scale=QD ** -0.5, accum_out=ssq[:, h:h + 1])\
                        .then_inc(ssq_ready, 1)

            def normalize(n, j):
                act.wait_ge(qstat_ready, n * 4 + (j + 1))
                for h in (2 * j, 2 * j + 1):
                    nc.scalar.activation(qh[:, QD * h:QD * h + QD], ps[0:T, j % 2, QD * (h % 2):QD * (h % 2) + QD],
                                         ACT.Identity, scale=rs[:, h:h + 1]).then_inc(qh_ready, 1)

            def affine(n, j):
                act.wait_ge(tr_ps, n * 4 + (j + 1))
                act.wait_ge(s_ps, n * 8 + (2 * j + 1))
                act.wait_ge(v2_ready, n * 4 + (j + 1))
                for f in range(2):
                    last = nc.scalar.activation(
                        vT[:, f, :, :], ps[:, 2, 2 * T * f:2 * T * f + 2 * T].rearrange("p (h t) -> p h t", h=2),
                        ACT.Identity, scale=lgc[:, f:f + 1], bias=lbc[:, f:f + 1])
                last.then_inc(vT_ready, 1)

            def scores_out(n, j, cur):
                for h in (2 * j, 2 * j + 1):
                    if cur is not None:
                        act.wait_ge(topk_done, cur * 8 + (h + 1))
                    act.wait_ge(s_ps, n * 8 + (h + 2))
                    nc.scalar.activation(sc[:, h, :, :],
                                         ps[0:T, 3 + h % 2, :].rearrange("p (f e) -> p f e", f=2), ACT.Copy)\
                        .then_inc(sc_ready, 1)

            def activate(n, p):
                if p is not None:
                    act.wait_ge(G_ready, n)
                act.wait_ge(inner_ps, n + 1)
                act.sem_inc(gelu_open, 1)
                nc.scalar.activation(gelu2[:, ds(n % 2, 1), :], ps[:, 7:8, 0:4 * T], ACT.Gelu)\
                    .then_inc(gelu_ready, 1)

            def spread_codes(i, q):
                if q == 0:
                    act.wait_ge(ci_ready, i + 1)
                a = slice(2 * q, 2 * q + 2)
                nc.scalar.activation(cirep[:, a, :, :], ci[:, a, :].unsqueeze(3).to_broadcast([T, 2, C, TK]), ACT.Copy)\
                    .then_inc(cirep_ready, 1)

            def expert_weights_out(p):
                for b in range(2):
                    act.wait_ge(W_ps, p * 2 + (b + 1))
                    c = min(64, T - 64 * b)
                    nc.scalar.activation(W0[:, 64 * b:64 * b + c, :],
                                         ps[:, 5 + b, 0:8 * c].rearrange("p (t j) -> p t j", j=8)[:, :, 0:4],
                                         ACT.Copy, scale=1.0 / WSCALE).then_inc(W0_ready, 1)

            def finish(p):
                act.wait_ge(out_ps, p + 1)
                act.wait_ge(stored, p * 16 + 1)
                nc.scalar.activation(res[:, :], ps[0:T, 7, :], ACT.Copy).then_inc(res_ready, 1)

            def exponentials(i):
                act.wait_ge(exp_in, i + 1)
                nc.scalar.activation(fs[:, :, :], fs[:, :, :], ACT.Exp).then_inc(exp_out, 1)

            def scores(n, cur, p):
                affine(n, 0)
                scores_out(n, 0, cur)
                square(n, 2)
                if p is None and cur is not None:
                    spread_codes(cur, 0)
                    spread_codes(cur, 1)
                affine(n, 1)
                normalize(n, 2)
                if p is not None:
                    finish(p)
                scores_out(n, 1, cur)
                square(n, 3)
                if p is None and cur is not None:
                    spread_codes(cur, 2)
                    spread_codes(cur, 3)
                affine(n, 2)
                if p is not None:
                    spread_codes(cur, 0)
                    spread_codes(cur, 1)
                normalize(n, 3)
                if p is None and cur is not None:
                    exponentials(cur)
                if p is not None:
                    spread_codes(cur, 2)
                    spread_codes(cur, 3)
                scores_out(n, 2, cur)
                affine(n, 3)
                activate(n, p)
                if p is not None:
                    exponentials(cur)
                scores_out(n, 3, cur)

            def prologue():
                queries_in(0)
                square(0, 0)
                square(0, 1)
                normalize(0, 0)
                normalize(0, 1)
                scores(0, None, None)
                queries_in(1)
                square(1, 0)
                square(1, 1)

            def iteration(i, p, n, n2):
                if n is not None:
                    normalize(n, 0)
                    normalize(n, 1)
                if p is not None:
                    expert_weights_out(p)
                if n is not None:
                    scores(n, i, p)
                else:
                    finish(p)
                    for q in range(4):
                        spread_codes(i, q)
                if n2 is not None:
                    queries_in(n2)
                if p is None:
                    act.wait_ge(iotas_ready, 1)
                if n is None:
                    exponentials(i)
                act.wait_ge(wT_ps, i + 1)
                nc.scalar.activation(wh16[:, 0:T], ps[:, 7, 0:T], ACT.Copy, scale=WSCALE).then_inc(wh_ready, 1)
                if n2 is not None:
                    square(n2, 0)
                    square(n2, 1)

            iterations(act, prologue, iteration)
            expert_weights_out(NT - 1)
            finish(NT - 1)

        @block.vector
        def _(dve):
            def prep(g):
                for o in (0, 2):
                    dve.wait_ge(prep_tr, 4 * g + o + 1)
                    nc.vector.tensor_copy(GROUPS[g][1][:, :, 128 * o:128 * o + 128],
                                          ps[:, PREP_BANK[o], :].rearrange("p (k q) -> p k q", k=KC))\
                        .then_inc(prep_dve, 1)

            steps = [0]

            def step(ins):
                steps[0] += 1
                ins.then_inc(dve_step, 1)
                dve.wait_ge(dve_step, steps[0])

            def clear_steps(n):
                dve.wait_ge(dve_step, n)
                dve.sem_clear(dve_step)

            dve.wait_ge(edges_loaded, 32)
            step(nc.vector.tensor_copy(edge_f[:, :, :, :], edge_i[:, :, :, :]))
            nc.vector.tensor_reduce(ends[:, 0:2], edge_f[:, 1, :, :], AX.X, ALU.min)
            step(nc.vector.tensor_reduce(ends[:, 2:4], edge_f[:, 1, :, :], AX.X, ALU.max))
            nc.vector.tensor_copy(ends_b, ends[:, :].unsqueeze(2).to_broadcast([CH, 4, NT])).then_inc(edge_cast, 1)
            prep(0)
            dve.wait_ge(edge_tr, 1)
            nc.vector.tensor_copy(ecol[:, 0:2 * NC], ps[0:T, 7, 0:2 * NC])\
                .then_inc(ecol_ready, 1)
            nc.vector.memset(ecol[:, 2 * NC:2 * NC + GC - 1], -1.0).then_inc(pads_ready, 1)
            dve.wait_ge(ends_tr, 1)
            nc.vector.tensor_copy(ends_row, ps[0:NT, 6, 0:2 * NC].rearrange("p (s c) -> p s c", s=2))\
                .then_inc(ends_out, 1)
            for g in range(1, EARLY):
                prep(g)
            clear_steps(steps[0])
            steps[0] = 0

            def both_norms(i):
                nc.vector.bn_stats(bn[:, 0, :], xs[:, ds(i, 1), :].rearrange("p a d -> p (a d)"))\
                    .then_inc(dve_step, 1)
                dve.wait_ge(dve_step, 1)
                nc.vector.bn_aggr(mv[:, 0, :], bn[:, 0, :]).then_inc(dve_step, 1)
                dve.wait_ge(dve_step, 2)
                nc.vector.tensor_scalar(rs[:, 0:1], mv[:, 0, 1:2], EPS, None, ALU.add)\
                    .then_inc(var1_ready, 1)
                dve.wait_ge(rstd1_ready, i * 2 + 1)
                dve.wait_ge(xnT_ps, i + 1)
                dve.wait_ge(xs_ready, i + 1)
                nc.vector.tensor_scalar(xn, xs[:, ds(i, 1), :].rearrange("p a d -> p (a d)"), mv[:, 0, 0:1],
                                        rs[:, 0:1], ALU.subtract, ALU.mult).then_inc(xn_ready, 1)
                dve.wait_ge(xn_ready, i + 1)
                nc.vector.bn_stats(bn[:, 1, :], xn).then_inc(dve_step, 1)
                dve.wait_ge(dve_step, 3)
                nc.vector.bn_aggr(mv[:, 1, :], bn[:, 1, :]).then_inc(dve_step, 1)
                dve.wait_ge(dve_step, 4)
                nc.vector.tensor_scalar(rs[:, 1:2], mv[:, 1, 1:2], EPS, None, ALU.add)\
                    .then_inc(var1_ready, 1)
                dve.wait_ge(rstd1_ready, i * 2 + 2)
                dve.wait_ge(hT_ps, i + 1)
                nc.vector.tensor_scalar(xh, xn, mv[:, 1, 0:1], rs[:, 1:2], ALU.subtract, ALU.mult)\
                    .then_inc(xh_ready, 1)
                clear_steps(4)

            def transposed(i, u):
                dve.wait_ge(xnT_ps, i + 2)
                nc.vector.tensor_copy(xnT[:, u, :, :], ps[:, 0, 0:4 * T].rearrange("p (k t) -> p k t", k=KC))\
                    .then_inc(xnT_ready, 1)

            def iteration1(i, u, more=True):
                if more:
                    both_norms(i + 1)
                dve.wait_ge(mm_ready, i * 5 + 2)
                nc.vector.tensor_tensor(R[:, ds(i, 1), :], ps[0:T, 3:4, :], bl_bc.unsqueeze(1), ALU.add)\
                    .then_inc(r_out, 1)
                dve.wait_ge(kv_done, i + 1)
                if more:
                    transposed(i + 1, 1 - u)
                dve.wait_ge(mm_ready, i * 5 + 4)
                nc.vector.tensor_copy(vS, ps[0:T, 2, :]).then_inc(v_out, 1)

            dve.wait_ge(x0_loaded, 16)
            both_norms(0)
            transposed(0, 0)

            dve.wait_ge(keys_loaded, 32)
            step(nc.vector.tensor_tensor(keysN[:, :, :], keys_raw[:, :, :], keys_raw[:, :, :], ALU.mult))
            step(nc.vector.tensor_reduce(kss[:, :], keysN[:, :, :], AX.X, ALU.add))
            nc.vector.tensor_scalar(kss[:, :], kss[:, :], LEAST_NORM ** 2, None, ALU.max).then_inc(kss_ready, 1)
            dve.wait_ge(bq_loaded, 16)
            step(nc.vector.memset(bq3[:, :], 0.0))
            step(nc.vector.tensor_reduce(bmean[:, :], bqf, AX.X, ALU.add))
            step(nc.vector.tensor_scalar(bmean[:, :], bmean[:, :], 1.0 / QD, None, ALU.mult))
            step(nc.vector.tensor_scalar(bqf, bqf, bmean[:, 0:1], None, ALU.subtract))
            for r in range(2):
                step(nc.vector.tensor_copy(bq_parts[:, r, :], bqf))
                step(nc.vector.tensor_tensor(bqf, bqf, bq_parts[:, r, :], ALU.subtract))
            nc.vector.tensor_copy(bq_parts[:, 2, :], bqf).then_inc(bq_split, 1)
            dve.wait_ge(krs_ready, 1)
            nc.vector.tensor_tensor(keysN[:, :, :], keys_raw[:, :, :], kss[:, :].unsqueeze(2).to_broadcast([128, 4, 128]),
                                    ALU.mult).then_inc(keys_normed, 1)
            dve.wait_ge(ends_out, 1)
            nc.vector.tensor_scalar(ov, ends_row[:, 1, :], tile_lo, None, ALU.is_ge)
            step(nc.vector.tensor_scalar(ov2, ends_row[:, 0, :], tile_hi, None, ALU.is_le))
            step(nc.vector.tensor_tensor(ov, ov, ov2, ALU.mult))
            step(nc.vector.tensor_tensor(ov2, ov, chunk_up, ALU.mult))
            step(nc.vector.tensor_reduce(window[:, 1:2], ov2, AX.X, ALU.max))
            step(nc.vector.tensor_tensor(ov2, ov, chunk_down, ALU.mult))
            step(nc.vector.tensor_reduce(window[:, 0:1], ov2, AX.X, ALU.max))
            step(nc.vector.tensor_scalar(window[:, 0:1], window[:, 0:1], -1.0, float(NC), ALU.mult, ALU.add))
            step(nc.vector.tensor_tensor(window[:, 1:2], window[:, 1:2], window[:, 0:1], ALU.max))
            step(nc.vector.tensor_tensor(window[:, 1:2], window[:, 1:2], window[:, 0:1], ALU.subtract))
            step(nc.vector.tensor_scalar(window[:, 1:2], window[:, 1:2], float(GC - 1), None, ALU.add))
            step(nc.vector.tensor_copy(groups_i, window[:, 1:2]))
            step(nc.vector.tensor_single_scalar(groups_i, groups_i, GC.bit_length() - 1, ALU.logical_shift_right))
            nc.vector.tensor_copy(window[:, 1:2], groups_i).then_inc(window_ready, 1)
            clear_steps(steps[0])
            steps[0] = 0

            dve.wait_ge(x_loaded, 16)
            with dve.Fori(0, NT // 2 - 1) as i2:
                for u in range(2):
                    iteration1(i2 * 2 + u, u)
            iteration1(NT - 2, 0)
            iteration1(NT - 1, 1, False)
            dve.wait_ge(keys_tr, 1)
            nc.vector.tensor_copy(knT[:, :, :], ps[:, 7, :].rearrange("p (f e) -> p f e", f=2)).then_inc(knT_ready, 1)
            dve.wait_ge(kv_closed, 1)
            nc.vector.tensor_tensor(Mb[:, :, :], ps[:, 5, :].rearrange("p (g c) -> p g c", g=4),
                                    bmask[:, :].unsqueeze(1).to_broadcast([128, 4, 128]), ALU.mult)
            nc.vector.tensor_copy(ksum[:, :], ps[:, 6, 0:4]).then_inc(attn_ready, 1)
            dve.wait_ge(attn_ready, 1)
            nc.vector.tensor_tensor(Kb[:, :, :], ksum[:, :].unsqueeze(2).to_broadcast([128, 4, 128]),
                                    bmask[:, :].unsqueeze(1).to_broadcast([128, 4, 128]), ALU.mult)\
                .then_inc(attn_ready, 1)
            prep(EARLY)
            dve.wait_ge(window_tr, 1)
            step(nc.vector.tensor_copy(wlim[:, 0:2, :], ps[0:1, 2, 0:2 * NT].rearrange("p (s m) -> p s m", s=2)))
            step(nc.vector.memset(wlim[:, 2, 0:1], 0.0))
            for m in range(1, NT):
                step(nc.vector.tensor_tensor(wlim[:, 2, m:m + 1], wlim[:, 2, m - 1:m], wlim[:, 1, m - 1:m], ALU.add))
                if m % 3 == 0:
                    prep(EARLY + m // 3)
            nc.vector.tensor_copy(bounds[:, :, :], wlim).then_inc(bounds_ready, 1)
            dve.wait_ge(bounds_ready, 1)
            prep(EARLY + 4)
            clear_steps(steps[0])
            steps[0] = 0

            dve.wait_ge(xs_ready, NT + 1)
            dve.wait_ge(p_out, NT)
            dve.wait_ge(pads_ready, 1)

            def onehots(m):
                first = dve.value_load(bounds[0:1, 0, ds(m, 1)], min_val=0, max_val=NC)
                groups = dve.value_load(bounds[0:1, 1, ds(m, 1)], min_val=0, max_val=GROUPS_MAX)
                before = dve.value_load(bounds[0:1, 2, ds(m, 1)], min_val=0, max_val=GROUPS_MAX * NT)
                with dve.Fori(0, groups) as n:
                    k = before + n
                    slot = k % RING
                    for u in range(GC):
                        if u % 2 == 0:
                            dve.wait_ge(onehots_free, k * 2 + (u // 2 + 1))
                        nc.vector.tensor_scalar(S1[:, ds(slot, 1), u, :].rearrange("p a n -> p (a n)"), iotaN[0:T, :],
                                                ecol[:, ds(first + n * GC + u, 1)], None, ALU.is_equal)
                        last = nc.vector.tensor_scalar(D1[:, ds(slot, 1), u, 0:T].rearrange("p a n -> p (a n)"),
                                                       iotaN[0:T, ds(m * T, T)], ecol[:, ds(first + n * GC + (u + NC), 1)],
                                                       None, ALU.is_equal)
                        if u % 2:
                            last.then_inc(onehots_ready, 1)

            def attend(p):
                dve.wait_ge(A_out, p + 2)
                dve.wait_ge(mean_out, p + 1)
                nc.vector.tensor_scalar(cnt[:, 1:2], cnt[:, 0:1], 1.0, None, ALU.max).then_inc(dve_step, 1)
                dve.wait_ge(dve_step, 1)
                nc.vector.reciprocal(cnt[:, 1:2], cnt[:, 1:2]).then_inc(degree_ready, 1)
                dve.wait_ge(den_out, p + 1)
                nc.vector.reciprocal(den, den).then_inc(dve_step, 1)
                dve.wait_ge(dve_step, 2)
                nc.vector.tensor_tensor(pin, qT[:, :, ds(p * T, T)], den, ALU.mult)\
                    .then_inc(pin_ready, 1)

            def sum_up(q, k=2):
                dve.wait_ge(mean_out, q + 2)
                nc.vector.tensor_tensor(gnn[:, :].unsqueeze(1), meanS.unsqueeze(1), R[:, ds(q, 1), :], ALU.add)\
                    .then_inc(dve_step, 1)
                dve.wait_ge(dve_step, k + 1)
                nc.vector.scalar_tensor_tensor(out=gnn[:, :].unsqueeze(1), in0=gnn[:, :].unsqueeze(1), scalar=0.0,
                                               in1=xs[:, ds(q, 1), :], op0=ALU.max, op1=ALU.add).then_inc(dve_step, 1)
                dve.wait_ge(dve_step, k + 2)
                dve.wait_ge(proj_out, q + 2)
                nc.vector.tensor_tensor(xs[:, ds(q, 1), :], gnn[:, :].unsqueeze(1), projS.unsqueeze(1), ALU.add)\
                    .then_inc(x1_ready, 1)
                dve.wait_ge(x1_ready, q + 2)
                dve.sem_inc(scores_seen, 1)
                nc.vector.bn_stats(bn[:, 0, :], xs[:, ds(q, 1), :].rearrange("p a d -> p (a d)")).then_inc(dve_step, 1)
                dve.wait_ge(dve_step, k + 3)
                nc.vector.bn_aggr(mv[:, 0, :], bn[:, 0, :]).then_inc(dve_step, 1)
                dve.wait_ge(dve_step, k + 4)
                nc.vector.tensor_scalar(x1rstd[:, ds(q, 1)], mv[:, 0, 1:2], EPS, None, ALU.add)
                nc.vector.tensor_copy(x1mean[:, ds(q, 1)], mv[:, 0, 0:1]).then_inc(yvar_ready, 1)

            def iteration2(m, p, q):
                onehots(m)
                if p is not None:
                    attend(p)
                if q is not None:
                    sum_up(q)
                if p is not None and q is None:
                    dve.wait_ge(prep_act, 2 * len(GROUPS))
                    dve.wait_ge(prep_dve, 2 * len(GROUPS))
                    nc.vector.tensor_reduce(wmean[:, :, :], WqT.rearrange("p k (h e) -> p k h e", h=H), AX.X, ALU.add)\
                        .then_inc(dve_step, 1)
                    dve.wait_ge(dve_step, 3)
                    nc.vector.tensor_scalar(wmean[:, :, :], wmean[:, :, :], 1.0 / QD, None, ALU.mult)\
                        .then_inc(dve_step, 1)
                    clear_steps(4)
                elif p is not None:
                    clear_steps(6)

            def center_weights(ks):
                w = WqT.rearrange("p k (h e) -> p k h e", h=H)
                for k in ks:
                    last = nc.vector.tensor_tensor(w[:, k, :, :], w[:, k, :, :],
                                                   wmean[:, k, :].unsqueeze(2).to_broadcast([128, H, QD]), ALU.subtract)
                last.then_inc(Wq_centered, 1)

            def norm_x1(n, first=False):
                if not first:
                    dve.wait_ge(yT_ps, n)
                nc.vector.tensor_scalar(y, xs[:, ds(n, 1), :].rearrange("p a d -> p (a d)"), x1mean[:, ds(n, 1)],
                                        x1rstd[:, ds(n, 1)], ALU.subtract, ALU.mult).then_inc(y_ready, 1)

            def last_tiles():
                sum_up(NT - 2, 0)
                clear_steps(4)
                center_weights((0, 1))
                attend(NT - 1)
                clear_steps(2)
                center_weights((2, 3))
                dve.wait_ge(yrstd_ready, 1)
                norm_x1(0, True)
                sum_up(NT - 1, 0)
                clear_steps(4)

            tiles(dve, iteration2, last_tiles)

            count = [0]

            def done(ins):
                count[0] += 1
                ins.then_inc(dve_step, 1)
                return count[0]

            def need(k):
                dve.wait_ge(dve_step, k)

            def two_rounds(pairs):
                k = [done(nc.vector.max(v[:, 0:8], x)) for x, x2, v, p in pairs]
                k2 = []
                for (x, x2, v, p), kk in zip(pairs, k):
                    need(kk)
                    k2.append(done(nc.vector.match_replace(x2, v[:, 0:8], x, LOWEST)))
                    nc.vector.max_index(p[:, 0:8], v[:, 0:8], x)
                k = []
                for (x, x2, v, p), kk in zip(pairs, k2):
                    need(kk)
                    k.append(done(nc.vector.max(v[:, 8:16], x2)))
                for (x, x2, v, p), kk in zip(pairs, k):
                    need(kk)
                    last = nc.vector.max_index(p[:, 8:16], v[:, 8:16], x2)
                return last

            def sort_scores(i, h):
                dve.wait_ge(sc_ready, i * H + (h + 2))
                dve.sem_inc(scores_seen, 1)
                two_rounds([(sc[:, h, f, :], sc2[:, f, :], top[:, f, h, :], topi[:, f, h, :]) for f in range(2)])\
                    .then_inc(topk_done, 1)

            def norms_out(n):
                dve.wait_ge(nrm_ps, n * 4 + 5)
                nc.vector.tensor_scalar(nrm[:, :], norms, LEAST_NORM ** 2, None, ALU.max).then_inc(nvar_ready, 1)

            def pair_and_weigh(i, n, n2):
                dve.wait_ge(topk_done, i * H + H)
                nc.vector.tensor_tensor(topif, topi, place_code[:, :, :].unsqueeze(2).to_broadcast([T, 2, H, TK]),
                                        ALU.add).then_inc(topif_ready, 1)
                if n2 is not None:
                    norm_x1(n2)
                dve.wait_ge(nrstd_ready, i + 1)
                k = done(nc.vector.tensor_tensor(top, top, nrm[:, :].rearrange("p (f h) -> p f h", f=2).unsqueeze(3)
                                                 .to_broadcast([T, 2, H, TK]), ALU.mult))
                need(k)
                a, b = top[:, 0, :, :], top[:, 1, :, :]
                for i0, i1 in PAIRS:
                    w, m = ROWS[i0], i1 - i0
                    o = cs[:, :, OFF[i0]:OFF[i0] + m * w].rearrange("p h (i j) -> p h i j", j=w)
                    k = done(nc.vector.tensor_tensor(
                        o, a[:, :, i0:i1].unsqueeze(3).to_broadcast([T, H, m, w]),
                        b[:, :, 0:w].unsqueeze(2).to_broadcast([T, H, m, w]), ALU.add))
                need(k)
                for h2 in range(0, H, 2):
                    k = done(two_rounds([(cs[:, h, :], cs2[:, h % 2, :], fs[:, h, :], posi[:, h, :])
                                         for h in (h2, h2 + 1)]))
                need(k)
                k_pos = done(nc.vector.tensor_single_scalar(place, posi, float(CODE), ALU.mult))
                k = done(nc.vector.tensor_copy(esum[:, :], fs[:, :, 0]))
                need(k)
                nc.vector.tensor_tensor(fs, fs, esum[:, :].unsqueeze(2).to_broadcast([T, H, TK]),
                                        ALU.subtract).then_inc(exp_in, 1)
                need(k_pos)
                for half in range(2):
                    g = slice(4 * half, 4 * half + 4)
                    dve.wait_ge(cirep_ready, i * 4 + (2 * half + 2))
                    k = done(nc.vector.tensor_tensor(found[:, g, :, :], cirep[:, g, :, :],
                                                     place[:, g, :].unsqueeze(2).to_broadcast([T, 4, C, TK]),
                                                     ALU.bitwise_xor))
                need(k)
                for w, m in ((25, 25), (12, 12), (6, 6), (3, 3), (1, 1)):
                    k = done(nc.vector.tensor_tensor(found[:, :, 0:w, :], found[:, :, 0:w, :], found[:, :, w:w + m, :],
                                                     ALU.min))
                    need(k)
                k = done(nc.vector.tensor_tensor(found[:, :, 0, :], found[:, :, 0, :], found[:, :, 2, :], ALU.min))
                need(k)
                k_fi = done(nc.vector.tensor_tensor(fi.rearrange("p (h r) -> p h r", h=H), found[:, :, 0, :],
                                                    found[:, :, 24, :], ALU.min))
                dve.wait_ge(exp_out, i + 1)
                k = done(nc.vector.tensor_reduce(esum[:, :], fs, AX.X, ALU.add))
                need(k)
                k = done(nc.vector.reciprocal(esum[:, :], esum[:, :]))
                need(k)
                nc.vector.tensor_tensor(fs, fs, esum[:, :].unsqueeze(2).to_broadcast([T, H, TK]),
                                        ALU.mult).then_inc(w_ready, 1)
                if n is not None:
                    sort_scores(n, 0)
                    norms_out(n)
                dve.wait_ge(wh_ready, i + 1)
                k = done(nc.vector.tensor_copy(lo_i[:, 0, :], ps[:, 7, 128:128 + T]))
                k_w = done(nc.vector.scalar_tensor_tensor(out=wl16[:, 0:T], in0=ps[:, 7, 0:T], scalar=WSCALE,
                                                          in1=wh16[:, 0:T], op0=ALU.mult, op1=ALU.subtract))
                need(k)
                k = done(nc.vector.tensor_single_scalar(lo_i[:, 1, :], lo_i[:, 0, :], LO - 1, ALU.bitwise_and))
                k_h = done(nc.vector.tensor_single_scalar(lo_i[:, 0, :], lo_i[:, 0, :], 6, ALU.logical_shift_right))
                need(k)
                k = done(nc.vector.tensor_copy(lo16[:, 0:T], lo_i[:, 1, :]))
                need(k_h)
                k_h = done(nc.vector.tensor_copy(hi16[:, 0:T], lo_i[:, 0, :]))
                need(k_h)
                k_h = done(nc.vector.tensor_tensor(Hh[:, 2, :, :], hi16.unsqueeze(1).to_broadcast([128, HI, TP]),
                                                   iotaH, ALU.is_equal))
                need(k)
                for b, (t0, t1) in enumerate(((0, 64), (64, TP))):
                    last = nc.vector.tensor_tensor(Lh[:, :, t0:t1], lo16[:, t0:t1].unsqueeze(1)
                                                   .to_broadcast([128, LO, t1 - t0]), iotaL[:, :, t0:t1], ALU.is_equal)
                    if b == 0:
                        need(k_h)
                        for s, w in ((0, wh16), (1, wl16)):
                            last = nc.vector.tensor_tensor(Hh[:, s, :, :], Hh[:, 2, :, :],
                                                           w.unsqueeze(1).to_broadcast([128, HI, TP]), ALU.mult)
                    last.then_inc(onehot3, 1)

            def apply_weights(p):
                dve.wait_ge(W0_ready, p * 2 + 2)
                for b2 in range(2):
                    c = min(64, T - 64 * b2)
                    k = done(nc.vector.scalar_tensor_tensor(
                        out=W0[:, 64 * b2:64 * b2 + c, :],
                        in0=ps[:, 5 + b2, 0:8 * c].rearrange("p (t j) -> p t j", j=8)[:, :, 4:8],
                        scalar=1.0 / WSCALE, in1=W0[:, 64 * b2:64 * b2 + c, :], op0=ALU.mult, op1=ALU.add))
                need(k)
                dve.wait_ge(gelu_ready, p + 1)
                nc.vector.tensor_tensor(GT, W0.rearrange("p t j -> p j t"),
                                        gelu2[:, ds(p % 2, 1), :].rearrange("p a (j t) -> p (a j) t", t=T),
                                        ALU.mult).then_inc(G_ready, 1)

            def prologue():
                done(nc.vector.tensor_copy(iotaL, iotaN[:, 0:LO].unsqueeze(2).to_broadcast([128, LO, TP])))
                for r in range(TK):
                    nc.vector.memset(place_code[:, 0, r:r + 1], float(CODE * OFF[r]))
                need(done(nc.vector.tensor_scalar(place_code[:, 1, :], iotaN[0:T, 0:TK], float(CODE), None, ALU.mult)))
                dve.wait_ge(yrstd_ready, 2)
                for a in (lo16, hi16, wh16, wl16):
                    last = nc.vector.memset(a, 0.0)
                last.then_inc(iotas_ready, 1)
                dve.wait_ge(iotas_ready, 1)
                sort_scores(0, 0)
                norm_x1(1)
                for h in range(1, H):
                    sort_scores(0, h)
                norms_out(0)
                clear_steps(count[0])
                count[0] = 0

            def iteration(i, p, n, n2):
                for h in range(1, H):
                    if p is not None:
                        sort_scores(i, h)
                    if p is not None and h == 4:
                        apply_weights(p)
                pair_and_weigh(i, n, n2)
                clear_steps(count[0])
                count[0] = 0

            iterations(dve, prologue, iteration)
            apply_weights(NT - 1)

        @block.tensor
        def _(pe):
            def prep(g):
                b = BUFFER_OF[g]
                pe.wait_ge(stage_loaded[b], 16 * loads(g))
                for o in range(4):
                    if g > 0:
                        pe.wait_ge(prep_act if o % 2 else prep_dve, 2 * g + o // 2 - 1)
                    for k in range(KC):
                        last = nc.tensor.transpose(ps[:, PREP_BANK[o], 128 * k:128 * k + 128],
                                                   BUFFERS[b][:, o, 128 * k:128 * k + 128], ident[:, :])
                    last.then_inc(prep_tr, 1)

            pe.wait_ge(consts_ready, 1)
            pe.wait_ge(edge_cast, 1)
            for s in range(2):
                for h in range(2):
                    last = nc.tensor.transpose(ps[0:T, 7, NC * s + CH * h:NC * s + CH * h + CH], edge_f[:, s, h, :],
                                               ident[0:CH, 0:CH])
            last.then_inc(edge_tr, 1)
            for n in range(4):
                last = nc.tensor.transpose(ps[0:NT, 6, CH * n:CH * n + CH], ends_b[:, n, :], ident[0:CH, 0:CH])
            last.then_inc(ends_tr, 1)
            for g in range(EARLY):
                prep(g)

            pe.wait_ge(prep_act, 2 * EARLY)
            pe.wait_ge(prep_dve, 2 * EARLY)
            pe.wait_ge(ends_out, 1)
            nc.tensor.matmul(ps[:, 5, :], zero16[:, 0:128], zero16[:, :], start=True, stop=False)
            nc.tensor.matmul(ps[:, 6, 0:4], zero16[:, 0:128], zero16[:, 0:4], start=True, stop=False)
            def transposes(i):
                pe.wait_ge(xn_ready, i + 1)
                pe.wait_ge(xnT_ready, i + 1)
                for k in range(KC):
                    last = nc.tensor.transpose(ps[:, 0, T * k:T * k + T], xn[:, 128 * k:128 * k + 128],
                                               ident[0:T, 0:T])
                last.then_inc(xnT_ps, 1)
                pe.wait_ge(xh_ready, i + 1)
                pe.wait_ge(hT_ready, i * 4 + 1)
                for k in range(KC):
                    last = nc.tensor.transpose(ps[:, 1, T * k:T * k + T], xh[:, 128 * k:128 * k + 128],
                                               ident[0:T, 0:T])
                last.then_inc(hT_ps, 1)

            def product(bank, lhs, w):
                for k in range(KC):
                    last = nc.tensor.matmul(ps[0:T, bank, :], lhs[:, k, :], w[:, k, :],
                                            start=(k == 0), stop=(k == KC - 1))
                last.then_inc(mm_ready, 1)

            def iteration1(i, u, more=True):
                pe.wait_ge(hT_ready, i * 4 + 5)
                pe.wait_ge(v_out, i + 1)
                product(2, hT[u], WlT)
                pe.wait_ge(q_out, i + 1)
                product(3, hT[u], WrT)
                pe.wait_ge(xnT_ready, i + 2)
                pe.wait_ge(k_out, i + 1)
                product(4, xnT[:, u, :, :], qkvT[:, :, 512:1024])
                if more:
                    transposes(i + 1)
                pe.wait_ge(p_out, i + 1)
                product(2, xnT[:, u, :, :], qkvT[:, :, 1024:1536])
                pe.wait_ge(r_out, i + 1)
                for g in range(4):
                    for k in range(KC):
                        last = nc.tensor.matmul(ps[:, 3, T * g:T * g + T], qkvT[:, k, 128 * g:128 * g + 128],
                                                xnT[:, u, k, :], start=(k == 0), stop=(k == KC - 1))
                last.then_inc(mm_ready, 1)
                pe.wait_ge(k_out, i + 2)
                pe.wait_ge(v_out, i + 2)
                for g in range(4):
                    c = slice(128 * g, 128 * g + 128)
                    nc.tensor.matmul(ps[:, 5, c], vS[:, c], kS[:, c], start=False, stop=False,
                                     skip_group_check=True)
                    last = nc.tensor.matmul(ps[:, 6, g:g + 1], kS[:, c], ones[0:T, :], start=False, stop=False,
                                            skip_group_check=True)
                last.then_inc(kv_done, 1)

            transposes(0)
            with pe.Fori(0, NT // 2 - 1) as i2:
                for u in range(2):
                    iteration1(i2 * 2 + u, u)
            iteration1(NT - 2, 0)
            iteration1(NT - 1, 1, False)
            pe.wait_ge(keys_normed, 1)
            pe.wait_ge(ecol_ready, 1)
            for n in range(4):
                last = nc.tensor.transpose(ps[:, 7, 128 * n:128 * n + 128], keysN[:, n, :], ident[:, :])
            last.then_inc(keys_tr, 1)
            pe.wait_ge(window_ready, 1)
            for n in range(2):
                last = nc.tensor.transpose(ps[0:1, 2, NT * n:NT * n + NT], window[:, n:n + 1], ident[0:NT, 0:NT])
            last.then_inc(window_tr, 1)
            nc.tensor.matmul(ps[:, 5, :], zero16[:, 0:128], zero16[:, :], start=False, stop=True)
            nc.tensor.matmul(ps[:, 6, 0:4], zero16[:, 0:128], zero16[:, 0:4], start=False, stop=True).then_inc(kv_closed, 1)
            pe.wait_ge(q_out, NT + 1)
            pe.wait_ge(k_out, NT + 1)
            for g in range(EARLY, len(GROUPS)):
                prep(g)

            pe.wait_ge(attn_ready, 2)
            pe.wait_ge(prep_act, 2 * len(GROUPS))
            pe.wait_ge(prep_dve, 2 * len(GROUPS))
            pe.wait_ge(q_out, NT + 1)
            pe.wait_ge(bounds_ready, 1)
            pe.sem_inc(onehots_free, 2 * RING)
            pe.wait_ge(knT_ready, 1)
            for g in range(4):
                last = nc.tensor.matmul(ps[:, 4 + g, :], Mb[:, g, :], projT[:, g, :], start=True, stop=True)
            last.then_inc(mixed_ps, 1)

            def counts(m):
                pe.wait_ge(A_out, m + 1)
                for b in range(3):
                    nc.tensor.matmul(ps[0:T, b, 0:AB], zero16[0:1, 0:T], zero16[0:1, 0:AB], start=True, stop=False)
                groups = pe.value_load(bounds[0:1, 1, ds(m, 1)], min_val=0, max_val=GROUPS_MAX)
                before = pe.value_load(bounds[0:1, 2, ds(m, 1)], min_val=0, max_val=GROUPS_MAX * NT)
                with pe.Fori(0, groups) as n:
                    k = before + n
                    slot = k % RING
                    for u in range(GC):
                        if u % 2 == 0:
                            pe.wait_ge(onehots_ready, k * 2 + (u // 2 + 1))
                        d_ap = D1[:, ds(slot, 1), u, 0:T].rearrange("p a n -> p (a n)")
                        for b in range(3):
                            last = nc.tensor.matmul(ps[0:T, b, 0:AB], d_ap,
                                                    S1[:, ds(slot, 1), u, AB * b:AB * b + AB].rearrange("p a n -> p (a n)"),
                                                    start=False, stop=False, skip_group_check=True)
                        if u % 2:
                            last.then_inc(onehots_free, 1)
                for b in range(3):
                    last = nc.tensor.matmul(ps[0:T, b, 0:AB], zero16[0:1, 0:T], zero16[0:1, 0:AB], start=False, stop=True)
                last.then_inc(A_ready, 1)

            def aggregate(p):
                pe.wait_ge(AT_act, p * 3 + 4)
                pe.wait_ge(mean_out, p + 1)
                for s in range(NT):
                    last = nc.tensor.matmul(ps[0:T, 7, :], AT[:, s, :], P[:, s, :], start=(s == 0),
                                            stop=(s == NT - 1))
                last.then_inc(agg_ready, 1)

            def project(p):
                pe.wait_ge(pin_ready, p + 2)
                pe.wait_ge(proj_out, p + 1)
                for g in range(4):
                    last = nc.tensor.matmul(ps[0:T, 5, :], pin[:, g, :], projT[:, g, :], start=(g == 0),
                                            stop=(g == 3))
                last.then_inc(proj_ready, 1)

            def transpose_counts(m, b):
                if b == 0:
                    pe.wait_ge(A_out, m + 2)
                    pe.wait_ge(AT_act, m * 3 + 1)
                elif b == 2:
                    pe.wait_ge(AT_act, m * 3 + 2)
                for s in range(4 * b, min(4 * b + 4, NT)):
                    last = nc.tensor.transpose(ps[0:T, 3 + b % 2, T * (s % 4):T * (s % 4) + T],
                                               As[:, T * s:T * s + T], ident[0:T, 0:T])
                last.then_inc(AT_ps, 1)

            def denominators(m):
                for g in range(4):
                    last = nc.tensor.matmul(ps[:, 6, T * g:T * g + T], Kb[:, g, :], qT[:, g, ds(m * T, T)],
                                            start=True, stop=True)
                last.then_inc(den_ps, 1)

            def iteration2(m, p, q):
                counts(m)
                if p is not None:
                    aggregate(p)
                    project(p)
                if p is None:
                    pe.wait_ge(mixed_ready, 1)
                transpose_counts(m, 0)
                transpose_counts(m, 1)
                denominators(m)
                transpose_counts(m, 2)

            def last_tile():
                aggregate(NT - 1)
                project(NT - 1)

            tiles(pe, iteration2, last_tile)

            pe.wait_ge(knT_ready, 1)
            pe.wait_ge(bq_ready, 48)
            pe.wait_ge(Wq_centered, 1)
            pe.wait_ge(up_loaded, 16)

            def queries(n, j):
                pe.wait_ge(qh_ready, n * 8 + max(2 * j - 2, 0) + 1)
                for k in range(KC):
                    nc.tensor.matmul(ps[0:T, j % 2, :], yT[:, k, :], WqT[:, k, 512 * j:512 * j + 512],
                                     start=(k == 0), stop=False)
                nc.tensor.matmul(ps[0:T, j % 2, :], onesb[:, :], bq3[:, 512 * j:512 * j + 512], start=False,
                                 stop=True).then_inc(q_ps, 1)

            def transpose_y(n):
                pe.wait_ge(y_ready, n + 1)
                pe.wait_ge(vT_ready, n * 4 + 1)
                for k in range(KC):
                    last = nc.tensor.transpose(ps[:, 2, T * k:T * k + T], y[:, 128 * k:128 * k + 128],
                                               ident[0:T, 0:T])
                last.then_inc(yT_ps, 1)

            def head(n):
                pe.wait_ge(yT_ready, n + 1)
                queries(n, 0)
                queries(n, 1)

            def transpose_queries(n, j):
                pe.wait_ge(qh_ready, n * 8 + (2 * j + 3))
                pe.wait_ge(vT_ready, n * 4 + (j + 1))
                for f in range(2):
                    for h in range(2):
                        c0 = QD * (2 * j + h) + 128 * f
                        last = nc.tensor.transpose(ps[:, 2, T * (2 * f + h):T * (2 * f + h) + T],
                                                   qh[:, c0:c0 + 128], ident[0:T, 0:T])
                last.then_inc(tr_ps, 1)

            def scores(n, j):
                pe.wait_ge(vT_ready, n * 4 + (j + 2))
                for h in range(2):
                    hh = 2 * j + h
                    pe.wait_ge(sc_ready, n * 8 + (max(hh - 1, 0) + 1))
                    for f in range(2):
                        last = nc.tensor.matmul(ps[0:T, 3 + h, NK * f:NK * f + NK], vT[:, f, h, :], knT[:, f, :],
                                                start=True, stop=True)
                    last.then_inc(s_ps, 1)

            def query_norms(n, j):
                pe.wait_ge(v2_ready, n * 4 + (j + 2))
                for h in range(2):
                    for f in range(2):
                        c = H * f + 2 * j + h
                        last = nc.tensor.matmul(norms[:, c:c + 1], v2[:, f, h, :], ones[:, :], start=True,
                                                stop=True)
                last.then_inc(nrm_ps, 1)

            def inner(n, cur, p):
                if p is not None:
                    pe.wait_ge(res_ready, n)
                elif cur is not None:
                    pe.wait_ge(gelu_ready, n)
                for b in range(4):
                    for k in range(KC):
                        last = nc.tensor.matmul(ps[:, 7, T * b:T * b + T], downT[:, k, 128 * b:128 * b + 128],
                                                yT[:, k, :], start=(k == 0), stop=(k == KC - 1))
                last.then_inc(inner_ps, 1)

            def body(n, cur, p):
                transpose_queries(n, 0)
                queries(n, 2)
                scores(n, 0)
                if cur is not None:
                    pe.wait_ge(nvar_ready, n)
                if p is not None:
                    pe.wait_ge(G_ready, p + 2)
                query_norms(n, 0)
                transpose_queries(n, 1)
                if p is not None:
                    output(p)
                queries(n, 3)
                scores(n, 1)
                query_norms(n, 1)
                transpose_queries(n, 2)
                inner(n, cur, p)
                scores(n, 2)
                query_norms(n, 2)
                transpose_queries(n, 3)
                scores(n, 3)
                query_norms(n, 3)

            def expert_weights(p):
                pe.wait_ge(onehot3, p * 2 + 1)
                pe.wait_ge(G_ready, p + 1)
                for t in range(T):
                    if t == 64:
                        pe.wait_ge(onehot3, p * 2 + 2)
                    for g in range(2):
                        last = nc.tensor.matmul(ps[64 * g:64 * g + 64, 5 + t // 64, 8 * (t % 64):8 * (t % 64) + 8],
                                                Lh[:, :, t], Hh[:, 0:2, g:HI:2, t], start=True, stop=True)
                    if t == 63 or t == T - 1:
                        last.then_inc(W_ps, 1)

            def output(p):
                pe.wait_ge(G_ready, p + 2)
                for j in range(4):
                    nc.tensor.matmul(ps[0:T, 7, :], GT[:, j, :], up[:, j, :], start=(j == 0), stop=False)
                nc.tensor.matmul(ps[0:T, 7, :], ident[0:T, 0:T], xs[:, ds(p, 1), :].rearrange("p a d -> p (a d)"),
                                 start=False, stop=True).then_inc(out_ps, 1)

            def prologue():
                transpose_y(0)
                head(0)
                body(0, None, None)
                transpose_y(1)
                head(1)

            def iteration(i, p, n, n2):
                if p is not None:
                    pe.wait_ge(nvar_ready, i + 1)
                    expert_weights(p)
                if n is not None:
                    body(n, i, p)
                elif p is not None:
                    output(p)
                if n2 is not None:
                    transpose_y(n2)
                pe.wait_ge(w_ready, i + 1)
                if n is not None:
                    pe.wait_ge(gelu_ready, n + 1)
                else:
                    pe.wait_ge(res_ready, i + 1)
                nc.tensor.transpose(ps[:, 7, 0:T], fs.rearrange("p h r -> p (h r)"), ident[0:T, 0:T])
                nc.tensor.transpose(ps[:, 7, 128:128 + T], fi, ident[0:T, 0:T]).then_inc(wT_ps, 1)
                if n2 is not None:
                    head(n2)

            iterations(pe, prologue, iteration)
            expert_weights(NT - 1)
            output(NT - 1)


_INS = ["x", "src", "dst", "L0_gnn_W_l", "L0_gnn_b_l", "L0_gnn_W_r", "L0_gnn_gamma", "L0_gnn_beta",
        "L0_mix_qkv_weight", "L0_mix_proj_weight", "L0_mix_proj_bias", "L0_ffn_Wq", "L0_ffn_bq", "L0_ffn_ln_g",
        "L0_ffn_ln_b", "L0_ffn_keys0", "L0_ffn_keys1", "L0_ffn_expert_down", "L0_ffn_expert_up"]


def kernel(**inputs):
    import numpy as _np
    import concourse.bacc as _bacc
    from concourse import mybir as _mybir
    from concourse.bass_utils import run_bass_kernel_spmd as _run

    nc = _bacc.Bacc("TRN2", target_bir_lowering=False, num_devices=1)
    arrays, args = {}, []
    for name in _INS:
        a = _np.ascontiguousarray(inputs[name])
        arrays[f"in_{name}"] = a
        args.append(nc.dram_tensor(f"in_{name}", a.shape, _mybir.dt.from_np(a.dtype), kind="ExternalInput").ap())
    args.append(nc.dram_tensor("out", inputs["x"].shape, _mybir.dt.float32, kind="ExternalOutput").ap())
    build(nc, *args)
    r = _run(nc, [arrays], core_ids=[0])
    return r.results[0]["out"]
```
